# Optimizing a Trainium2 kernel written in Bass

```python
import numpy as np
import jax
import jax.numpy as jnp

def _softmax(x, axis=-1):
    return jax.nn.softmax(x, axis=axis)

def _gelu(x):
    return jax.nn.gelu(x, approximate=True)

def _silu(x):
    return jax.nn.silu(x)

def _sigmoid(x):
    return jax.nn.sigmoid(x)

def _layernorm(x, axis=-1, eps=1e-05):
    m = jnp.mean(x, axis=axis, keepdims=True)
    v = jnp.var(x, axis=axis, keepdims=True)
    return (x - m) / jnp.sqrt(v + eps)

def _scatter_add(tgt, idx, src, axis=0):
    return tgt.at[idx].add(src)

def _segment_sum(src, seg, n):
    return jax.ops.segment_sum(src, seg, n)
kernel_name = 'mk_flamingo_gated_d2_seqx_r4_e1defa'

def setup_inputs(seed: int=0):
    np.random.seed(seed)
    _w = jnp.asarray

    def _rec_inputs():
        import jax
        import jax.numpy as jnp
        _rk = jax.random.key(seed)
        x = 0.0003765 + 1 * jax.random.normal(jax.random.fold_in(_rk, 1), (8, 256, 512), jnp.float32)
        _lenS = 256 - jax.random.randint(jax.random.fold_in(_rk, 7), (8,), 0, max(1, 256 // 4) + 1, jnp.int32)
        _lenS2 = 256 - jax.random.randint(jax.random.fold_in(_rk, 8), (8,), 0, max(1, 256 // 4) + 1, jnp.int32)
        _ctx_2048P = jax.random.normal(jax.random.fold_in(_rk, 11), (8, 16, 512), jnp.float32)
        _ctx_2048c = jax.random.dirichlet(jax.random.fold_in(_rk, 511), 0.3 * jnp.ones((16,), jnp.float32), (8, 256))
        _ctx_2048t = jnp.einsum('bsk,bkd->bsd', _ctx_2048c, _ctx_2048P)
        _ctx_2048t = _ctx_2048t * jax.lax.rsqrt(jnp.mean(jnp.square(_ctx_2048t)) + 1e-12) * 0.953939
        ctx_2048 = -0.000292821 + 1.00034 * (_ctx_2048t + 0.3 * jax.random.normal(jax.random.fold_in(_rk, 611), (8, 256, 512), jnp.float32))
        _g = jax.random.normal(jax.random.fold_in(_rk, 9001), (2, 2), jnp.float32)
        _g = jnp.sign(_g) * jnp.maximum(jnp.abs(_g), 1.0) + (_g == 0) * 1.0
        g_xattn = _g[0]
        g_ffn = _g[1]
        return (x, ctx_2048, g_xattn, g_ffn)
    x, ctx_2048, g_xattn, g_ffn = _rec_inputs()

    def _L0_xattn_setup():
        import jax, jax.numpy as jnp
        import numpy as np
        key = jax.random.key(seed)
        k1, k2, k3, k4, k5 = jax.random.split(key, 5)
        B, D_MODEL, L = (2, 256, 512)
        HEAD_DIM = 8
        H = D_MODEL // HEAD_DIM
        return {'k': jax.random.normal(k1, (B, D_MODEL, L), dtype=jnp.float32), 'v': jax.random.normal(k2, (B, D_MODEL, L), dtype=jnp.float32), 'q': jax.random.normal(k3, (B, D_MODEL, L), dtype=jnp.float32), 'ssm_kernel': jax.random.normal(k4, (H, L), dtype=jnp.float32), 'D': jax.random.normal(k5, (H,), dtype=jnp.float32), 'head_dim': HEAD_DIM}
    _L0_xattn_all = _L0_xattn_setup()
    _L0_xattn_in = {k: v for k, v in _L0_xattn_all.items() if k in ('ssm_kernel', 'D')}
    del _L0_xattn_all

    def _L0_ffn_setup():
        import jax, jax.numpy as jnp
        import numpy as np
        B, S, H, I, E, TOP_K, NS = (2, 512, 512, 352, 8, 2, 2)
        SI = I * NS
        INIT = 0.02
        key = jax.random.key(seed)
        ks = jax.random.split(key, 9)
        f32 = jnp.float32
        return {'hidden_states': jax.random.normal(ks[0], (B, S, H), f32), 'router_w': jax.random.normal(ks[1], (E, H), f32) * INIT, 'gate_w': jax.random.normal(ks[2], (E, H, I), f32) * INIT, 'up_w': jax.random.normal(ks[3], (E, H, I), f32) * INIT, 'down_w': jax.random.normal(ks[4], (E, I, H), f32) * INIT, 's_gate_w': jax.random.normal(ks[5], (H, SI), f32) * INIT, 's_gate_b': jnp.zeros((SI,), f32), 's_up_w': jax.random.normal(ks[6], (H, SI), f32) * INIT, 's_up_b': jnp.zeros((SI,), f32), 's_down_w': jax.random.normal(ks[7], (SI, H), f32) * INIT, 's_down_b': jnp.zeros((H,), f32)}
    _L0_ffn_all = _L0_ffn_setup()
    _L0_ffn_in = {k: v for k, v in _L0_ffn_all.items() if k in ('router_w', 'gate_w', 'up_w', 'down_w', 's_gate_w', 's_gate_b', 's_up_w', 's_up_b', 's_down_w', 's_down_b')}
    del _L0_ffn_all

    def _L1_xattn_setup():
        import jax, jax.numpy as jnp
        import numpy as np
        EPS = 1e-06
        NUM_HEADS = 16

        def _feature_map(x):
            return jnp.where(x > 0, x + 1.0, jnp.exp(x))
        key = jax.random.key(seed)
        ks = jax.random.split(key, 7)
        B, L, S, D = (4, 1024, 1024, 512)
        sc = 1.0 / np.sqrt(D)
        return {'query': jax.random.normal(ks[0], (B, L, D), jnp.float32), 'kv': jax.random.normal(ks[1], (B, S, D), jnp.float32), 'Wq': jax.random.normal(ks[2], (D, D), jnp.float32) * sc, 'Wg': jax.random.normal(ks[3], (D, D), jnp.float32) * sc, 'bg': jnp.ones((D,), jnp.float32), 'Wkv': jax.random.normal(ks[4], (2 * D, D), jnp.float32) * sc, 'Wo': jax.random.normal(ks[5], (D, D), jnp.float32) * sc}
    _L1_xattn_all = _L1_xattn_setup()
    _L1_xattn_in = {k: v for k, v in _L1_xattn_all.items() if k in ('Wq', 'Wg', 'bg', 'Wkv', 'Wo')}
    del _L1_xattn_all

    def _L1_ffn_setup():
        import jax, jax.numpy as jnp
        import numpy as np
        LN_EPS = 1e-05
        L2_EPS = 1e-12

        def _l2norm(v, axis):
            n = jnp.sqrt(jnp.sum(v * v, axis=axis, keepdims=True))
            return v / jnp.maximum(n, L2_EPS)
        key = jax.random.key(seed)
        ks = jax.random.split(key, 4)
        B, N, D, E, S, H = (8, 512, 512, 16, 128, 128)
        x = jax.random.normal(ks[0], (B, N, D), dtype=jnp.float32)
        mu = jax.random.normal(ks[1], (D, E, S), dtype=jnp.float32) / np.sqrt(D)
        W1 = jax.random.normal(ks[2], (E, D, H), dtype=jnp.float32) * np.sqrt(2.0 / D)
        W2 = jax.random.normal(ks[3], (E, H, D), dtype=jnp.float32) * np.sqrt(2.0 / (H + D))
        return {'x': x, 'gamma': jnp.ones((D,), jnp.float32), 'beta': jnp.zeros((D,), jnp.float32), 'mu': mu, 'scale': jnp.ones((1,), jnp.float32), 'W1': W1, 'b1': jnp.zeros((E, H), jnp.float32), 'W2': W2, 'b2': jnp.zeros((E, D), jnp.float32)}
    _L1_ffn_all = _L1_ffn_setup()
    _L1_ffn_in = {k: v for k, v in _L1_ffn_all.items() if k in ('gamma', 'beta', 'mu', 'scale', 'W1', 'b1', 'W2', 'b2')}
    del _L1_ffn_all
    return {'x': x, 'ctx_2048': ctx_2048, 'g_xattn': g_xattn, 'g_ffn': g_ffn, 'L0_xattn_ssm_kernel': _L0_xattn_in['ssm_kernel'], 'L0_xattn_D': _L0_xattn_in['D'], 'L0_ffn_router_w': _L0_ffn_in['router_w'], 'L0_ffn_gate_w': _L0_ffn_in['gate_w'], 'L0_ffn_up_w': _L0_ffn_in['up_w'], 'L0_ffn_down_w': _L0_ffn_in['down_w'], 'L0_ffn_s_gate_w': _L0_ffn_in['s_gate_w'], 'L0_ffn_s_gate_b': _L0_ffn_in['s_gate_b'], 'L0_ffn_s_up_w': _L0_ffn_in['s_up_w'], 'L0_ffn_s_up_b': _L0_ffn_in['s_up_b'], 'L0_ffn_s_down_w': _L0_ffn_in['s_down_w'], 'L0_ffn_s_down_b': _L0_ffn_in['s_down_b'], 'L1_xattn_Wq': _L1_xattn_in['Wq'], 'L1_xattn_Wg': _L1_xattn_in['Wg'], 'L1_xattn_bg': _L1_xattn_in['bg'], 'L1_xattn_Wkv': _L1_xattn_in['Wkv'], 'L1_xattn_Wo': _L1_xattn_in['Wo'], 'L1_ffn_gamma': _L1_ffn_in['gamma'], 'L1_ffn_beta': _L1_ffn_in['beta'], 'L1_ffn_mu': _L1_ffn_in['mu'], 'L1_ffn_scale': _L1_ffn_in['scale'], 'L1_ffn_W1': _L1_ffn_in['W1'], 'L1_ffn_b1': _L1_ffn_in['b1'], 'L1_ffn_W2': _L1_ffn_in['W2'], 'L1_ffn_b2': _L1_ffn_in['b2']}

def reference(x, ctx_2048, g_xattn, g_ffn, L0_xattn_ssm_kernel, L0_xattn_D, L0_ffn_router_w, L0_ffn_gate_w, L0_ffn_up_w, L0_ffn_down_w, L0_ffn_s_gate_w, L0_ffn_s_gate_b, L0_ffn_s_up_w, L0_ffn_s_up_b, L0_ffn_s_down_w, L0_ffn_s_down_b, L1_xattn_Wq, L1_xattn_Wg, L1_xattn_bg, L1_xattn_Wkv, L1_xattn_Wo, L1_ffn_gamma, L1_ffn_beta, L1_ffn_mu, L1_ffn_scale, L1_ffn_W1, L1_ffn_b1, L1_ffn_W2, L1_ffn_b2):
    import jax
    import jax.numpy as jnp

    def _L0_xattn_ref(k, v, q, ssm_kernel, D, head_dim):
        import jax, jax.numpy as jnp
        import numpy as np
        B, HD, L = k.shape
        H = HD // head_dim
        fft_size = 2 * L
        k_ = k.reshape(B, H, head_dim, L)
        v_ = v.reshape(B, H, head_dim, L)
        q_ = q.reshape(B, H, head_dim, L)
        kv = jnp.einsum('bhil,bhjl->bijhl', k_, v_)
        kv_f = jnp.fft.rfft(kv, n=fft_size)
        kernel_f = jnp.fft.rfft(ssm_kernel, n=fft_size)
        y = jnp.fft.irfft(kv_f * kernel_f, n=fft_size)[..., :L]
        out = y + kv * D[None, None, None, :, None]
        out = jnp.einsum('bijhl,bhil->bjhl', out, q_)
        out = jnp.transpose(out, (0, 2, 1, 3)).reshape(B, H * head_dim, L)
        return out.astype(k.dtype)

    def _L0_ffn_ref(hidden_states, router_w, gate_w, up_w, down_w, s_gate_w, s_gate_b, s_up_w, s_up_b, s_down_w, s_down_b):
        import jax, jax.numpy as jnp
        import numpy as np
        B, S, H, I, E, TOP_K, NS = (2, 512, 512, 352, 8, 2, 2)
        SI = I * NS
        INIT = 0.02
        b, s, h = hidden_states.shape
        x = hidden_states.reshape(-1, h)
        T = x.shape[0]
        num_experts = router_w.shape[0]
        logits = x @ router_w.T
        probs = jax.nn.softmax(logits.astype(jnp.float32), axis=-1)
        topk_w, topk_idx = jax.lax.top_k(probs, TOP_K)
        topk_w = topk_w / jnp.sum(topk_w, axis=-1, keepdims=True)
        combine = jnp.zeros((T, num_experts), probs.dtype)
        combine = combine.at[jnp.arange(T)[:, None], topk_idx].add(topk_w)

        def expert_step(acc, ws):
            gw, uw, dw, ce = ws
            out = jax.nn.silu(x @ gw) * (x @ uw) @ dw
            return (acc + ce[:, None].astype(out.dtype) * out, None)
        moe_out, _ = jax.lax.scan(expert_step, jnp.zeros_like(x), (gate_w, up_w, down_w, combine.T))
        shared = jax.nn.silu(x @ s_gate_w + s_gate_b) * (x @ s_up_w + s_up_b) @ s_down_w + s_down_b
        return (moe_out + shared).reshape(b, s, h)

    def _L1_xattn_ref(query, kv, Wq, Wg, bg, Wkv, Wo):
        import jax, jax.numpy as jnp
        import numpy as np
        EPS = 1e-06
        NUM_HEADS = 16

        def _feature_map(x):
            return jnp.where(x > 0, x + 1.0, jnp.exp(x))
        B, L, D = query.shape
        S = kv.shape[1]
        H = NUM_HEADS
        hd = D // H
        q = query @ Wq.T
        gate = jax.nn.sigmoid(query @ Wg.T + bg)
        kvp = kv @ Wkv.T
        k, v = jnp.split(kvp, 2, axis=-1)
        q = _feature_map(q.reshape(B, L, H, hd).transpose(0, 2, 1, 3))
        k = _feature_map(k.reshape(B, S, H, hd).transpose(0, 2, 1, 3))
        v = v.reshape(B, S, H, hd).transpose(0, 2, 1, 3)
        kv_summary = jnp.einsum('bhsd,bhse->bhde', k, v)
        k_sum = k.sum(axis=-2)
        z = 1.0 / (jnp.einsum('bhld,bhd->bhl', q, k_sum)[..., None] + EPS)
        attn = jnp.einsum('bhld,bhde->bhle', q, kv_summary) * z
        attn = attn.transpose(0, 2, 1, 3).reshape(B, L, D)
        out = attn * gate @ Wo.T
        return out

    def _L1_ffn_ref(x, gamma, beta, mu, scale, W1, b1, W2, b2):
        import jax, jax.numpy as jnp
        import numpy as np
        LN_EPS = 1e-05
        L2_EPS = 1e-12

        def _l2norm(v, axis):
            n = jnp.sqrt(jnp.sum(v * v, axis=axis, keepdims=True))
            return v / jnp.maximum(n, L2_EPS)
        B, N, D = x.shape
        _, E, S = mu.shape
        mean = jnp.mean(x, axis=-1, keepdims=True)
        var = jnp.mean(jnp.square(x - mean), axis=-1, keepdims=True)
        x_ln = (x - mean) / jnp.sqrt(var + LN_EPS) * gamma + beta
        x_n = _l2norm(x_ln, -1) * scale
        mu_n = _l2norm(mu, 0)
        logits = jnp.einsum('bnd,des->bnes', x_n, mu_n)
        dispatch = jax.nn.softmax(logits, axis=1)
        combine = jax.nn.softmax(logits.reshape(B, N, E * S), axis=-1)
        slot_in = jnp.einsum('bnd,bnes->besd', x_ln, dispatch)
        h = jax.nn.gelu(jnp.einsum('besd,edh->besh', slot_in, W1) + b1[None, :, None, :], approximate=False)
        slot_out = jnp.einsum('besh,ehd->besd', h, W2) + b2[None, :, None, :]
        out = jnp.einsum('bsd,bns->bnd', slot_out.reshape(B, E * S, D), combine)
        return out
    x = x + jnp.tanh(g_xattn[0]) * _L0_xattn_ref(ctx_2048, ctx_2048, _layernorm(x, axis=-1), L0_xattn_ssm_kernel, L0_xattn_D, 8)
    x = x + jnp.tanh(g_ffn[0]) * _L0_ffn_ref(_layernorm(x, axis=-1), L0_ffn_router_w, L0_ffn_gate_w, L0_ffn_up_w, L0_ffn_down_w, L0_ffn_s_gate_w, L0_ffn_s_gate_b, L0_ffn_s_up_w, L0_ffn_s_up_b, L0_ffn_s_down_w, L0_ffn_s_down_b)
    x = x + jnp.tanh(g_xattn[1]) * _L1_xattn_ref(_layernorm(x, axis=-1), ctx_2048, L1_xattn_Wq, L1_xattn_Wg, L1_xattn_bg, L1_xattn_Wkv, L1_xattn_Wo)
    x = x + jnp.tanh(g_ffn[1]) * _L1_ffn_ref(_layernorm(x, axis=-1), L1_ffn_gamma, L1_ffn_beta, L1_ffn_mu, L1_ffn_scale, L1_ffn_W1, L1_ffn_b1, L1_ffn_W2, L1_ffn_b2)
    return x

_drawn_inputs = setup_inputs


def setup_inputs(seed=0):
    import zlib

    import numpy as np

    out = dict(_drawn_inputs(seed))
    spreads = {'g_ffn': (-1.0, 0.6),
     'L0_ffn_s_gate_b': (0.0, 0.8),
     'L0_ffn_s_up_b': (0.0, 0.8),
     'L0_ffn_s_down_b': (0.0, 2.0),
     'L1_xattn_bg': (1.0, 0.6),
     'L1_ffn_gamma': (1.0, 0.6),
     'L1_ffn_beta': (0.0, 0.8),
     'L1_ffn_b1': (0.0, 2.0),
     'L1_ffn_b2': (0.0, 2.0)}
    factors = {'L0_ffn_router_w': 8.0,
     'L0_ffn_gate_w': 8.0,
     'L0_ffn_up_w': 8.0,
     'L0_ffn_down_w': 8.0,
     'L0_ffn_s_gate_w': 8.0,
     'L0_ffn_s_up_w': 8.0,
     'L0_ffn_s_down_w': 8.0,
     'L1_xattn_Wq': 8.0,
     'L1_xattn_Wg': 8.0,
     'L1_xattn_Wkv': 6.678,
     'L1_xattn_Wo': 6.82,
     'L1_ffn_mu': 64.0,
     'L1_ffn_W1': 8.0,
     'L1_ffn_W2': 8.0}
    for name, (base, spread) in spreads.items():
        noise = np.random.default_rng([zlib.crc32(name.encode()), seed]).standard_normal(out[name].shape)
        drawn = base * np.exp(spread * noise) if base else spread * noise
        out[name] = jnp.asarray(drawn.astype(out[name].dtype))
    for name, factor in factors.items():
        out[name] = (out[name] * factor).astype(out[name].dtype)
    return out
```

```python
from contextlib import ExitStack, contextmanager

import numpy as np

import concourse.bass as bass
from concourse import mybir

F32, F16, I32 = mybir.dt.float32, mybir.dt.float16, mybir.dt.int32
ACT = mybir.ActivationFunctionType
ALU = mybir.AluOpType
AX = mybir.AxisListType

P = 128
B, N, D = 8, 256, 512
T = B * N
TT = T // P
KD = D // P
CH = 4 * P
NCH = T // CH
SSM_H, SSM_I = 32, 8
PAIRS = SSM_I * (SSM_I + 1) // 2
GH = 16
GROUPS = SSM_H // GH
LN_EPS = 1e-5


@contextmanager
def phase(nc):
    with nc.cleanup_on_exit(), ExitStack() as stack:
        yield stack


def opener(nc, stack):
    def sb(name, shape, dt=F32):
        return stack.enter_context(nc.sbuf_tensor(name, shape, dt))

    def ps(name, shape, dt=F32):
        return stack.enter_context(nc.psum_tensor(name, shape, dt))

    def sem(name):
        return nc.alloc_semaphore(name)
    return sb, ps, sem


def pair_at(i):
    return i * SSM_I - i * (i - 1) // 2


class LayerNorm:

    def __init__(self, sb, sem, name, tiles=4):
        self.tiles = tiles
        self.stats = sb(f"{name}_stats", [P, tiles, 6])
        self.mean, self.var = sb(f"{name}_mean", [P, tiles]), sb(f"{name}_var", [P, tiles])
        self.gap, self.spread = sb(f"{name}_gap", [P, tiles]), sb(f"{name}_spread", [P, tiles])
        self.std, self.rstd = sb(f"{name}_std", [P, tiles]), sb(f"{name}_rstd", [P, tiles])
        self.stats_done, self.parts_done = sem(f"{name}_stats_done"), sem(f"{name}_parts_done")
        self.gap_squared, self.var_done = sem(f"{name}_gap_squared"), sem(f"{name}_var_done")
        self.std_done, self.rstd_done = sem(f"{name}_std_done"), sem(f"{name}_rstd_done")

    def statistics(self, nc, dve, rows, c):
        for t in range(self.tiles):
            self.tile(nc, rows, t)
        self.finish(nc, dve, c)

    def tile(self, nc, rows, t):
        nc.vector.bn_stats(self.stats[:, t, :], rows[:, t, :]).then_inc(self.stats_done, 1)

    def finish(self, nc, dve, c):
        even_mean, even_m2 = self.stats[:, :, 1], self.stats[:, :, 2]
        odd_mean, odd_m2 = self.stats[:, :, 4], self.stats[:, :, 5]
        dve.wait_ge(self.stats_done, (c + 1) * self.tiles)
        nc.vector.tensor_tensor(self.mean[:, :], even_mean, odd_mean, ALU.add).then_inc(self.parts_done, 1)
        nc.vector.tensor_tensor(self.gap[:, :], even_mean, odd_mean, ALU.subtract).then_inc(self.parts_done, 1)
        nc.vector.tensor_tensor(self.spread[:, :], even_m2, odd_m2, ALU.add).then_inc(self.parts_done, 1)
        dve.wait_ge(self.parts_done, (c + 1) * 3)
        nc.vector.tensor_scalar(self.mean[:, :], self.mean[:, :], 0.5, None, ALU.mult).then_inc(self.gap_squared, 1)
        nc.vector.scalar_tensor_tensor(self.gap[:, :], self.gap[:, :], 0.25, self.gap[:, :], ALU.mult, ALU.mult
                                       ).then_inc(self.gap_squared, 1)
        nc.vector.tensor_scalar(self.spread[:, :], self.spread[:, :], 1.0 / D, LN_EPS, ALU.mult, ALU.add
                                ).then_inc(self.gap_squared, 1)
        dve.wait_ge(self.gap_squared, (c + 1) * 3)
        nc.vector.tensor_tensor(self.var[:, :], self.gap[:, :], self.spread[:, :], ALU.add).then_inc(self.var_done, 1)
        dve.wait_ge(self.std_done, c + 1)
        nc.vector.reciprocal(self.rstd[:, :], self.std[:, :]).then_inc(self.rstd_done, 1)
        dve.wait_ge(self.rstd_done, c + 1)

    def root(self, nc, act, c):
        act.wait_ge(self.var_done, c + 1)
        nc.scalar.activation(self.std[:, :], self.var[:, :], ACT.Sqrt).then_inc(self.std_done, 1)


def constants(nc, k, g_xattn, g_ffn):
    with phase(nc) as st:
        sb, ps, sem = opener(nc, st)
        ident_zeroed, ident_ready = sem("ident_zeroed"), sem("ident_ready")
        gates_loaded, gates_ready = sem("gates_loaded"), sem("gates_ready")
        block = st.enter_context(nc.Block())

        @block.sync
        def _(sp):
            sp.dma_start(k.gates[:, 0:2], g_xattn.partition_broadcast(P)).then_inc(gates_loaded, 16)
            sp.dma_start(k.gates[:, 2:4], g_ffn.partition_broadcast(P)).then_inc(gates_loaded, 16)

        @block.gpsimd
        def _(pool):
            nc.gpsimd.memset(k.ident[:, :], 0.0).then_inc(ident_zeroed, 1)
            pool.wait_ge(ident_zeroed, 1)
            nc.gpsimd.affine_select(out=k.ident[:, :], in_=k.ident[:, :], compare_op=ALU.not_equal, fill=1.0,
                                    base=0, pattern=[[-1, P]], channel_multiplier=1).then_inc(ident_ready, 1)

        @block.scalar
        def _(act):
            act.wait_ge(gates_loaded, 32)
            nc.scalar.activation(k.tanh_gates[:, :], k.gates[:, :], ACT.Tanh).then_inc(gates_ready, 1)

        @block.vector
        def _(dve):
            dve.wait_ge(ident_ready, 1)
            nc.vector.tensor_copy(k.ident16[:, :], k.ident[:, :])


def conv_operands(nc, k, x, ctx, q_t, c_t):
    with phase(nc) as st:
        sb, ps, sem = opener(nc, st)
        x_in, c_in = sb("x_in", [P, 2, KD, D]), sb("c_in", [P, 2, KD, D])
        ln = LayerNorm(sb, sem, "x")
        tr = [ps(f"tr{n}", [P, D]) for n in range(8)]
        loaded = [sem(f"loaded{u}") for u in range(2)]
        normed = sem("normed")
        x_tr, c_tr = sem("x_tr"), sem("c_tr")
        x_out, c_out = sem("x_out"), sem("c_out")
        block = st.enter_context(nc.Block())
        x_d = x.rearrange("b (k p) d -> p (b k) d", p=P)
        c_d = ctx.rearrange("b (k p) d -> p (b k) d", p=P)

        @block.sync
        def _(sp):
            with sp.Fori(0, NCH // 2) as i:
                for u in range(2):
                    sp.wait_ge(x_out, i * 8 + 4 * (u + 1))
                    sp.dma_start(x_in[:, u], x_d[:, bass.ds(i * 8 + u * 4, 4), :]).then_inc(loaded[u], 16)
                    sp.dma_start(c_in[:, u], c_d[:, bass.ds(i * 8 + u * 4, 4), :]).then_inc(loaded[u], 16)

        @block.vector
        def _(dve):
            with dve.Fori(0, NCH // 2) as i:
                for u in range(2):
                    c = i * 2 + u
                    dve.wait_ge(loaded[u], (i + 1) * 32)
                    ln.statistics(nc, dve, x_in[:, u], c)
                    for t in range(4):
                        nc.vector.tensor_scalar(x_in[:, u, t, :], x_in[:, u, t, :], ln.mean[:, t:t + 1],
                                                ln.rstd[:, t:t + 1], ALU.subtract, ALU.mult).then_inc(normed, 1)
                    for t in range(4):
                        dve.wait_ge(x_tr, c * 4 + (t + 1))
                        dst = q_t[:, :, (t % 2) * 16:(t % 2) * 16 + 16, bass.ds(i * 4 + (2 * u + t // 2), 1), :]
                        nc.vector.tensor_copy(dst, tr[t][:, :].rearrange("p (k h o i) -> p k h o i", k=KD, o=1, i=SSM_I)
                                              ).then_inc(x_out, 1)

        @block.scalar
        def _(act):
            nc.scalar.preload_act_table(ACT.Sqrt)
            with act.Fori(0, NCH // 2) as i:
                for u in range(2):
                    c = i * 2 + u
                    ln.root(nc, act, c)
                    for t in range(4):
                        act.wait_ge(c_tr, c * 4 + (t + 1))
                        dst = c_t[:, :, (t % 2) * 16:(t % 2) * 16 + 16, bass.ds(i * 4 + (2 * u + t // 2), 1), :]
                        nc.scalar.activation(dst, tr[4 + t][:, :].rearrange("p (k h o i) -> p k h o i", k=KD, o=1, i=SSM_I),
                                             ACT.Copy).then_inc(c_out, 1)

        @block.tensor
        def _(pe):
            with pe.Fori(0, NCH // 2) as i:
                for u in range(2):
                    c = i * 2 + u
                    pe.wait_ge(loaded[u], (i + 1) * 32)
                    for t in range(4):
                        pe.wait_ge(c_out, c * 4 + (t + 1))
                        for b in range(KD):
                            last = nc.tensor.transpose(tr[4 + t][:, b * P:(b + 1) * P], c_in[:, u, t, b * P:(b + 1) * P], k.ident[:, :])
                        last.then_inc(c_tr, 1)
                    for t in range(4):
                        pe.wait_ge(normed, c * 4 + (t + 1))
                        pe.wait_ge(x_out, c * 4 + (t + 5))
                        for b in range(KD):
                            last = nc.tensor.transpose(tr[t][:, b * P:(b + 1) * P], x_in[:, u, t, b * P:(b + 1) * P], k.ident[:, :])
                        last.then_inc(x_tr, 1)

        @block.gpsimd
        def _(pool):
            nc.gpsimd.nop().then_inc(c_out, 4)
            nc.gpsimd.nop().then_inc(x_out, 8)



def conv_phase(nc, k, q_t, c_t, ssm_reversed, ssm_d, x, x1):
    assert GH * SSM_I == P
    STEPS = SSM_H // 2
    GSTEPS = GH // 2
    with phase(nc) as st:
        sb, ps, sem = opener(nc, st)
        d_all = sb("d_all", [P, SSM_H])
        toep = sb("toep", [P, 2, 2, D])
        toep_hi, toep_lo = sb("toep_hi", [P, 2, 2, D], F16), sb("toep_lo", [P, 2, 2, D], F16)
        prod = sb("prod", [P, KD, 2 * B, PAIRS])
        prod_hi = sb("prod_hi", [P, 2, KD, 2 * B, PAIRS], F16)
        prod_lo = sb("prod_lo", [P, 2, KD, 2 * B, PAIRS], F16)
        y = sb("y", [P, 2, KD, 2 * B, PAIRS])
        terms = sb("terms", [P, SSM_I, KD, 2 * B, SSM_I])
        sums = sb("sums", [P, 2, KD, B, GH, SSM_I])
        x_rows, gated = sb("x_rows", [P, B, D]), sb("gated", [P, B, D])
        conv = ps("conv", [P, 2, KD, D])
        d_loaded = sem("d_loaded")
        toep_loaded = [sem(f"toep_loaded{u}") for u in range(2)]
        toep_summed = sem("toep_summed")
        toep_hi_done, toep_lo_done = sem("toep_hi_done"), sem("toep_lo_done")
        prod_done, prod_hi_done, prod_lo_done = sem("prod_done"), sem("prod_hi_done"), sem("prod_lo_done")
        conv_done, conv_read = sem("conv_done"), sem("conv_read")
        weighed, half_sums, summed = sem("weighed"), sem("half_sums"), sem("summed")
        sum_done, sum_read = sem("sum_done"), sem("sum_read")
        x_loaded, x_added, x_stored = sem("x_loaded"), sem("x_added"), sem("x_stored")
        block = st.enter_context(nc.Block())
        x_g = x.rearrange("b (g r) d -> g r b d", g=GROUPS)
        x1_g = x1.rearrange("b (g r) d -> g r b d", g=GROUPS)

        def toeplitz(s, u):
            return bass.AP(tensor=ssm_reversed.tensor, offset=s * (2 * (P + D)),
                           ap=[[1, P], [P + D, 2], [1, D]])

        @block.sync
        def _(sp):
            sp.dma_start(d_all[:, :], ssm_d.partition_broadcast(P)).then_inc(d_loaded, 16)
            with sp.Fori(0, GROUPS) as g:
                sp.wait_ge(x_stored, (g + 1) * 16)
                sp.dma_start(x_rows[:, :, :], x_g[bass.ds(g, 1), :, :, :].rearrange("o r b d -> (o r) b d")
                             ).then_inc(x_loaded, 16)
                for j in range(GSTEPS):
                    s, u = g * GSTEPS + j, j % 2
                    sp.wait_ge(toep_lo_done, s + 1)
                    sp.dma_start(toep[:, u], toeplitz(s, u)).then_inc(toep_loaded[u], 16)
                sp.wait_ge(x_added, g + 1)
                sp.dma_start(x1_g[bass.ds(g, 1), :, :, :].rearrange("o r b d -> (o r) b d"), gated[:, :, :]
                             ).then_inc(x_stored, 16)
            sp.wait_ge(x_stored, (GROUPS + 1) * 16)

        @block.vector
        def _(dve):
            dve.wait_ge(d_loaded, 16)

            def make_products(g, j):
                s, u = g * GSTEPS + j, j % 2
                dve.wait_ge(toep_loaded[u], g * (GSTEPS * 8) + (j // 2 + 1) * 16)
                for e in range(2):
                    nc.vector.scalar_tensor_tensor(toep[:, u, e, D - P:D], k.ident[:, ::-1], d_all[:, bass.ds(s * 2 + e, 1)],
                                                   toep[:, u, e, D - P:D], ALU.mult, ALU.add).then_inc(toep_summed, 1)
                dve.wait_ge(prod_hi_done, s + 1)
                dve.wait_ge(prod_lo_done, s + 1)
                ch = c_t[:, :, bass.ds(s * 2, 2), :, :].rearrange("p k h b i -> p k (h b) i")
                for i in range(SSM_I):
                    n = SSM_I - i
                    nc.vector.tensor_tensor(prod[:, :, :, pair_at(i):pair_at(i) + n],
                                            ch[:, :, :, i:i + 1].to_broadcast([P, KD, 2 * B, n]),
                                            ch[:, :, :, i:SSM_I], ALU.mult).then_inc(prod_done, 1)

            def weigh(g, j):
                s = g * GSTEPS + j
                dve.wait_ge(conv_read, s * 2 + 6)
                dve.wait_ge(summed, s * 2 + 2)
                q = q_t[:, :, bass.ds(s * 2, 2), :, :].rearrange("p k h b i -> p k (h b) i")
                for i in range(SSM_I):
                    n = SSM_I - i
                    last = nc.vector.tensor_tensor(terms[:, i, :, :, i:SSM_I], y[:, j % 2, :, :, pair_at(i):pair_at(i) + n],
                                                   q[:, :, :, i:i + 1].to_broadcast([P, KD, 2 * B, n]), ALU.mult)
                    if i < SSM_I - 1:
                        dst = terms[:, i + 1:SSM_I, :, :, i].rearrange("p i k b -> p k b i")
                        last = nc.vector.tensor_tensor(dst, y[:, j % 2, :, :, pair_at(i) + 1:pair_at(i) + n],
                                                       q[:, :, :, i + 1:SSM_I], ALU.mult)
                last.then_inc(weighed, 1)
                dve.wait_ge(weighed, s + 3)
                flat = terms[:, :, :, :, :].rearrange("p i k b j -> p i (k b j)")
                nc.vector.tensor_tensor(flat[:, 0:4], flat[:, 0:4], flat[:, 4:8], ALU.add).then_inc(half_sums, 1)
                dve.wait_ge(half_sums, s + 1)
                for e in range(2):
                    dst = sums[:, :, :, :, 2 * j + e].rearrange("p i k b j -> p (i k) b j")
                    src = terms[:, :, :, e * B:(e + 1) * B, :].rearrange("p i k b j -> p (i k) b j")
                    nc.vector.tensor_tensor(dst, src[:, 0:2 * KD], src[:, 2 * KD:4 * KD], ALU.add).then_inc(summed, 1)

            with dve.Fori(0, GROUPS) as g:
                for j in range(GSTEPS):
                    make_products(g, j)
                    if j == 2:
                        dve.wait_ge(sum_done, (g + 1) * B)
                    if j >= 2:
                        weigh(g, j - 2)
                weigh(g, GSTEPS - 2)
                weigh(g, GSTEPS - 1)

        @block.scalar
        def _(act):
            nc.scalar.preload_act_table(ACT.Copy)
            nc.scalar.nop().then_inc(prod_hi_done, 1)
            nc.scalar.nop().then_inc(sum_read, B)
            nc.scalar.nop().then_inc(conv_read, 4)

            def copy_out(g, j):
                s = g * GSTEPS + j
                act.wait_ge(weighed, s + 1)
                for e in range(2):
                    act.wait_ge(conv_done, s * 2 + (e + 1))
                    nc.scalar.activation(y[:, j % 2, :, e * B:(e + 1) * B, :].rearrange("p k b r -> p k (b r)"),
                                         conv[:, e, :, 0:B * PAIRS], ACT.Copy).then_inc(conv_read, 1)

            with act.Fori(0, GROUPS) as g:
                for j in range(GSTEPS):
                    s, u = g * GSTEPS + j, j % 2
                    act.wait_ge(toep_summed, (s + 1) * 2)
                    nc.scalar.activation(toep_hi[:, u], toep[:, u, :, ::-1], ACT.Copy).then_inc(toep_hi_done, 1)
                    act.wait_ge(prod_done, (s + 1) * SSM_I)
                    nc.scalar.activation(prod_hi[:, u].rearrange("p k b r -> p (k b r)"),
                                         prod[:, :, :, :].rearrange("p k b r -> p (k b r)"), ACT.Copy).then_inc(prod_hi_done, 1)
                    if j:
                        copy_out(g, j - 1)
                copy_out(g, GSTEPS - 1)
                act.wait_ge(x_stored, (g + 1) * 16)
                for b in range(B):
                    act.wait_ge(sum_done, (g + 1) * B + (b + 1))
                    nc.scalar.activation(gated[:, b, :], conv[:, b // KD, b % KD, :], ACT.Copy,
                                         scale=k.tanh_gates[:, 0:1]).then_inc(sum_read, 1)

        @block.gpsimd
        def _(pool):
            nc.gpsimd.nop().then_inc(toep_lo_done, 2)
            nc.gpsimd.nop().then_inc(prod_lo_done, 1)
            nc.gpsimd.nop().then_inc(weighed, 2)
            nc.gpsimd.nop().then_inc(summed, 2)
            nc.gpsimd.nop().then_inc(sum_done, B)
            nc.gpsimd.nop().then_inc(x_stored, 16)
            with pool.Fori(0, GROUPS) as g:
                for j in range(GSTEPS):
                    s, u = g * GSTEPS + j, j % 2
                    pool.wait_ge(toep_hi_done, s + 1)
                    pool.wait_ge(conv_read, (s + 1) * 2)
                    nc.gpsimd.tensor_tensor(toep_lo[:, u], toep[:, u, :, ::-1], toep_hi[:, u], ALU.subtract).then_inc(toep_lo_done, 1)
                    pool.wait_ge(prod_hi_done, s + 2)
                    nc.gpsimd.tensor_tensor(prod_lo[:, u].rearrange("p k b r -> p (k b r)"),
                                            prod[:, :, :, :].rearrange("p k b r -> p (k b r)"),
                                            prod_hi[:, u].rearrange("p k b r -> p (k b r)"), ALU.subtract).then_inc(prod_lo_done, 1)
                pool.wait_ge(x_loaded, (g + 1) * 16)
                pool.wait_ge(sum_read, (g + 2) * B)
                nc.gpsimd.tensor_tensor(gated[:, :, :], gated[:, :, :], x_rows[:, :, :], ALU.add).then_inc(x_added, 1)

        @block.tensor
        def _(pe):
            with pe.Fori(0, GROUPS) as g:
                for j in range(GSTEPS):
                    s, u = g * GSTEPS + j, j % 2
                    pe.wait_ge(toep_lo_done, s + 3)
                    pe.wait_ge(prod_lo_done, s + 2)
                    if j == 0:
                        pe.wait_ge(sum_read, (g + 1) * B)
                    for e in range(2):
                        pe.wait_ge(conv_read, s * 2 + (e + 3))
                        for m in range(KD):
                            out = conv[:, e, m, 0:B * PAIRS]
                            for n in range(m + 1):
                                t = slice((m - n) * P, (m - n + 1) * P)
                                hi = prod_hi[:, u, n, e * B:(e + 1) * B, :]
                                lo = prod_lo[:, u, n, e * B:(e + 1) * B, :]
                                nc.tensor.matmul(out, toep_hi[:, u, e, t], hi, start=(n == 0), stop=False)
                                nc.tensor.matmul(out, toep_hi[:, u, e, t], lo, start=False, stop=False)
                                last = nc.tensor.matmul(out, toep_lo[:, u, e, t], hi, start=False, stop=(n == m))
                        last.then_inc(conv_done, 1)
                pe.wait_ge(conv_read, (g + 1) * GH + 4)
                pe.wait_ge(summed, (g + 1) * GH + 2)
                for b in range(B):
                    for m in range(KD):
                        out = conv[:, b // KD, b % KD, m * P:(m + 1) * P]
                        for i in range(2):
                            last = nc.tensor.matmul(out, sums[:, i, m, b].rearrange("p h j -> p (h j)"), k.ident[:, :],
                                                    is_transpose=True, start=(i == 0), stop=(i == 1))
                    last.then_inc(sum_done, 1)


E, I_MOE = 8, 352
I_SH = 704
MK = -(-I_MOE // P)
SK = -(-I_SH // P)
TILES = (2 * T + E * (P - 1)) // P
SLOTS = TILES * P


def rows_of(width, m):
    return min(P, width - m * P)


def shared_phase(nc, k, w, x1, xn_out, x1s, router_t, gate, up, s_gate, s_gate_b, s_up, s_up_b, s_down, s_down_b):
    with phase(nc) as st:
        sb, ps, sem = opener(nc, st)
        ln = LayerNorm(sb, sem, "x1")
        x_in = sb("x1_in", [P, 2, 4, D])
        xn = sb("xn", [P, 4, D])
        xt_hi, xt_lo = sb("xt_hi", [P, KD, CH], F16), sb("xt_lo", [P, KD, CH], F16)
        sg_hi, sg_lo = sb("sg_hi", [P, KD, I_SH], F16), sb("sg_lo", [P, KD, I_SH], F16)
        su_hi, su_lo = sb("su_hi", [P, KD, I_SH], F16), sb("su_lo", [P, KD, I_SH], F16)
        sd_hi, sd_lo = sb("sd_hi", [P, SK, D], F16), sb("sd_lo", [P, SK, D], F16)
        rw, rw_hi, rw_lo = sb("rw", [P, KD, E]), sb("rw_hi", [P, KD, E], F16), sb("rw_lo", [P, KD, E], F16)
        bg, bu, bd = sb("bg", [P, SK]), sb("bu", [P, SK]), sb("bd", [P, D])
        stage = sb("stage", [P, 2, KD * I_MOE])
        silu, h = sb("silu", [P, 2, CH]), sb("h", [P, 2, CH])
        h_hi, h_lo = sb("h_hi", [P, SK, CH], F16), sb("h_lo", [P, SK, CH], F16)
        summed = sb("ffn_sum", [P, D])
        tr = ps("tr", [P, KD, CH])
        gu = ps("gu", [P, 2, 2, CH])

        small_loaded = sem("small_loaded")
        stage_loaded = [sem(f"stage_loaded{u}") for u in range(2)]
        x_loaded = [sem(f"x1_loaded{u}") for u in range(2)]
        sw_hi, sw_lo = sem("sw_hi"), sem("sw_lo")
        ew_hi, ew_lo = sem("ew_hi"), sem("ew_lo")
        normed, xn_stored, turned = sem("xn_normed"), sem("xn_stored"), sem("turned")
        xt_hi_done, xt_lo_done = sem("xt_hi_done"), sem("xt_lo_done")
        routed, logits_read = sem("routed"), sem("logits_read")
        gu_done, silu_done, h_done = sem("gu_done"), sem("silu_done"), sem("h_done")
        h_hi_done, h_lo_done = sem("h_hi_done"), sem("h_lo_done")
        down_done, bias_added, out_done, out_stored = sem("down_done"), sem("bias_added"), sem("out_done"), sem("out_stored")
        block = st.enter_context(nc.Block())
        x1_d, x1s_d, xn_d = (a.rearrange("(c k p) d -> p (c k) d", p=P, k=4) for a in (x1, x1s, xn_out))

        pieces = []
        for hi, lo, m in ((sg_hi, sg_lo, s_gate), (su_hi, su_lo, s_up)):
            for b in range(0, KD, 2):
                pieces.append((hi[:, b:b + 2, :], lo[:, b:b + 2, :], m[b * P:(b + 2) * P, :].rearrange("(k p) n -> p k n", p=P), P))
        whole = I_SH // P
        for b in range(0, whole, 2):
            e = min(b + 2, whole)
            pieces.append((sd_hi[:, b:e, :], sd_lo[:, b:e, :], s_down[b * P:e * P, :].rearrange("(k p) n -> p k n", p=P), P))
        rest = I_SH - whole * P
        pieces.append((sd_hi[0:rest, whole:SK, :], sd_lo[0:rest, whole:SK, :],
                       s_down[whole * P:I_SH, :].rearrange("(k p) n -> p k n", k=1), rest))
        NP = len(pieces)
        assert NP % 2 == 0

        def staged(piece, u):
            hi, _, _, rows = piece
            k_, n = hi.shape[1], hi.shape[2]
            return stage[0:rows, u, 0:k_ * n].rearrange("p (k n) -> p k n", n=n)

        @block.sync
        def _(sp):
            def load_x(c, u):
                sp.wait_ge(out_stored, c * 16 + 16)
                sp.dma_start(x_in[:, u], x1_d[:, bass.ds(c * 4, 4), :]).then_inc(x_loaded[u], 16)

            load_x(0, 0)
            sp.dma_start(rw[:, :, :], router_t.rearrange("(k p) e -> p k e", p=P)).then_inc(small_loaded, 16)
            sp.dma_start(bd[:, :], s_down_b.partition_broadcast(P)).then_inc(small_loaded, 16)
            for dst, b in ((bg, s_gate_b), (bu, s_up_b)):
                sp.dma_start(dst[:, :], b).then_inc(small_loaded, 16)
            for n, piece in enumerate(pieces):
                if n >= 2:
                    sp.wait_ge(sw_lo, n - 1)
                sp.dma_start(staged(piece, n % 2), piece[2]).then_inc(stage_loaded[n % 2], 16)
            sp.wait_ge(sw_lo, NP)

            def chunk(c, u, last):
                if not last:
                    load_x(c + 1, 1 - u)
                sp.wait_ge(normed, (c + 1) * 4)
                sp.dma_start(xn_d[:, bass.ds(c * 4, 4), :], xn[:, :, :]).then_inc(xn_stored, 16)
                for q in range(4):
                    sp.wait_ge(ew_lo, c * 4 + (q + 1))
                    src = (gate, up)[q % 2][bass.ds(c * 2 + q // 2, 1), :, :].rearrange("o (k p) i -> p (o k) i", p=P)
                    sp.dma_start(stage[:, q % 2, :].rearrange("p (k i) -> p k i", k=KD), src).then_inc(stage_loaded[q % 2], 16)
                sp.wait_ge(out_done, (c + 2) * 4)
                sp.dma_start(x1s_d[:, bass.ds(c * 4, 4), :], x_in[:, u]).then_inc(out_stored, 16)

            for c in range(NCH):
                chunk(c, c % 2, c == NCH - 1)
            sp.wait_ge(out_stored, (NCH + 2) * 16)
            sp.wait_ge(xn_stored, (NCH + 1) * 16)

        @block.scalar
        def _(act):
            nc.scalar.nop().then_inc(xn_stored, 16)
            ln.root(nc, act, 0)
            for n, piece in enumerate(pieces):
                act.wait_ge(stage_loaded[n % 2], (n // 2 + 1) * 16)
                nc.scalar.activation(piece[0], staged(piece, n % 2), ACT.Copy).then_inc(sw_hi, 1)

            def chunk(c, last):
                for b in range(KD):
                    act.wait_ge(turned, c * KD + (b + 1))
                    nc.scalar.activation(xt_hi[:, b, :], tr[:, b, :], ACT.Copy).then_inc(xt_hi_done, 1)
                for m in range(SK):
                    r, u = rows_of(I_SH, m), m % 2
                    act.wait_ge(gu_done, c * SK + (m + 1))
                    act.wait_ge(h_done, c * SK + (m + 1))
                    nc.scalar.activation(silu[0:r, u, :], gu[0:r, u, 0, :], ACT.Silu, bias=bg[0:r, m:m + 1]).then_inc(silu_done, 1)
                    if m < 4:
                        split_expert(c, m)
                    act.wait_ge(h_done, c * SK + (m + 3))
                    nc.scalar.activation(h_hi[0:r, m, :], h[0:r, u, :], ACT.Copy).then_inc(h_hi_done, 1)
                if not last:
                    ln.root(nc, act, c + 1)

            def split_expert(c, q):
                act.wait_ge(stage_loaded[q % 2], c * 32 + (NP // 2 + q // 2 + 1) * 16)
                dst = (w.gate_hi, w.up_hi)[q % 2][:, bass.ds(c * 2 + q // 2, 1), :, :].rearrange("p o k i -> p (o k i)")
                nc.scalar.activation(dst, stage[:, q % 2, :], ACT.Copy).then_inc(ew_hi, 1)

            for c in range(NCH):
                chunk(c, c == NCH - 1)

        @block.gpsimd
        def _(pool):
            nc.gpsimd.nop().then_inc(out_stored, 32)
            nc.gpsimd.nop().then_inc(ew_lo, 2)
            nc.gpsimd.nop().then_inc(h_done, 2)
            nc.gpsimd.nop().then_inc(logits_read, 1)
            nc.gpsimd.nop().then_inc(out_done, 4)

            def chunk(c):
                for m in range(SK):
                    r, u = rows_of(I_SH, m), m % 2
                    pool.wait_ge(h_hi_done, c * SK + (m + 1))
                    nc.gpsimd.tensor_tensor(h_lo[0:r, m, :], h[0:r, u, :], h_hi[0:r, m, :], ALU.subtract).then_inc(h_lo_done, 1)
                    if m < 4:
                        q = m
                        pool.wait_ge(ew_hi, c * 4 + (q + 1))
                        hi, lo = ((w.gate_hi, w.gate_lo), (w.up_hi, w.up_lo))[q % 2]
                        hi, lo = (a[:, bass.ds(c * 2 + q // 2, 1), :, :].rearrange("p o k i -> p (o k i)") for a in (hi, lo))
                        nc.gpsimd.tensor_tensor(lo, stage[:, q % 2, :], hi, ALU.subtract).then_inc(ew_lo, 1)

            for c in range(NCH):
                chunk(c)

        @block.vector
        def _(dve):
            def normalise(c, u):
                dve.wait_ge(x_loaded[u], (c // 2 + 1) * 16)
                ln.statistics(nc, dve, x_in[:, u], c)
                dve.wait_ge(xn_stored, (c + 1) * 16)
                for t in range(4):
                    nc.vector.tensor_scalar(xn[:, t, :], x_in[:, u, t, :], ln.mean[:, t:t + 1], ln.rstd[:, t:t + 1],
                                            ALU.subtract, ALU.mult).then_inc(normed, 1)

            normalise(0, 0)
            dve.wait_ge(small_loaded, 16 * 4)
            for n, piece in enumerate(pieces):
                dve.wait_ge(sw_hi, n + 1)
                nc.vector.tensor_tensor(piece[1], staged(piece, n % 2), piece[0], ALU.subtract).then_inc(sw_lo, 1)
            nc.vector.tensor_copy(rw_hi[:, :, :], rw[:, :, :]).then_inc(sw_lo, 1)
            dve.wait_ge(sw_lo, NP + 1)
            nc.vector.tensor_tensor(rw_lo[:, :, :], rw[:, :, :], rw_hi[:, :, :], ALU.subtract).then_inc(sw_lo, 1)

            def chunk(c, u, last):
                for b in range(KD):
                    dve.wait_ge(xt_hi_done, c * KD + (b + 1))
                    nc.vector.tensor_tensor(xt_lo[:, b, :], tr[:, b, :], xt_hi[:, b, :], ALU.subtract).then_inc(xt_lo_done, 1)
                dve.wait_ge(routed, c + 1)
                nc.vector.tensor_copy(k.logits[:, bass.ds(c * 4, 4), :], tr[:, 0, 0:4 * E].rearrange("p (t e) -> p t e", e=E)
                                      ).then_inc(logits_read, 1)
                for m in range(SK):
                    r, v = rows_of(I_SH, m), m % 2
                    dve.wait_ge(silu_done, c * SK + (m + 1))
                    if not (isinstance(c, int) and c == 0 and m < 2):
                        dve.wait_ge(h_lo_done, c * SK + (m - 1))
                    nc.vector.scalar_tensor_tensor(h[0:r, v, :], gu[0:r, v, 1, :], bu[0:r, m:m + 1], silu[0:r, v, :],
                                                   ALU.add, ALU.mult).then_inc(h_done, 1)
                if not last:
                    normalise(c + 1, 1 - u)
                for t in range(4):
                    dve.wait_ge(down_done, c * 4 + (t + 1))
                    dve.wait_ge(out_done, c * 4 + (t + 4))
                    nc.vector.tensor_tensor(summed[:, :], tr[:, t, :], bd[:, :], ALU.add).then_inc(bias_added, 1)
                    dve.wait_ge(bias_added, c * 4 + (t + 1))
                    nc.vector.scalar_tensor_tensor(x_in[:, u, t, :], summed[:, :], k.tanh_gates[:, 2:3], x_in[:, u, t, :],
                                                   ALU.mult, ALU.add).then_inc(out_done, 1)

            for c in range(NCH):
                chunk(c, c % 2, c == NCH - 1)

        @block.tensor
        def _(pe):
            def chunk(c, u):
                for b in range(KD):
                    for t in range(4):
                        if b == 0:
                            pe.wait_ge(normed, c * 4 + (t + 1))
                        if t == 0:
                            if not (isinstance(c, int) and c == 0):
                                pe.wait_ge(bias_added, (c - 1) * 4 + (b + 1))
                        last = nc.tensor.transpose(tr[:, b, t * P:(t + 1) * P], xn[:, t, b * P:(b + 1) * P], k.ident[:, :])
                    last.then_inc(turned, 1)
                if isinstance(c, int) and c == 0:
                    pe.wait_ge(sw_lo, NP + 2)
                pe.wait_ge(xt_lo_done, (c + 1) * KD)
                for t in range(4):
                    tok = slice(t * P, (t + 1) * P)
                    for b in range(KD):
                        for n, (x_, r_) in enumerate(((xt_hi, rw_hi), (xt_hi, rw_lo), (xt_lo, rw_hi))):
                            last = nc.tensor.matmul(tr[:, 0, t * E:(t + 1) * E], x_[:, b, tok], r_[:, b, :],
                                                    start=(b == 0 and n == 0), stop=(b == KD - 1 and n == 2))
                last.then_inc(routed, 1)
                for m in range(SK):
                    r, v = rows_of(I_SH, m), m % 2
                    cols = slice(m * P, m * P + r)
                    pe.wait_ge(h_done, c * SK + (m + 1))
                    for o, (hi, lo) in enumerate(((sg_hi, sg_lo), (su_hi, su_lo))):
                        for b in range(KD):
                            nc.tensor.matmul(gu[0:r, v, o, :], hi[:, b, cols], xt_hi[:, b, :], start=(b == 0), stop=False)
                            nc.tensor.matmul(gu[0:r, v, o, :], hi[:, b, cols], xt_lo[:, b, :], start=False, stop=False)
                            last = nc.tensor.matmul(gu[0:r, v, o, :], lo[:, b, cols], xt_hi[:, b, :], start=False, stop=(b == KD - 1))
                    last.then_inc(gu_done, 1)
                pe.wait_ge(logits_read, c + 2)
                pe.wait_ge(h_lo_done, (c + 1) * SK)
                for t in range(4):
                    tok = slice(t * P, (t + 1) * P)
                    for m in range(SK):
                        r = rows_of(I_SH, m)
                        nc.tensor.matmul(tr[:, t, :], h_hi[0:r, m, tok], sd_hi[0:r, m, :], start=(m == 0), stop=False)
                        nc.tensor.matmul(tr[:, t, :], h_hi[0:r, m, tok], sd_lo[0:r, m, :], start=False, stop=False)
                        last = nc.tensor.matmul(tr[:, t, :], h_lo[0:r, m, tok], sd_hi[0:r, m, :], start=False, stop=(m == SK - 1))
                    last.then_inc(down_done, 1)

            for c in range(NCH):
                chunk(c, c % 2)



def route_phase(nc, k, w, down, slot_token):
    C = 2 * TT
    with phase(nc) as st:
        sb, ps, sem = opener(nc, st)
        small = [P, TT, E]
        first_i, steps_i, tiles_i = sb("first_i", [P, E], I32), sb("steps_i", [P, TT], I32), sb("tiles_i", [P, TILES], I32)
        first, steps, tiles_f = sb("first", [P, E]), sb("steps", [P, TT]), sb("tiles_f", [P, TILES])
        token = sb("token", [P, TT], I32)
        zeros = sb("zeros", [TILES, P], I32)
        before, ones = sb("before", [P, P], F16), sb("ones", [P, P], F16)
        best = [sb(f"best{n}", [P, TT]) for n in range(2)]
        tie = [sb(f"tie{n}", small) for n in range(2)]
        tie_best = [sb(f"tie_best{n}", [P, TT]) for n in range(2)]
        pick = [sb(f"pick{n}", small) for n in range(2)]
        rest = sb("rest", small)
        picked = sb("picked", [P, 2 * TT, E], F16)
        gap, e2, den = sb("r_gap", [P, TT]), sb("r_e2", [P, TT]), sb("r_den", [P, TT])
        over, tiles_of, tiles_to = sb("over", [P, E, TT]), sb("tiles_of", [P, E]), sb("tiles_to", [P, E])
        one8, start = sb("one8", [P, E]), sb("start", [P, E])
        place, placed = sb("place", small), [sb(f"placed{n}", small) for n in range(2)]
        slot_f = sb("slot_f", [P, 2, TT])
        past, texp_f = sb("past", [P, TILES, E]), sb("texp_f", [P, TILES])
        stage = sb("d_stage", [P, 2, MK, D])
        rank, total = ps("rank", [P, TT * E]), ps("total", [P, E])
        consts_made, before_zeroed = sem("consts_made"), sem("before_zeroed")
        zero_stored = sem("zero_stored")
        chain = sem("route_chain")
        e2_done, picked_done, ranked = sem("e2_done"), sem("picked_done"), sem("ranked")
        gap_done, slots_done, scattered, listed = sem("gap_done"), sem("slots_done"), sem("scattered"), sem("listed")
        stage_loaded = [sem(f"d_stage_loaded{u}") for u in range(2)]
        d_hi, d_lo = sem("d_hi"), sem("d_lo")
        block = st.enter_context(nc.Block())
        whole = I_MOE // P
        tail = I_MOE - whole * P

        @block.sync
        def _(sp):
            sp.wait_ge(consts_made, 1)
            sp.dma_start(slot_token.rearrange("(t p) o -> t (p o)", p=P), zeros[:, :]).then_inc(zero_stored, 16)
            for e in range(E):
                if e >= 2:
                    sp.wait_ge(d_lo, 2 * (e - 1))
                u = e % 2
                sp.dma_start(stage[:, u, 0:whole, :], down[e, 0:whole * P, :].rearrange("(k p) n -> p k n", p=P)).then_inc(stage_loaded[u], 16)
                sp.dma_start(stage[0:tail, u, whole, :], down[e, whole * P:I_MOE, :]).then_inc(stage_loaded[u], 16)
            sp.wait_ge(scattered, C * 16)
            with nc.allow_non_contiguous_dma(reason="one token number a slot"):
                sp.dma_start(k.slot_token[:, :], slot_token.rearrange("(t p) o -> p (t o)", p=P)).then_inc(listed, 16)
            sp.wait_ge(listed, 16)

        @block.gpsimd
        def _(pool):
            nc.gpsimd.memset(zeros[:, :], 0).then_inc(consts_made, 1)
            nc.gpsimd.memset(before[:, :], 1.0).then_inc(before_zeroed, 1)
            nc.gpsimd.memset(ones[:, :], 1.0)
            nc.gpsimd.memset(picked[:, 0:TT, :], 0.0)
            nc.gpsimd.memset(one8[:, :], 1.0)
            nc.gpsimd.iota(first_i[:, :], pattern=[[-1, E]], base=E, channel_multiplier=0)
            nc.gpsimd.iota(steps_i[:, :], pattern=[[P, TT]], base=0, channel_multiplier=0)
            nc.gpsimd.iota(tiles_i[:, :], pattern=[[1, TILES]], base=0, channel_multiplier=0)
            nc.gpsimd.iota(token[:, :], pattern=[[P, TT]], base=0, channel_multiplier=1)
            pool.wait_ge(before_zeroed, 1)
            nc.gpsimd.affine_select(out=before[:, :], in_=before[:, :], compare_op=ALU.is_gt, fill=0.0,
                                    base=0, pattern=[[1, P]], channel_multiplier=-1).then_inc(consts_made, 1)
            pool.wait_ge(zero_stored, 16)
            pool.wait_ge(slots_done, 1)
            for t in range(TT):
                for n in range(2):
                    nc.gpsimd.indirect_dma_start(slot_token, bass.IndirectOffsetOnAxis(ap=k.slots[:, n, t:t + 1], axis=0),
                                                 token[:, t:t + 1], None).then_inc(scattered, 16)

        @block.scalar
        def _(act):
            nc.scalar.preload_act_table(ACT.Exp)
            act.wait_ge(gap_done, 1)
            nc.scalar.activation(e2[:, :], gap[:, :], ACT.Exp).then_inc(e2_done, 1)
            for e in range(E):
                act.wait_ge(stage_loaded[e % 2], (e // 2 + 1) * 32)
                nc.scalar.activation(w.down_hi[:, e, 0:whole, :], stage[:, e % 2, 0:whole, :], ACT.Copy).then_inc(d_hi, 1)
                nc.scalar.activation(w.down_hi[0:tail, e, whole, :], stage[0:tail, e % 2, whole, :], ACT.Copy).then_inc(d_hi, 1)

        @block.tensor
        def _(pe):
            pe.wait_ge(picked_done, 1)
            nc.tensor.matmul(rank[:, :], before[:, :], picked[:, TT:2 * TT, :], start=True, stop=False)
            for s in range(1, TT):
                nc.tensor.matmul(rank[:, :], ones[:, :], picked[:, TT - s:2 * TT - s, :], start=False, stop=(s == TT - 1))
            for t in range(TT):
                last = nc.tensor.matmul(total[:, :], ones[:, :], picked[:, TT + t, :], start=(t == 0), stop=(t == TT - 1))
            last.then_inc(ranked, 1)

        @block.vector
        def _(dve):
            done = [0]

            def then(*made):
                for m in made:
                    m.then_inc(chain, 1)
                done[0] += len(made)
                dve.wait_ge(chain, done[0])

            V = nc.vector
            over_e = lambda a: a[:, :].unsqueeze(2).to_broadcast([P, TT, E])
            dve.wait_ge(consts_made, 2)
            then(V.tensor_copy(first[:, :], first_i[:, :]), V.tensor_copy(steps[:, :], steps_i[:, :]),
                 V.tensor_copy(tiles_f[:, :], tiles_i[:, :]))
            scores = k.logits
            for n in range(2):
                then(V.tensor_reduce(best[n][:, :], scores[:, :, :], AX.X, ALU.max))
                then(V.tensor_tensor(tie[n][:, :, :], scores[:, :, :], over_e(best[n]), ALU.is_equal))
                then(V.tensor_tensor(tie[n][:, :, :], tie[n][:, :, :], first[:, :].unsqueeze(1).to_broadcast(small), ALU.mult))
                then(V.tensor_reduce(tie_best[n][:, :], tie[n][:, :, :], AX.X, ALU.max))
                then(V.tensor_tensor(pick[n][:, :, :], tie[n][:, :, :], over_e(tie_best[n]), ALU.is_equal))
                if n == 0:
                    then(V.scalar_tensor_tensor(rest[:, :, :].rearrange("p t e -> p (t e)"), pick[0][:, :, :].rearrange("p t e -> p (t e)"),
                                                -3e38, scores[:, :, :].rearrange("p t e -> p (t e)"), ALU.mult, ALU.add))
                    scores = rest
            V.tensor_tensor(picked[:, TT:2 * TT, :], pick[0][:, :, :], pick[1][:, :, :], ALU.add).then_inc(picked_done, 1)
            V.tensor_tensor(gap[:, :], best[1][:, :], best[0][:, :], ALU.subtract).then_inc(gap_done, 1)
            dve.wait_ge(e2_done, 1)
            then(V.tensor_scalar(den[:, :], e2[:, :], 1.0, None, ALU.add))
            then(V.reciprocal(den[:, :], den[:, :]))
            then(V.tensor_scalar(k.mix[:, 0, :], den[:, :], k.tanh_gates[:, 2:3], None, ALU.mult))
            then(V.tensor_tensor(k.mix[:, 1, :], k.mix[:, 0, :], e2[:, :], ALU.mult))
            dve.wait_ge(ranked, 1)
            then(V.tensor_tensor(over[:, :, :], total[:, :].unsqueeze(2).to_broadcast([P, E, TT]),
                                 steps[:, :].unsqueeze(1).to_broadcast([P, E, TT]), ALU.is_gt))
            then(V.tensor_reduce(tiles_of[:, :], over[:, :, :], AX.X, ALU.add))
            then(V.tensor_tensor_scan(tiles_to[:, :], one8[:, :], tiles_of[:, :], 0.0, ALU.mult, ALU.add))
            then(V.tensor_tensor(start[:, :], tiles_to[:, :], tiles_of[:, :], ALU.subtract),
                 V.tensor_tensor(past[:, :, :], tiles_to[:, :].unsqueeze(1).to_broadcast([P, TILES, E]),
                                 tiles_f[:, :].unsqueeze(2).to_broadcast([P, TILES, E]), ALU.is_le))
            then(V.tensor_scalar(start[:, :], start[:, :], float(P), None, ALU.mult),
                 V.tensor_reduce(texp_f[:, :], past[:, :, :], AX.X, ALU.add))
            then(V.tensor_tensor(place[:, :, :], rank[:, :].rearrange("p (t e) -> p t e", e=E),
                                 start[:, :].unsqueeze(1).to_broadcast(small), ALU.add),
                 V.tensor_scalar(k.tile_expert[:, :], texp_f[:, :], float(E - 1), None, ALU.min))
            then(*(V.tensor_tensor(placed[n][:, :, :], place[:, :, :], pick[n][:, :, :], ALU.mult) for n in range(2)))
            then(*(V.tensor_reduce(slot_f[:, n, :], placed[n][:, :, :], AX.X, ALU.add) for n in range(2)))
            V.tensor_copy(k.slots[:, :, :], slot_f[:, :, :]).then_inc(slots_done, 1)
            for e in range(E):
                dve.wait_ge(d_hi, 2 * e + 2)
                V.tensor_tensor(w.down_lo[:, e, 0:whole, :], stage[:, e % 2, 0:whole, :], w.down_hi[:, e, 0:whole, :], ALU.subtract).then_inc(d_lo, 1)
                V.tensor_tensor(w.down_lo[0:tail, e, whole, :], stage[0:tail, e % 2, whole, :], w.down_hi[0:tail, e, whole, :],
                                ALU.subtract).then_inc(d_lo, 1)




def expert_phase(nc, k, w, xn, y_out):
    U = 3
    assert TILES % U == 0
    MT = MK - 1
    TAIL = I_MOE - MT * P
    with phase(nc) as st:
        sb, ps, sem = opener(nc, st)
        rows = sb("e_rows", [P, U, D])
        xt_hi, xt_lo = sb("e_xt_hi", [P, U, D], F16), sb("e_xt_lo", [P, U, D], F16)
        silu, h = sb("e_silu", [P, U, I_MOE]), sb("e_h", [P, U, I_MOE])
        h_hi, h_lo = sb("e_h_hi", [P, U, MK, P], F16), sb("e_h_lo", [P, U, MK, P], F16)
        y = sb("e_y", [P, U, D])
        turn, h_turn = ps("e_turn", [P, D]), ps("e_h_turn", [P, MK, P])
        gate_ps, up_ps, out_ps = ps("e_gate", [P, 2, D]), ps("e_up", [P, 2, D]), ps("e_out", [P, 2, D])
        gathered = [sem(f"gathered{u}") for u in range(U)]
        stored = [sem(f"e_stored{u}") for u in range(U)]
        turned, xt_hi_done, xt_lo_done = sem("e_turned"), sem("e_xt_hi_done"), sem("e_xt_lo_done")
        expanded, silu_done, h_done = sem("e_expanded"), sem("e_silu_done"), sem("e_h_done")
        h_turned, h_hi_done, h_lo_done = sem("e_h_turned"), sem("e_h_hi_done"), sem("e_h_lo_done")
        contracted, y_done = sem("e_contracted"), sem("e_y_done")
        block = st.enter_context(nc.Block())
        BODY = 2 * U
        PEEL = 9
        LOOPS = (TILES - PEEL) // BODY
        assert PEEL + LOOPS * BODY == TILES

        def over_tiles(eng, step):
            for n in range(PEEL):
                step(n, n // U, n, n, 0)
            with eng.Fori(0, LOOPS) as i:
                for j in range(PEEL, PEEL + BODY):
                    step(i * BODY + j, i * 2 + j // U, j, PEEL, 0)
            for n in range(TILES, TILES + 3):
                step(n, n // U, n, PEEL, n - TILES + 1)

        @block.gpsimd
        def _(pool):
            for n in range(TILES):
                if n >= U:
                    pool.wait_ge(turned, n - U + 1)
                nc.gpsimd.indirect_dma_start(rows[:, n % U, :], None, xn,
                                             bass.IndirectOffsetOnAxis(ap=k.slot_token[:, n:n + 1], axis=0)
                                             ).then_inc(gathered[n % U], 16)

        @block.tensor
        def _(pe):
            def step(n, rounds, r, early, late):
                if not late:
                    u = r % U
                    pe.wait_ge(gathered[u], rounds * 16 + 16)
                    if early >= 1:
                        pe.wait_ge(xt_lo_done, n)
                    for c in range(KD):
                        last = nc.tensor.transpose(turn[:, c * P:(c + 1) * P], rows[:, u, c * P:(c + 1) * P], k.ident[:, :])
                    last.then_inc(turned, 1)
                if early >= 1 and late <= 1:
                    u, b = (r - 1) % U, (r - 1) % 2
                    expert = nc.tensor.value_load(k.tile_expert[0:1, bass.ds(n - 1, 1)], min_val=0, max_val=E - 1)
                    pe.wait_ge(xt_lo_done, n)
                    if early >= 3:
                        pe.wait_ge(h_done, n - 2)
                    for dst, hi, lo in ((gate_ps, w.gate_hi, w.gate_lo), (up_ps, w.up_hi, w.up_lo)):
                        out = dst[:, b, 0:I_MOE]
                        for c in range(KD):
                            x_hi, x_lo = (a[:, u, c * P:(c + 1) * P] for a in (xt_hi, xt_lo))
                            w_hi, w_lo = (a[:, bass.ds(expert, 1), c, :].rearrange("p o i -> p (o i)") for a in (hi, lo))
                            nc.tensor.matmul(out, x_hi, w_hi, start=(c == 0), stop=False)
                            nc.tensor.matmul(out, x_lo, w_hi, start=False, stop=False)
                            last = nc.tensor.matmul(out, x_hi, w_lo, start=False, stop=(c == KD - 1))
                    last.then_inc(expanded, 1)
                if early >= 2 and late <= 2:
                    u = (r - 2) % U
                    pe.wait_ge(h_done, n - 1)
                    if early >= 3:
                        pe.wait_ge(h_lo_done, (n - 2) * 2)
                    for q in range(MK):
                        i_ = slice(q * P, min((q + 1) * P, I_MOE))
                        last = nc.tensor.transpose(h_turn[0:i_.stop - i_.start, q, :], h[:, u, i_], k.ident[:, :])
                    last.then_inc(h_turned, 1)
                if early >= 3:
                    u, b = (r - 3) % U, (r - 3) % 2
                    expert = nc.tensor.value_load(k.tile_expert[0:1, bass.ds(n - 3, 1)], min_val=0, max_val=E - 1)
                    pe.wait_ge(h_lo_done, (n - 2) * 2)
                    if early >= 5:
                        pe.wait_ge(y_done, n - 4)
                    for q in range(MK):
                        n_ = min(P, I_MOE - q * P)
                        a_hi, a_lo = (a[0:n_, u, q, :] for a in (h_hi, h_lo))
                        w_hi, w_lo = (a[0:n_, bass.ds(expert, 1), q, :].rearrange("p o d -> p (o d)") for a in (w.down_hi, w.down_lo))
                        nc.tensor.matmul(out_ps[:, b, :], a_hi, w_hi, start=(q == 0), stop=False)
                        nc.tensor.matmul(out_ps[:, b, :], a_lo, w_hi, start=False, stop=False)
                        last = nc.tensor.matmul(out_ps[:, b, :], a_hi, w_lo, start=False, stop=(q == MK - 1))
                    last.then_inc(contracted, 1)
            over_tiles(pe, step)

        parts = ((slice(0, P), slice(0, MT)), (slice(0, TAIL), slice(MT, MK)))

        @block.scalar
        def _(act):
            nc.scalar.preload_act_table(ACT.Silu)

            def step(n, rounds, r, early, late):
                if not late:
                    act.wait_ge(turned, n + 1)
                    if early >= 3:
                        act.wait_ge(expanded, n - 2)
                    nc.scalar.activation(xt_hi[:, r % U, :], turn[:, :], ACT.Copy).then_inc(xt_hi_done, 1)
                if early >= 1 and late <= 1:
                    act.wait_ge(expanded, n)
                    nc.scalar.activation(silu[:, (r - 1) % U, :], gate_ps[:, (r - 1) % 2, 0:I_MOE], ACT.Silu).then_inc(silu_done, 1)
                if early >= 2 and late <= 2:
                    act.wait_ge(h_turned, n - 1)
                    if early >= 5:
                        act.wait_ge(contracted, n - 4)
                    for rows_, blocks in parts:
                        nc.scalar.activation(h_hi[rows_, (r - 2) % U, blocks, :], h_turn[rows_, blocks, :], ACT.Copy).then_inc(h_hi_done, 1)
            over_tiles(act, step)

        @block.vector
        def _(dve):
            def step(n, rounds, r, early, late):
                if not late:
                    dve.wait_ge(xt_hi_done, n + 1)
                    nc.vector.tensor_tensor(xt_lo[:, r % U, :], turn[:, :], xt_hi[:, r % U, :], ALU.subtract).then_inc(xt_lo_done, 1)
                if early >= 1 and late <= 1:
                    dve.wait_ge(silu_done, n)
                    if early >= 4:
                        dve.wait_ge(h_turned, n - 3)
                    nc.vector.tensor_tensor(h[:, (r - 1) % U, :], up_ps[:, (r - 1) % 2, 0:I_MOE], silu[:, (r - 1) % U, :],
                                            ALU.mult).then_inc(h_done, 1)
                if early >= 2 and late <= 2:
                    dve.wait_ge(h_hi_done, (n - 1) * 2)
                    for rows_, blocks in parts:
                        nc.vector.tensor_tensor(h_lo[rows_, (r - 2) % U, blocks, :], h_turn[rows_, blocks, :],
                                                h_hi[rows_, (r - 2) % U, blocks, :], ALU.subtract).then_inc(h_lo_done, 1)
                if early >= 3:
                    u, b = (r - 3) % U, (r - 3) % 2
                    dve.wait_ge(contracted, n - 2)
                    if early >= 6:
                        dve.wait_ge(stored[u], rounds * 16 - 16)
                    nc.vector.tensor_copy(y[:, u, :], out_ps[:, b, :]).then_inc(y_done, 1)
            over_tiles(dve, step)

        @block.sync
        def _(sp):
            with sp.Fori(0, TILES // U) as i:
                for u in range(U):
                    sp.wait_ge(y_done, i * U + (u + 1))
                    sp.dma_start(y_out[bass.ds((i * U + u) * P, P), :], y[:, u, :]).then_inc(stored[u], 16)
            for u in range(U):
                sp.wait_ge(stored[u], TILES // U * 16)


HEADS1 = 16
HD1 = D // HEADS1
QUAD = P // HD1
XATTN_EPS = 1e-6
KV_SCALE = 1.0 / N


def xattn_phase(nc, k, x1s, y_rows, ctx, wq_t, wg_t, bg_cols, wkv_t, wo_t, x3):
    with phase(nc) as st:
        sb, ps, sem = opener(nc, st)
        ln = LayerNorm(sb, sem, "x2")
        wq, wg, wkv, wo = (tuple(sb(f"{n}_{q}", [P, KD, m], F16) for q in ("hi", "lo"))
                           for n, m in (("wq", D), ("wg", D), ("wkv", 2 * D), ("wo", D)))
        stage = sb("a_stage", [P, 2, 2, 2 * D])
        bg = sb("a_bg", [P, KD])
        mask = sb("a_mask", [P, 2 * P])
        ctx_in, x2 = sb("a_ctx", [P, 4, D]), sb("a_x2", [P, 2, 4, D])
        y_in = sb("a_y", [P, 2, 2, D])
        xn = sb("a_xn", [P, 4, D])
        ct = tuple(sb(f"a_ct_{q}", [P, KD, CH], F16) for q in ("hi", "lo"))
        xt = tuple(sb(f"a_xt_{q}", [P, KD, CH], F16) for q in ("hi", "lo"))
        low, low_exp = sb("a_low", [P, 2, D]), sb("a_low_exp", [P, 2, D])
        feat = sb("a_feat", [P, 2, D])
        k_hi, k_lo = sb("a_k_hi", [P, 4, D], F16), sb("a_k_lo", [P, 4, D], F16)
        q_hi, q_lo = sb("a_q_hi", [P, KD, CH], F16), sb("a_q_lo", [P, KD, CH], F16)
        v_hi, v_lo = sb("a_v_hi", [P, 4, KD, 2 * P], F16), sb("a_v_lo", [P, 4, KD, P], F16)
        gate = sb("a_gate", [P, KD, CH])
        kv = sb("a_kv", [P, 2, KD, 2, P])
        kv_hi, kv_lo = sb("a_kv_hi", [P, 2, KD, 2, P], F16), sb("a_kv_lo", [P, 2, KD, 2, P], F16)
        denom, mixed = sb("a_denom", [P, 2, N]), sb("a_mixed", [P, 2, N])
        a_hi, a_lo = sb("a_a_hi", [P, KD, CH], F16), sb("a_a_lo", [P, KD, CH], F16)
        tr = ps("a_tr", [P, 2, KD, P])
        pair = ps("a_pair", [P, 2, 2, D])
        sm = ps("a_sm", [P, 2, 2, N])

        w_loaded = [sem(f"a_w_loaded{u}") for u in range(2)]
        small_loaded, mask_made, mask_scaled, bg_negated = (sem(f"a_{n}") for n in ("small_loaded", "mask_made", "mask_scaled", "bg_negated"))
        w_hi, w_lo = sem("a_w_hi"), sem("a_w_lo")
        ctx_loaded, x_loaded = sem("a_ctx_loaded"), [sem(f"a_x_loaded{u}") for u in range(2)]
        y_loaded = [sem(f"a_y_loaded{u}") for u in range(2)]
        first_added, combined, normed = sem("a_first_added"), sem("a_combined"), sem("a_normed")
        turned, t_hi, t_lo = sem("a_turned"), sem("a_t_hi"), sem("a_t_lo")
        pair_done, pair_read = sem("a_pair_done"), sem("a_pair_read")
        v_hi_done, low_done, low_exp_done = sem("a_v_hi_done"), sem("a_low_done"), sem("a_low_exp_done")
        feat_done, feat_hi, feat_lo = sem("a_feat_done"), sem("a_feat_hi"), sem("a_feat_lo")
        v_lo_done, gate_exp = sem("a_v_lo_done"), sem("a_gate_exp")
        sm_done = sem("a_sm_done")
        kv_done, kv_hi_done, kv_lo_done = sem("a_kv_done"), sem("a_kv_hi_done"), sem("a_kv_lo_done")
        denom_done, recip_done, mixed_done = sem("a_denom_done"), sem("a_recip_done"), sem("a_mixed_done")
        a_hi_done, a_lo_done, stored = sem("a_a_hi_done"), sem("a_a_lo_done"), sem("a_stored")
        block = st.enter_context(nc.Block())
        x1s_d, x3_d, ctx_d = (a.rearrange("(c k p) d -> p (c k) d", p=P, k=4) for a in (x1s, x3, ctx))

        pieces = [(m, dst, b) for m, dst in ((wkv_t, wkv), (wq_t, wq), (wg_t, wg), (wo_t, wo)) for b in (0, 2)]
        NP = len(pieces)

        def staged(n):
            cols = pieces[n][1][0].shape[2]
            return stage[:, n % 2, :, 0:cols]

        @block.sync
        def _(sp):
            def load(c):
                u = c % 2
                if c >= 1:
                    sp.wait_ge(turned, 8 * c - 4)
                sp.dma_start(ctx_in[:, :, :], ctx_d[:, c * 4:c * 4 + 4, :]).then_inc(ctx_loaded, 16)
                if c >= 2:
                    sp.wait_ge(stored, (c - 1) * 16)
                sp.dma_start(x2[:, u], x1s_d[:, c * 4:c * 4 + 4, :]).then_inc(x_loaded[u], 16)

            load(0)
            sp.dma_start(bg[:, :], bg_cols).then_inc(small_loaded, 16)
            for n, (m, dst, b) in enumerate(pieces):
                if n >= 2:
                    sp.wait_ge(w_lo, n - 1)
                sp.dma_start(staged(n), m[b * P:(b + 2) * P, :].rearrange("(k p) n -> p k n", p=P)).then_inc(w_loaded[n % 2], 16)
            for c in range(NCH):
                if c < NCH - 1:
                    load(c + 1)
                sp.wait_ge(pair_read, c * 12 + 12)
                sp.dma_start(x3_d[:, c * 4:c * 4 + 4, :], x2[:, c % 2]).then_inc(stored, 16)
            sp.wait_ge(stored, NCH * 16)

        @block.gpsimd
        def _(pool):
            nc.gpsimd.memset(v_hi[:, :, :, P:2 * P], 1.0).then_inc(mask_made, 1)
            nc.gpsimd.memset(mask[:, :], 0.0).then_inc(mask_made, 1)
            pool.wait_ge(mask_made, 2)
            for rep in range(2):
                m = mask[:, rep * P:(rep + 1) * P].rearrange("p (j i) -> p j i", i=HD1)
                nc.gpsimd.affine_select(out=m, in_=m, compare_op=ALU.is_gt, fill=KV_SCALE, base=0,
                                        pattern=[[HD1, QUAD], [0, HD1]], channel_multiplier=-1).then_inc(mask_made, 1)
            pool.wait_ge(mask_made, 4)
            for rep in range(2):
                m = mask[:, rep * P:(rep + 1) * P].rearrange("p (j i) -> p j i", i=HD1)
                nc.gpsimd.affine_select(out=m, in_=m, compare_op=ALU.is_gt, fill=0.0, base=HD1,
                                        pattern=[[HD1, QUAD], [0, HD1]], channel_multiplier=-1).then_inc(mask_made, 1)

            def gather(c, t):
                n = c * 4 + t
                if n >= 2:
                    pool.wait_ge(combined, n - 1)
                for e in range(2):
                    nc.gpsimd.indirect_dma_start(y_in[:, t % 2, e, :], None, y_rows,
                                                 bass.IndirectOffsetOnAxis(ap=k.slots[:, e, n:n + 1], axis=0)
                                                 ).then_inc(y_loaded[t % 2], 16)

            for t in range(4):
                gather(0, t)
            for c in range(NCH):
                for t in range(4):
                    pool.wait_ge(feat_hi, c * 8 + t + 1)
                    nc.gpsimd.tensor_tensor(k_lo[:, t, :], feat[:, t % 2, :], k_hi[:, t, :], ALU.subtract).then_inc(feat_lo, 1)
                    if c < NCH - 1:
                        gather(c + 1, t)
                for m in range(KD):
                    pool.wait_ge(feat_hi, c * 8 + m + 5)
                    nc.gpsimd.tensor_tensor(q_lo[:, m, :], feat[:, m % 2, :], q_hi[:, m, :], ALU.subtract).then_inc(feat_lo, 1)
                for b in range(2):
                    for m in range(KD):
                        n = b * KD + m
                        pool.wait_ge(a_hi_done, c * 8 + n + 1)
                        nc.gpsimd.tensor_tensor(a_lo[:, m, b * N:(b + 1) * N], mixed[:, n % 2, :], a_hi[:, m, b * N:(b + 1) * N],
                                                ALU.subtract).then_inc(a_lo_done, 1)

        @block.scalar
        def _(act):
            def split_turned(n, dst, t):
                act.wait_ge(turned, n + 1)
                nc.scalar.activation(dst[0][:, :, t * P:(t + 1) * P], tr[:, n % 2], ACT.Copy).then_inc(t_hi, 1)

            ln.root(nc, act, 0)
            for t in range(4):
                split_turned(t, ct, t)
            for n in range(NP):
                act.wait_ge(w_loaded[n % 2], (n // 2 + 1) * 16)
                _, dst, b = pieces[n]
                nc.scalar.activation(dst[0][:, b:b + 2, :], staged(n), ACT.Copy).then_inc(w_hi, 1)
            for t in range(4):
                split_turned(4 + t, xt, t)
            for c in range(NCH):
                for t in range(4):
                    n = c * 12 + t
                    act.wait_ge(pair_done, n + 1)
                    if c:
                        act.wait_ge(sm_done, (c - 1) * 12 + 4)
                    nc.scalar.activation(v_hi[:, t, :, 0:P], pair[:, n % 2, 1, :].rearrange("p (m i) -> p m i", i=P), ACT.Copy
                                         ).then_inc(v_hi_done, 1)
                    act.wait_ge(low_done, c * 8 + t + 1)
                    nc.scalar.activation(low_exp[:, t % 2, :], low[:, t % 2, :], ACT.Exp).then_inc(low_exp_done, 1)
                    act.wait_ge(feat_done, c * 8 + t + 1)
                    nc.scalar.activation(k_hi[:, t, :], feat[:, t % 2, :], ACT.Copy).then_inc(feat_hi, 1)
                for m in range(KD):
                    n = c * 12 + 4 + m
                    act.wait_ge(pair_done, n + 1)
                    if c:
                        act.wait_ge(mixed_done, c * 8)
                    nc.scalar.activation(gate[:, m, :], pair[:, n % 2, 1, :], ACT.Exp, bias=bg[:, m:m + 1], scale=-1.0).then_inc(gate_exp, 1)
                    act.wait_ge(low_done, c * 8 + m + 5)
                    nc.scalar.activation(low_exp[:, m % 2, :], low[:, m % 2, :], ACT.Exp).then_inc(low_exp_done, 1)
                    act.wait_ge(feat_done, c * 8 + m + 5)
                    nc.scalar.activation(q_hi[:, m, :], feat[:, m % 2, :], ACT.Copy).then_inc(feat_hi, 1)
                for b in range(2):
                    act.wait_ge(kv_done, c * 4 + b * 2 + 2)
                    nc.scalar.activation(kv_hi[:, b], kv[:, b], ACT.Copy).then_inc(kv_hi_done, 1)
                if c < NCH - 1:
                    for t in range(4):
                        split_turned(8 * (c + 1) + t, ct, t)
                for b in range(2):
                    for m in range(KD):
                        n = b * KD + m
                        act.wait_ge(mixed_done, c * 8 + n + 1)
                        nc.scalar.activation(a_hi[:, m, b * N:(b + 1) * N], mixed[:, n % 2, :], ACT.Copy).then_inc(a_hi_done, 1)
                if c < NCH - 1:
                    ln.root(nc, act, c + 1)
                    for t in range(4):
                        split_turned(8 * (c + 1) + 4 + t, xt, t)

        @block.vector
        def _(dve):
            V = nc.vector

            def combine(c, t):
                u, n = c % 2, c * 4 + t
                dve.wait_ge(x_loaded[u], (c // 2 + 1) * 16)
                dve.wait_ge(y_loaded[t % 2], (n // 2 + 1) * 32)
                V.scalar_tensor_tensor(x2[:, u, t, :], y_in[:, t % 2, 0, :], k.mix[:, 0, n:n + 1], x2[:, u, t, :],
                                       ALU.mult, ALU.add).then_inc(first_added, 1)
                dve.wait_ge(first_added, n + 1)
                V.scalar_tensor_tensor(x2[:, u, t, :], y_in[:, t % 2, 1, :], k.mix[:, 1, n:n + 1], x2[:, u, t, :],
                                       ALU.mult, ALU.add).then_inc(combined, 1)
                dve.wait_ge(combined, n + 1)
                ln.tile(nc, x2[:, u], t)

            def normalise(c):
                ln.finish(nc, dve, c)
                if c:
                    dve.wait_ge(turned, 8 * c)
                for t in range(4):
                    V.tensor_scalar(xn[:, t, :], x2[:, c % 2, t, :], ln.mean[:, t:t + 1], ln.rstd[:, t:t + 1],
                                    ALU.subtract, ALU.mult).then_inc(normed, 1)

            def rest_of_turned(n, dst, t):
                dve.wait_ge(t_hi, n + 1)
                V.tensor_tensor(dst[1][:, :, t * P:(t + 1) * P], tr[:, n % 2], dst[0][:, :, t * P:(t + 1) * P], ALU.subtract).then_inc(t_lo, 1)

            def feature(c, n, f, buf):
                z = pair[:, n % 2, 0, :]
                dve.wait_ge(pair_done, n + 1)
                if f >= 2:
                    dve.wait_ge(low_exp_done, f - 1)
                V.tensor_scalar(low[:, buf, :], z, 0.0, None, ALU.min).then_inc(low_done, 1)
                dve.wait_ge(low_exp_done, f + 1)
                if f >= 2:
                    dve.wait_ge(feat_lo, f - 1)
                V.scalar_tensor_tensor(feat[:, buf, :], z, 0.0, low_exp[:, buf, :], ALU.max, ALU.add).then_inc(feat_done, 1)

            dve.wait_ge(small_loaded, 16)
            V.tensor_scalar(bg[:, :], bg[:, :], -1.0, None, ALU.mult).then_inc(bg_negated, 1)
            for t in range(4):
                combine(0, t)
            normalise(0)
            for t in range(4):
                rest_of_turned(t, ct, t)
            for n in range(NP):
                dve.wait_ge(w_hi, n + 1)
                _, dst, b = pieces[n]
                V.tensor_tensor(dst[1][:, b:b + 2, :], staged(n), dst[0][:, b:b + 2, :], ALU.subtract).then_inc(w_lo, 1)
            for t in range(4):
                rest_of_turned(4 + t, xt, t)
            for c in range(NCH):
                for t in range(4):
                    n = c * 12 + t
                    feature(c, n, c * 8 + t, t % 2)
                    dve.wait_ge(v_hi_done, c * 4 + t + 1)
                    V.tensor_tensor(v_lo[:, t], pair[:, n % 2, 1, :].rearrange("p (m i) -> p m i", i=P), v_hi[:, t, :, 0:P],
                                    ALU.subtract).then_inc(pair_read, 1)
                    if c < NCH - 1:
                        combine(c + 1, t)
                for m in range(KD):
                    n = c * 12 + 4 + m
                    feature(c, n, c * 8 + 4 + m, m % 2)
                    dve.wait_ge(gate_exp, c * 4 + m + 1)
                    V.tensor_scalar(gate[:, m, :], gate[:, m, :], 1.0, None, ALU.add).then_inc(pair_read, 1)
                for b in range(2):
                    for half in range(2):
                        s = c * 12 + b * 2 + half
                        dve.wait_ge(sm_done, s + 1)
                        V.tensor_tensor(kv[:, b, 2 * half:2 * half + 2].rearrange("p m s i -> p m (s i)"), sm[:, s % 2],
                                        mask[:, :].unsqueeze(1).to_broadcast([P, 2, 2 * P]), ALU.mult).then_inc(kv_done, 1)
                    dve.wait_ge(kv_hi_done, c * 2 + b + 1)
                    V.tensor_tensor(kv_lo[:, b], kv[:, b], kv_hi[:, b], ALU.subtract).then_inc(kv_lo_done, 1)
                if c < NCH - 1:
                    for t in range(4):
                        rest_of_turned(8 * (c + 1) + t, ct, t)
                for b in range(2):
                    for m in range(KD):
                        n = c * 8 + b * KD + m
                        s = c * 12 + 4 + b * KD + m
                        tok = slice(b * N, (b + 1) * N)
                        dve.wait_ge(sm_done, s + 1)
                        if n >= 2:
                            dve.wait_ge(mixed_done, n - 1)
                        V.scalar_tensor_tensor(denom[:, n % 2, :], sm[:, s % 2, 1, :], XATTN_EPS * KV_SCALE, gate[:, m, tok],
                                               ALU.add, ALU.mult).then_inc(denom_done, 1)
                        dve.wait_ge(denom_done, n + 1)
                        V.reciprocal(denom[:, n % 2, :], denom[:, n % 2, :]).then_inc(recip_done, 1)
                        dve.wait_ge(recip_done, n + 1)
                        if n >= 2:
                            dve.wait_ge(a_lo_done, n - 1)
                        V.tensor_tensor(mixed[:, n % 2, :], sm[:, s % 2, 0, :], denom[:, n % 2, :], ALU.mult).then_inc(mixed_done, 1)
                if c < NCH - 1:
                    normalise(c + 1)
                    for t in range(4):
                        rest_of_turned(8 * (c + 1) + 4 + t, xt, t)
                for t in range(4):
                    n = c * 12 + 8 + t
                    dve.wait_ge(pair_done, n + 1)
                    V.scalar_tensor_tensor(x2[:, c % 2, t, :], pair[:, n % 2, 0, :], k.tanh_gates[:, 1:2], x2[:, c % 2, t, :],
                                           ALU.mult, ALU.add).then_inc(pair_read, 1)

        def bank_read(s):
            c, r = divmod(s, 12)
            return (kv_done, c * 4 + r + 1) if r < 4 else (mixed_done, c * 8 + r - 4 + 1)

        @block.tensor
        def _(pe):
            mm = nc.tensor.matmul

            def three(out, a, b, first, last):
                mm(out, a[0], b[0], start=first, stop=False)
                mm(out, a[0], b[1], start=False, stop=False)
                return mm(out, a[1], b[0], start=False, stop=last)

            def turn(n, src, t):
                if n >= 2:
                    pe.wait_ge(t_lo, n - 1)
                for b in range(KD):
                    last = nc.tensor.transpose(tr[:, n % 2, b, :], src[:, t, b * P:(b + 1) * P], k.ident[:, :])
                last.then_inc(turned, 1)

            def turn_ctx(c):
                pe.wait_ge(ctx_loaded, (c + 1) * 16)
                for t in range(4):
                    turn(8 * c + t, ctx_in, t)

            def turn_x(c):
                for t in range(4):
                    pe.wait_ge(normed, c * 4 + t + 1)
                    turn(8 * c + 4 + t, xn, t)

            turn_ctx(0)
            turn_x(0)
            pe.wait_ge(w_lo, NP)
            for c in range(NCH):
                pe.wait_ge(t_lo, 8 * c + 4)
                for t in range(4):
                    n = c * 12 + t
                    if n >= 2:
                        pe.wait_ge(pair_read, n - 1)
                    tok = slice(t * P, (t + 1) * P)
                    for o in range(2):
                        for b in range(KD):
                            last = three(pair[:, n % 2, o, :], [a[:, b, tok] for a in ct],
                                         [a[:, b, o * D:(o + 1) * D] for a in wkv], b == 0, b == KD - 1)
                    last.then_inc(pair_done, 1)
                pe.wait_ge(t_lo, 8 * c + 8)
                for m in range(KD):
                    n = c * 12 + 4 + m
                    pe.wait_ge(pair_read, n - 1)
                    cols = slice(m * P, (m + 1) * P)
                    for o, wt in enumerate((wq, wg)):
                        for b in range(KD):
                            last = three(pair[:, n % 2, o, :], [a[:, b, cols] for a in wt], [a[:, b, :] for a in xt], b == 0, b == KD - 1)
                    last.then_inc(pair_done, 1)
                pe.wait_ge(feat_lo, c * 8 + 4)
                pe.wait_ge(pair_read, c * 12 + 4)
                pe.wait_ge(mask_made, 1)
                for b in range(2):
                    for half in range(2):
                        s = c * 12 + b * 2 + half
                        if s >= 2:
                            pe.wait_ge(*bank_read(s - 2))
                        for q in range(2):
                            m = half * 2 + q
                            for t in (2 * b, 2 * b + 1):
                                kh, kl = (a[:, t, m * P:(m + 1) * P] for a in (k_hi, k_lo))
                                mm(sm[:, s % 2, q, :], kh, v_hi[:, t, m, :], start=(t == 2 * b), stop=False)
                                mm(sm[:, s % 2, q, 0:P], kh, v_lo[:, t, m, :], start=False, stop=False)
                                last = mm(sm[:, s % 2, q, :], kl, v_hi[:, t, m, :], start=False, stop=(t == 2 * b + 1))
                        last.then_inc(sm_done, 1)
                if c < NCH - 1:
                    turn_ctx(c + 1)
                pe.wait_ge(feat_lo, c * 8 + 8)
                for b in range(2):
                    pe.wait_ge(kv_lo_done, c * 2 + b + 1)
                    for m in range(KD):
                        s = c * 12 + 4 + b * KD + m
                        pe.wait_ge(*bank_read(s - 2))
                        qs = [a[:, m, b * N:(b + 1) * N] for a in (q_hi, q_lo)]
                        for o in range(2):
                            last = three(sm[:, s % 2, o, :], [a[:, b, m, o, :] for a in (kv_hi, kv_lo)], qs, True, True)
                        last.then_inc(sm_done, 1)
                if c < NCH - 1:
                    turn_x(c + 1)
                for t in range(4):
                    n = c * 12 + 8 + t
                    pe.wait_ge(pair_read, n - 1)
                    pe.wait_ge(a_lo_done, c * 8 + (t // 2 + 1) * 4)
                    for m in range(KD):
                        last = three(pair[:, n % 2, 0, :], [a[:, m, t * P:(t + 1) * P] for a in (a_hi, a_lo)],
                                     [a[:, m, :] for a in wo], m == 0, m == KD - 1)
                    last.then_inc(pair_done, 1)


EXPERTS2, SLOTS2, HID2 = 16, 128, 128
ES = EXPERTS2 * SLOTS2
NJ = ES // D
JE = D // SLOTS2
L2_EPS = 1e-12


def soft_weights_phase(nc, k, w, mu, w1, w2):
    with phase(nc) as st:
        sb, ps, sem = opener(nc, st)
        raw = sb("mu_raw", [P, KD, ES])
        square = sb("mu_square", [P, 2, ES])
        ones = sb("mu_ones", [P, P])
        norm = sb("mu_norm", [P, ES])
        stage = sb("w_stage", [P, 2, 2 * D])
        total = ps("mu_total", [P, NJ, D])
        loaded = sem("mu_loaded")
        ones_made, squared, summed = sem("mu_ones_made"), sem("mu_squared"), sem("mu_summed")
        rooted, floored, inverted, scaled, mu_hi = (sem(f"mu_{n}") for n in ("rooted", "floored", "inverted", "scaled", "hi"))
        w_loaded = [sem(f"w12_loaded{u}") for u in range(2)]
        w_hi, w_lo = sem("w12_hi"), sem("w12_lo")
        block = st.enter_context(nc.Block())
        w1_d, w2_d = w1.rearrange("e (k p) h -> p k e h", p=P), w2.rearrange("e h d -> h e d")
        pieces = []
        for c in range(KD):
            for e in range(0, EXPERTS2, 8):
                pieces.append((w.w1, (slice(None), c, slice(e, e + 8), slice(None)), w1_d[:, c, e:e + 8, :]))
        for e in range(0, EXPERTS2, 2):
            pieces.append((w.w2, (slice(None), slice(e, e + 2), slice(None)), w2_d[:, e:e + 2, :]))
        NP = len(pieces)

        def staged(n):
            a, b = pieces[n][2].shape[1:]
            return stage[:, n % 2, :].rearrange("p (a b) -> p a b", a=a, b=b)

        @block.sync
        def _(sp):
            for c in range(KD):
                sp.dma_start(raw[:, c, :], mu[c * P:(c + 1) * P, :]).then_inc(loaded, 16)
            for n in range(NP):
                if n >= 2:
                    sp.wait_ge(w_lo, n - 1)
                sp.dma_start(staged(n), pieces[n][2]).then_inc(w_loaded[n % 2], 16)
            sp.wait_ge(w_lo, NP)

        @block.gpsimd
        def _(pool):
            nc.gpsimd.memset(ones[:, :], 1.0).then_inc(ones_made, 1)
            for n in range(NP):
                pool.wait_ge(w_hi, n + 1)
                hi, lo = (a[pieces[n][1]] for a in pieces[n][0])
                nc.gpsimd.tensor_tensor(lo, staged(n), hi, ALU.subtract).then_inc(w_lo, 1)

        @block.tensor
        def _(pe):
            pe.wait_ge(ones_made, 1)
            for c in range(KD):
                pe.wait_ge(squared, c + 1)
                for j in range(NJ):
                    last = nc.tensor.matmul(total[:, j, :], ones[:, :], square[:, c % 2, j * D:(j + 1) * D], start=(c == 0), stop=(c == KD - 1))
                last.then_inc(summed, 1)

        @block.scalar
        def _(act):
            def split(n):
                act.wait_ge(w_loaded[n % 2], (n // 2 + 1) * 16)
                nc.scalar.activation(pieces[n][0][0][pieces[n][1]], staged(n), ACT.Copy).then_inc(w_hi, 1)

            act.wait_ge(loaded, 16 * KD)
            for c in range(KD):
                if c >= 2:
                    act.wait_ge(summed, c - 1)
                nc.scalar.activation(square[:, c % 2, :], raw[:, c, :], ACT.Square).then_inc(squared, 1)
            for n in range(6):
                split(n)
            act.wait_ge(summed, KD)
            nc.scalar.activation(norm[:, :], total[:, :, :].rearrange("p j d -> p (j d)"), ACT.Sqrt).then_inc(rooted, 1)
            for n in range(6, NP):
                split(n)
            for c in range(KD):
                act.wait_ge(scaled, c + 1)
                nc.scalar.activation(w.mu[0][:, c, :], raw[:, c, :], ACT.Copy).then_inc(mu_hi, 1)

        @block.vector
        def _(dve):
            dve.wait_ge(rooted, 1)
            nc.vector.tensor_scalar(norm[:, :], norm[:, :], L2_EPS, None, ALU.max).then_inc(floored, 1)
            dve.wait_ge(floored, 1)
            nc.vector.reciprocal(norm[:, :], norm[:, :]).then_inc(inverted, 1)
            dve.wait_ge(inverted, 1)
            for c in range(KD):
                nc.vector.tensor_tensor(raw[:, c, :], raw[:, c, :], norm[:, :], ALU.mult).then_inc(scaled, 1)
            for c in range(KD):
                dve.wait_ge(mu_hi, c + 1)
                nc.vector.tensor_tensor(w.mu[1][:, c, :], raw[:, c, :], w.mu[0][:, c, :], ALU.subtract)


def soft_moe_phase(nc, k, w, x3, gamma, beta, scale, b1_cols, b2, out):
    with phase(nc) as st:
        sb, ps, sem = opener(nc, st)
        ln1, ln2 = LayerNorm(sb, sem, "s1", 2), LayerNorm(sb, sem, "s2", 2)
        gam, bet = sb("s_gamma", [P, D]), sb("s_beta", [P, D])
        scl, b1 = sb("s_scale", [P, 1]), sb("s_b1", [P, EXPERTS2])
        b2s = sb("s_b2", [EXPERTS2, D])
        x_in, x_ln, x_res = sb("s_x", [P, 2, D]), sb("s_xln", [P, 2, D]), sb("s_res", [P, 2, D])
        waste = sb("s_waste", [P, 2, D], F16)
        squares, l2, rs = sb("s_squares", [P, 2]), sb("s_l2", [P, 2]), sb("s_rs", [P, 2])
        xl = tuple(sb(f"s_xl_{q}", [P, 2, D], F16) for q in ("hi", "lo"))
        xt = tuple(sb(f"s_xt_{q}", [P, KD, N], F16) for q in ("hi", "lo"))
        lg = sb("s_lg", [P, 2, ES])
        top, low = sb("s_top", [P, 2, NJ]), sb("s_low", [P, 2])
        slot_top, slot_low = sb("s_slot_top", [P, 2, 2]), sb("s_slot_low", [P, 2, 2])
        slot_sum, slot_inv = sb("s_slot_sum", [P, 2, 2]), sb("s_slot_inv", [P, 2, 2])
        dt = sb("s_dt", [P, 2, 2, N])
        ed = tuple(sb(f"s_ed_{q}", [P, 2, ES], F16) for q in ("hi", "lo"))
        et = tuple(sb(f"s_et_{q}", [P, EXPERTS2, N], F16) for q in ("hi", "lo"))
        part = sb("s_part", [P, 2, EXPERTS2])
        part_t = sb("s_part_t", [EXPERTS2, 2, P])
        rn = sb("s_rn", [P, 2])
        si = tuple(sb(f"s_si_{q}", [P, 2, KD, D], F16) for q in ("hi", "lo"))
        h32 = sb("s_h32", [P, 2, D])
        hp = tuple(sb(f"s_h_{q}", [P, 2, D], F16) for q in ("hi", "lo"))
        so = tuple(sb(f"s_so_{q}", [P, 2, D], F16) for q in ("hi", "lo"))
        ring = ps("s_ring", [P, 4, D])
        acc = ps("s_acc", [P, 2, D])
        x_bank = ps("s_x_bank", [P, 2, D])

        names = ("small", "x_loaded", "res_loaded", "x1_done", "x_affine", "xln_done", "squared",
                 "l2_done", "l2_floored", "l2_inverted", "rs_done", "xn_done", "xl_hi", "xl_lo", "turned", "xt_hi", "xt_lo",
                 "logits", "lg_out", "top_done", "top_all", "low_done", "d_turned", "slot_top_done", "slot_low_done", "dt_exp",
                 "slot_divided", "slot_inverted", "dt_done", "u_turned", "ed_hi", "ed_lo", "e_done", "part_done",
                 "zn_done", "zn_inv", "rn_done", "part_turned", "part_out", "et_turned", "et_hi", "et_lo",
                 "s_done", "si_hi", "si_lo", "h_done", "h_act", "h_hi", "h_lo", "o_done", "o_hi", "o_lo",
                 "c_done", "out_done", "stored")
        S = {n: sem(f"s_{n}") for n in names}
        block = st.enter_context(nc.Block())
        x_d, out_d = (a.rearrange("(c p) d -> p c d", p=P) for a in (x3, out))

        def ops(op, first, end, nxt=0):
            return [(nxt, op, n) for n in range(first, end)]

        def contract(j):
            return [o for e in range(JE * j, JE * j + JE) for o in [(0, "O", e)] + ([(0, "C", e - 1)] if e else [])]

        def mixed(a, b):
            at = [((i + 0.5) / len(a), 0, o) for i, o in enumerate(a)] + [((i + 0.5) / len(b), 1, o) for i, o in enumerate(b)]
            return [o for _, _, o in sorted(at, key=lambda v: v[:2])]

        TURNS = ES * 2 // (4 * P)
        dispatch = []
        for n in range(TURNS + 2):
            if n >= 2:
                dispatch += [(1, "U", n - 2)]
            if n < TURNS:
                dispatch += [(1, "D", n)]
            if 1 <= n <= TURNS:
                dispatch += [(1, "W", n - 1)]
        norms = ops("N1", 0, 1, 1) + ops("N2", 0, 1, 1)
        middle = ops("N3", 0, 1, 1) + ops("X", 0, 2, 1) + ops("XL", 0, 1, 1)
        logits = ops("L", 0, 2 * NJ, 1)
        exps = ops("E", 0, 2 * NJ, 1)
        tail = 6
        body = (ops("T", 0, TURNS) + ops("S", 0, KD) + ops("B", 0, 1) + ops("S", KD, 2 * KD) + norms[:1] + ops("H", 0, 1)
                + ops("S", 2 * KD, 3 * KD) + norms[1:] + contract(0) + ops("H", 1, 2) + ops("S", 3 * KD, 4 * KD) + middle
                + mixed(contract(1), logits) + ops("H", 2, 3)
                + mixed(contract(2), dispatch[:len(dispatch) // 2]) + ops("H", 3, 4)
                + mixed(contract(3), dispatch[len(dispatch) // 2:-tail]) + mixed(ops("C", EXPERTS2 - 1, EXPERTS2), dispatch[-tail:])
                + ops("OUT", 0, 1) + exps)
        before = norms + middle + logits + dispatch + exps
        last = [op for op in body if not op[0]]

        READ = {"L": ("lg_out", 2 * NJ), "D": ("dt_exp", TURNS), "U": ("ed_lo", TURNS), "T": ("et_lo", TURNS),
                "S": ("si_lo", NJ * KD), "H": ("h_act", NJ), "O": ("o_lo", EXPERTS2)}
        RING = 4

        def placed(ops_, uses):
            uses, result = list(uses), []
            for nxt, op, n in ops_:
                bank = prev = None
                if op in READ:
                    bank = len(uses) % RING
                    prev = uses[-RING] if len(uses) >= RING else None
                    uses.append((nxt, op, n))
                result.append((nxt, op, n, bank, prev))
            return result, [(nxt - 1, op, n) for nxt, op, n in uses[-RING:]]

        start, carry = placed(before, [])
        loop_ops, loop_carry = placed(body, carry)
        last_ops, _ = placed(last, carry)
        assert loop_carry == carry and sum(o[3] is not None for o in start) % RING == 0
        assert sum(o[3] is not None for o in loop_ops) % RING == 0

        def run(eng, step):
            def go(b, ops_):
                for nxt, op, n, bank, prev in ops_:
                    step(b + nxt, op, n, bank, prev and (b + prev[0], prev[1], prev[2]))
            go(-1, start)
            go(0, loop_ops)
            with eng.Fori(1, B - 1) as b:
                go(b, loop_ops)
            go(B - 1, last_ops)

        def count(b, per_batch, n):
            return b * per_batch + (n + 1)

        def reusable(b, per_batch, n):
            return b * per_batch + max(n - 1, 0)

        def later(b):
            return not (isinstance(b, int) and b == 0)

        @block.sync
        def _(sp):
            for dst, src in ((gam, gamma), (bet, beta), (scl, scale)):
                sp.dma_start(dst[:, :], src.partition_broadcast(P)).then_inc(S["small"], 16)
            sp.dma_start(b1[:, :], b1_cols).then_inc(S["small"], 16)
            sp.dma_start(b2s[:, :], b2).then_inc(S["small"], 16)
            sp.dma_start(x_in[:, :, :], x_d[:, 0:2, :]).then_inc(S["x_loaded"], 16)

            def batch(b, is_last):
                if later(b):
                    sp.wait_ge(S["stored"], b * 16)
                sp.dma_start(x_res[:, :, :], x_d[:, bass.ds(b * 2, 2), :]).then_inc(S["res_loaded"], 16)
                if not is_last:
                    sp.wait_ge(S["turned"], b * 2 + 2)
                    sp.dma_start(x_in[:, :, :], x_d[:, bass.ds(b * 2 + 2, 2), :]).then_inc(S["x_loaded"], 16)
                sp.wait_ge(S["out_done"], b * 2 + 2)
                sp.dma_start(out_d[:, bass.ds(b * 2, 2), :], x_res[:, :, :]).then_inc(S["stored"], 16)

            batch(0, False)
            with sp.Fori(1, B - 1) as b:
                batch(b, False)
            batch(B - 1, True)
            sp.wait_ge(S["stored"], B * 16)

        @block.gpsimd
        def _(pool):
            def step(b, op, n, bank, prev):
                if op == "H":
                    pool.wait_ge(S["h_hi"], count(b, NJ, n))
                    nc.gpsimd.tensor_tensor(hp[1][:, n % 2, :], h32[:, n % 2, :], hp[0][:, n % 2, :], ALU.subtract).then_inc(S["h_lo"], 1)
            run(pool, step)

        @block.scalar
        def _(act):
            A = nc.scalar.activation

            def step(b, op, n, bank, prev):
                if op == "N1":
                    ln1.root(nc, act, b)
                if op == "N2":
                    ln2.root(nc, act, b)
                    if later(b):
                        act.wait_ge(S["l2_done"], b)
                    for t in range(2):
                        act.wait_ge(S["xln_done"], count(b, 2, t))
                        A(waste[:, t, :], x_ln[:, t, :], ACT.Square, accum_out=squares[:, t:t + 1]).then_inc(S["squared"], 1)
                if op == "N3":
                    act.wait_ge(S["squared"], count(b, 2, 1))
                    if later(b):
                        act.wait_ge(S["l2_inverted"], b)
                    A(l2[:, :], squares[:, :], ACT.Sqrt).then_inc(S["l2_done"], 1)
                if op == "XL":
                    if later(b):
                        act.wait_ge(S["s_done"], b * (NJ * KD))
                    A(xl[0][:, :, :], x_ln[:, :, :], ACT.Copy).then_inc(S["xl_hi"], 1)
                if op == "X":
                    act.wait_ge(S["turned"], count(b, 2, n))
                    if later(b):
                        act.wait_ge(S["logits"], b * (2 * NJ))
                    A(xt[0][:, :, n * P:(n + 1) * P], x_bank[:, n, :].rearrange("p (k i) -> p k i", i=P), ACT.Copy).then_inc(S["xt_hi"], 1)
                if op == "L":
                    t, j = divmod(n, NJ)
                    act.wait_ge(S["logits"], count(b, 2 * NJ, n))
                    if later(b):
                        act.wait_ge(S["et_turned"], b * TURNS)
                        act.wait_ge(S["part_done"], b * (2 * NJ))
                    A(lg[:, t, j * D:(j + 1) * D], ring[:, bank, :], ACT.Copy).then_inc(S["lg_out"], 1)
                if op == "D":
                    act.wait_ge(S["slot_low_done"], count(b, TURNS, n))
                    if later(b) or n >= 2:
                        act.wait_ge(S["u_turned"], reusable(b, TURNS, n))
                    for e in range(2):
                        last_ = A(dt[:, n % 2, e, :], ring[:, bank, e * N:(e + 1) * N], ACT.Exp, bias=slot_low[:, n % 2, e:e + 1],
                                  accum_out=slot_sum[:, n % 2, e:e + 1])
                    last_.then_inc(S["dt_exp"], 1)
                if op == "U":
                    act.wait_ge(S["u_turned"], count(b, TURNS, n))
                    if later(b):
                        act.wait_ge(S["s_done"], b * (NJ * KD))
                    A(ed[0][:, :, 2 * n * P:(2 * n + 2) * P], ring[:, bank, :].rearrange("p (t s) -> p t s", t=2), ACT.Copy
                      ).then_inc(S["ed_hi"], 1)
                if op == "E":
                    t, j = divmod(n, NJ)
                    act.wait_ge(S["low_done"], count(b, 2, t))
                    act.wait_ge(S["d_turned"], count(b, TURNS, 2 * j + 1))
                    A(lg[:, t, j * D:(j + 1) * D], lg[:, t, j * D:(j + 1) * D], ACT.Exp, bias=low[:, t:t + 1]).then_inc(S["e_done"], 1)
                if op == "T":
                    act.wait_ge(S["et_turned"], count(b, TURNS, n))
                    if later(b):
                        act.wait_ge(S["c_done"], b * EXPERTS2)
                    A(et[0][:, 2 * n:2 * n + 2, :], ring[:, bank, :].rearrange("p (e i) -> p e i", e=2), ACT.Copy).then_inc(S["et_hi"], 1)
                if op == "S":
                    j, m = divmod(n, KD)
                    act.wait_ge(S["s_done"], count(b, NJ * KD, n))
                    if later(b) or j >= 2:
                        act.wait_ge(S["h_done"], reusable(b, NJ, j))
                    A(si[0][:, j % 2, m, :], ring[:, bank, :], ACT.Copy, scale=1.0 / N).then_inc(S["si_hi"], 1)
                if op == "H":
                    act.wait_ge(S["h_done"], count(b, NJ, n))
                    if later(b) or n >= 2:
                        act.wait_ge(S["h_lo"], reusable(b, NJ, n))
                    for e in range(JE):
                        last_ = A(h32[:, n % 2, e * SLOTS2:(e + 1) * SLOTS2], ring[:, bank, e * SLOTS2:(e + 1) * SLOTS2], ACT.Gelu,
                                  bias=b1[:, n * JE + e:n * JE + e + 1])
                    last_.then_inc(S["h_act"], 1)
                if op == "O":
                    act.wait_ge(S["o_done"], count(b, EXPERTS2, n))
                    if later(b) or n >= 2:
                        act.wait_ge(S["c_done"], reusable(b, EXPERTS2, n))
                    A(so[0][:, n % 2, :], ring[:, bank, :], ACT.Copy).then_inc(S["o_hi"], 1)
            act.wait_ge(S["small"], 16 * 5)
            run(act, step)

        @block.vector
        def _(dve):
            V = nc.vector

            def step(b, op, n, bank, prev):
                if op == "N1":
                    dve.wait_ge(S["x_loaded"], b * 16 + 16)
                    ln1.statistics(nc, dve, x_in, b)
                    if later(b):
                        dve.wait_ge(S["xl_lo"], b)
                        dve.wait_ge(S["xn_done"], b * 2)
                    for t in range(2):
                        V.tensor_scalar(x_ln[:, t, :], x_in[:, t, :], ln1.mean[:, t:t + 1], ln1.rstd[:, t:t + 1], ALU.subtract,
                                        ALU.mult).then_inc(S["x1_done"], 1)
                if op == "N2":
                    dve.wait_ge(S["x1_done"], b * 2 + 2)
                    ln2.statistics(nc, dve, x_ln, b)
                    for t in range(2):
                        V.tensor_scalar(x_ln[:, t, :], x_ln[:, t, :], ln2.mean[:, t:t + 1], ln2.rstd[:, t:t + 1], ALU.subtract,
                                        ALU.mult).then_inc(S["x_affine"], 1)
                    dve.wait_ge(S["x_affine"], b * 4 + 2)
                    for t in range(2):
                        V.tensor_tensor(x_ln[:, t, :], x_ln[:, t, :], gam[:, :], ALU.mult).then_inc(S["x_affine"], 1)
                    dve.wait_ge(S["x_affine"], b * 4 + 4)
                    for t in range(2):
                        V.tensor_tensor(x_ln[:, t, :], x_ln[:, t, :], bet[:, :], ALU.add).then_inc(S["xln_done"], 1)
                if op == "N3":
                    dve.wait_ge(S["l2_done"], b + 1)
                    V.tensor_scalar(l2[:, :], l2[:, :], L2_EPS, None, ALU.max).then_inc(S["l2_floored"], 1)
                    dve.wait_ge(S["l2_floored"], b + 1)
                    V.reciprocal(rs[:, :], l2[:, :]).then_inc(S["l2_inverted"], 1)
                    dve.wait_ge(S["l2_inverted"], b + 1)
                    V.tensor_scalar(rs[:, :], rs[:, :], scl[:, 0:1], None, ALU.mult).then_inc(S["rs_done"], 1)
                    dve.wait_ge(S["rs_done"], b + 1)
                    dve.wait_ge(S["xln_done"], b * 2 + 2)
                    for t in range(2):
                        V.tensor_scalar(x_in[:, t, :], x_ln[:, t, :], rs[:, t:t + 1], None, ALU.mult).then_inc(S["xn_done"], 1)
                if op == "XL":
                    dve.wait_ge(S["xl_hi"], b + 1)
                    V.tensor_tensor(xl[1][:, :, :], x_ln[:, :, :], xl[0][:, :, :], ALU.subtract).then_inc(S["xl_lo"], 1)
                if op == "X":
                    dve.wait_ge(S["xt_hi"], count(b, 2, n))
                    tok = slice(n * P, (n + 1) * P)
                    V.tensor_tensor(xt[1][:, :, tok], x_bank[:, n, :].rearrange("p (k i) -> p k i", i=P), xt[0][:, :, tok], ALU.subtract
                                    ).then_inc(S["xt_lo"], 1)
                if op == "L":
                    t, j = divmod(n, NJ)
                    dve.wait_ge(S["lg_out"], count(b, 2 * NJ, n))
                    V.tensor_reduce(top[:, t, j:j + 1], lg[:, t, j * D:(j + 1) * D], AX.X, ALU.max).then_inc(S["top_done"], 1)
                    if j == NJ - 1:
                        dve.wait_ge(S["top_done"], count(b, 2 * NJ, n))
                        V.tensor_reduce(low[:, t:t + 1], top[:, t, :], AX.X, ALU.max).then_inc(S["top_all"], 1)
                        dve.wait_ge(S["top_all"], count(b, 2, t))
                        V.tensor_scalar(low[:, t:t + 1], low[:, t:t + 1], -1.0, None, ALU.mult).then_inc(S["low_done"], 1)
                if op == "D":
                    dve.wait_ge(S["d_turned"], count(b, TURNS, n))
                    V.tensor_reduce(slot_top[:, n % 2, :], ring[:, bank, :].rearrange("p (e i) -> p e i", e=2), AX.X, ALU.max
                                    ).then_inc(S["slot_top_done"], 1)
                    dve.wait_ge(S["slot_top_done"], count(b, TURNS, n))
                    V.tensor_scalar(slot_low[:, n % 2, :], slot_top[:, n % 2, :], -1.0, None, ALU.mult).then_inc(S["slot_low_done"], 1)
                if op == "W":
                    dve.wait_ge(S["dt_exp"], count(b, TURNS, n))
                    V.tensor_scalar(slot_inv[:, n % 2, :], slot_sum[:, n % 2, :], 1.0 / N, None, ALU.mult).then_inc(S["slot_divided"], 1)
                    dve.wait_ge(S["slot_divided"], count(b, TURNS, n))
                    V.reciprocal(slot_inv[:, n % 2, :], slot_inv[:, n % 2, :]).then_inc(S["slot_inverted"], 1)
                    dve.wait_ge(S["slot_inverted"], count(b, TURNS, n))
                    for e in range(2):
                        last_ = V.tensor_scalar(dt[:, n % 2, e, :], dt[:, n % 2, e, :], slot_inv[:, n % 2, e:e + 1], None, ALU.mult)
                    last_.then_inc(S["dt_done"], 1)
                if op == "U":
                    dve.wait_ge(S["ed_hi"], count(b, TURNS, n))
                    s = slice(2 * n * P, (2 * n + 2) * P)
                    V.tensor_tensor(ed[1][:, :, s], ring[:, bank, :].rearrange("p (t s) -> p t s", t=2), ed[0][:, :, s], ALU.subtract
                                    ).then_inc(S["ed_lo"], 1)
                if op == "E":
                    t, j = divmod(n, NJ)
                    dve.wait_ge(S["e_done"], count(b, 2 * NJ, n))
                    if later(b) and n == 0:
                        dve.wait_ge(S["part_turned"], b)
                    V.tensor_reduce(part[:, t, j * JE:(j + 1) * JE], lg[:, t, j * D:(j + 1) * D].rearrange("p (e i) -> p e i", i=SLOTS2),
                                    AX.X, ALU.add).then_inc(S["part_done"], 1)
                if op == "B":
                    dve.wait_ge(S["part_done"], (b + 1) * (2 * NJ))
                    if later(b):
                        dve.wait_ge(S["out_done"], b * 2)
                        dve.wait_ge(S["c_done"], b * EXPERTS2)
                    V.tensor_reduce(rn[:, :], part[:, :, :], AX.X, ALU.add).then_inc(S["zn_done"], 1)
                    dve.wait_ge(S["zn_done"], b + 1)
                    V.reciprocal(rn[:, :], rn[:, :]).then_inc(S["zn_inv"], 1)
                    dve.wait_ge(S["zn_inv"], b + 1)
                    V.tensor_scalar(rn[:, :], rn[:, :], k.tanh_gates[:, 3:4], None, ALU.mult).then_inc(S["rn_done"], 1)
                    dve.wait_ge(S["part_turned"], b + 1)
                    V.tensor_copy(part_t[:, :, :], x_bank[0:EXPERTS2, 0, 0:2 * P].rearrange("p (t i) -> p t i", i=P)).then_inc(S["part_out"], 1)
                if op == "T":
                    dve.wait_ge(S["et_hi"], count(b, TURNS, n))
                    V.tensor_tensor(et[1][:, 2 * n:2 * n + 2, :], ring[:, bank, :].rearrange("p (e i) -> p e i", e=2),
                                    et[0][:, 2 * n:2 * n + 2, :], ALU.subtract).then_inc(S["et_lo"], 1)
                if op == "S":
                    j, m = divmod(n, KD)
                    dve.wait_ge(S["si_hi"], count(b, NJ * KD, n))
                    V.scalar_tensor_tensor(si[1][:, j % 2, m, :], ring[:, bank, :], 1.0 / N, si[0][:, j % 2, m, :], ALU.mult, ALU.subtract
                                           ).then_inc(S["si_lo"], 1)
                if op == "H":
                    dve.wait_ge(S["h_act"], count(b, NJ, n))
                    if later(b) or n >= 2:
                        dve.wait_ge(S["o_done"], b * EXPERTS2 + max(n - 1, 0) * JE)
                    V.tensor_copy(hp[0][:, n % 2, :], h32[:, n % 2, :]).then_inc(S["h_hi"], 1)
                if op == "O":
                    dve.wait_ge(S["o_hi"], count(b, EXPERTS2, n))
                    V.tensor_tensor(so[1][:, n % 2, :], ring[:, bank, :], so[0][:, n % 2, :], ALU.subtract).then_inc(S["o_lo"], 1)
                if op == "OUT":
                    dve.wait_ge(S["c_done"], (b + 1) * EXPERTS2)
                    dve.wait_ge(S["res_loaded"], b * 16 + 16)
                    dve.wait_ge(S["rn_done"], b + 1)
                    for t in range(2):
                        V.scalar_tensor_tensor(x_res[:, t, :], acc[:, t, :], rn[:, t:t + 1], x_res[:, t, :], ALU.mult, ALU.add
                                               ).then_inc(S["out_done"], 1)
            dve.wait_ge(S["small"], 16 * 5)
            run(dve, step)

        @block.tensor
        def _(pe):
            mm = nc.tensor.matmul

            def three(out_, a, b_, first, last_):
                mm(out_, a[0], b_[0], start=first, stop=False)
                mm(out_, a[0], b_[1], start=False, stop=False)
                return mm(out_, a[1], b_[0], start=False, stop=last_)

            def step(b, op, n, bank, prev):
                if prev:
                    name, per = READ[prev[1]]
                    pe.wait_ge(S[name], count(prev[0], per, prev[2]))
                if op == "X":
                    pe.wait_ge(S["xn_done"], count(b, 2, n))
                    if later(b):
                        pe.wait_ge(S["part_out"], b)
                    for c in range(KD):
                        last_ = nc.tensor.transpose(x_bank[:, n, c * P:(c + 1) * P], x_in[:, n, c * P:(c + 1) * P], k.ident[:, :])
                    last_.then_inc(S["turned"], 1)
                if op == "L":
                    t, j = divmod(n, NJ)
                    pe.wait_ge(S["xt_lo"], count(b, 2, t))
                    tok = slice(t * P, (t + 1) * P)
                    for c in range(KD):
                        last_ = three(ring[:, bank, :], [a[:, c, tok] for a in xt], [a[:, c, j * D:(j + 1) * D] for a in w.mu],
                                      c == 0, c == KD - 1)
                    last_.then_inc(S["logits"], 1)
                if op == "D":
                    pe.wait_ge(S["lg_out"], count(b, 2 * NJ, NJ + n // 2))
                    for e in range(2):
                        for t in range(2):
                            at = (e * 2 + t) * P
                            last_ = nc.tensor.transpose(ring[:, bank, at:at + P], lg[:, t, (2 * n + e) * P:(2 * n + e + 1) * P], k.ident[:, :])
                    last_.then_inc(S["d_turned"], 1)
                if op == "U":
                    pe.wait_ge(S["dt_done"], count(b, TURNS, n))
                    for t in range(2):
                        for e in range(2):
                            at = (t * 2 + e) * P
                            last_ = nc.tensor.transpose(ring[:, bank, at:at + P], dt[:, n % 2, e, t * P:(t + 1) * P], k.ident[:, :])
                    last_.then_inc(S["u_turned"], 1)
                if op == "T":
                    pe.wait_ge(S["e_done"], count(b, 2 * NJ, NJ + n // 2))
                    for e in range(2):
                        for t in range(2):
                            at = (e * 2 + t) * P
                            last_ = nc.tensor.transpose(ring[:, bank, at:at + P], lg[:, t, (2 * n + e) * P:(2 * n + e + 1) * P], k.ident[:, :])
                    last_.then_inc(S["et_turned"], 1)
                if op == "B":
                    pe.wait_ge(S["part_done"], (b + 1) * (2 * NJ))
                    pe.wait_ge(S["xt_lo"], (b + 1) * 2)
                    for t in range(2):
                        last_ = nc.tensor.transpose(x_bank[0:EXPERTS2, 0, t * P:(t + 1) * P], part[:, t, :], k.ident[:, :])
                    last_.then_inc(S["part_turned"], 1)
                if op == "S":
                    j, m = divmod(n, KD)
                    pe.wait_ge(S["xl_lo"], b + 1)
                    pe.wait_ge(S["ed_lo"], count(b, TURNS, 2 * j + 1))
                    for t in range(2):
                        last_ = three(ring[:, bank, :], [a[:, t, m * P:(m + 1) * P] for a in xl],
                                      [a[:, t, j * D:(j + 1) * D] for a in ed], t == 0, t == 1)
                    last_.then_inc(S["s_done"], 1)
                if op == "H":
                    pe.wait_ge(S["si_lo"], b * (NJ * KD) + (n + 1) * KD)
                    for e in range(JE):
                        s = slice(e * SLOTS2, (e + 1) * SLOTS2)
                        for c in range(KD):
                            last_ = three(ring[:, bank, s], [a[:, c, n * JE + e, :] for a in w.w1], [a[:, n % 2, c, s] for a in si],
                                          c == 0, c == KD - 1)
                    last_.then_inc(S["h_done"], 1)
                if op == "O":
                    j, e = divmod(n, JE)
                    pe.wait_ge(S["h_lo"], count(b, NJ, j))
                    s = slice(e * SLOTS2, (e + 1) * SLOTS2)
                    three(ring[:, bank, :], [a[:, j % 2, s] for a in hp], [a[:, n, :] for a in w.w2], True, True).then_inc(S["o_done"], 1)
                if op == "C":
                    if n == 0:
                        pe.wait_ge(S["part_out"], b + 1)
                        if later(b):
                            pe.wait_ge(S["out_done"], b * 2)
                        for t in range(2):
                            mm(acc[:, t, :], part_t[:, t, :], b2s[:, :], start=True, stop=False)
                        pe.wait_ge(S["et_lo"], (b + 1) * TURNS)
                    pe.wait_ge(S["o_lo"], count(b, EXPERTS2, n))
                    for t in range(2):
                        last_ = three(acc[:, t, :], [a[:, n, t * P:(t + 1) * P] for a in et], [a[:, n % 2, :] for a in so],
                                      False, n == EXPERTS2 - 1)
                    last_.then_inc(S["c_done"], 1)
            pe.wait_ge(S["small"], 16 * 5)
            run(pe, step)



class OnChip:
    pass


def transformer(nc, a, out):
    F, X = "L0_ffn_", "L1_xattn_"

    def scratch(name, shape, dt=F32):
        return nc.dram_tensor(name, shape, dt).ap()

    x1, xn, x1s, x3 = (scratch(name, (T, D)) for name in ("after_conv", "normed_rows", "after_shared", "after_xattn"))
    expert_rows, slot_token = scratch("expert_rows", (SLOTS, D)), scratch("slot_token_rows", (SLOTS, 1), I32)
    flat = {name: a[name].rearrange("b n d -> (b n) d") for name in ("x", "ctx_2048")}
    with ExitStack() as whole:
        sb, _, _ = opener(nc, whole)
        k = OnChip()
        k.ident, k.ident16 = sb("ident", [P, P]), sb("ident16", [P, P], F16)
        k.gates, k.tanh_gates = sb("gates", [P, 4]), sb("tanh_gates", [P, 4])
        constants(nc, k, a["g_xattn"], a["g_ffn"])

        with ExitStack() as st:
            sb, _, _ = opener(nc, st)
            q_t, c_t = (sb(name, [P, KD, SSM_H, B, SSM_I]) for name in ("q_t", "c_t"))
            conv_operands(nc, k, a["x"], a["ctx_2048"], q_t, c_t)
            conv_phase(nc, k, q_t, c_t, a["ssm_reversed"], a["L0_xattn_D"], a["x"], x1.rearrange("(b n) d -> b n d", n=N))

        with ExitStack() as routed:
            sb, _, _ = opener(nc, routed)
            k.slots, k.mix = sb("slots", [P, 2, TT], I32), sb("mix", [P, 2, TT])
            with ExitStack() as st:
                sb, _, _ = opener(nc, st)
                w = OnChip()
                k.logits = sb("router_logits", [P, TT, E])
                k.tile_expert, k.slot_token = sb("tile_expert", [P, TILES], I32), sb("slot_token", [P, TILES], I32)
                w.gate_hi, w.gate_lo, w.up_hi, w.up_lo = (sb(f"w_{n}", [P, E, KD, I_MOE], F16) for n in ("gate_hi", "gate_lo", "up_hi", "up_lo"))
                shared_phase(nc, k, w, x1, xn, x1s, a["router_t"], a[F + "gate_w"], a[F + "up_w"], a[F + "s_gate_w"],
                             a["s_gate_b_cols"], a[F + "s_up_w"], a["s_up_b_cols"], a[F + "s_down_w"], a[F + "s_down_b"])
                w.down_hi, w.down_lo = (sb(f"w_down_{q}", [P, E, MK, D], F16) for q in ("hi", "lo"))
                route_phase(nc, k, w, a[F + "down_w"], slot_token)
                expert_phase(nc, k, w, xn, expert_rows)
            xattn_phase(nc, k, x1s, expert_rows, flat["ctx_2048"], a["wq_t"], a["wg_t"], a["bg_cols"], a["wkv_t"], a["wo_t"], x3)

        with ExitStack() as st:
            sb, _, _ = opener(nc, st)
            w = OnChip()
            w.mu = tuple(sb(f"w_mu_{q}", [P, KD, ES], F16) for q in ("hi", "lo"))
            w.w1 = tuple(sb(f"w_w1_{q}", [P, KD, EXPERTS2, HID2], F16) for q in ("hi", "lo"))
            w.w2 = tuple(sb(f"w_w2_{q}", [P, EXPERTS2, D], F16) for q in ("hi", "lo"))
            F = "L1_ffn_"
            soft_weights_phase(nc, k, w, a[F + "mu"], a[F + "W1"], a[F + "W2"])
            soft_moe_phase(nc, k, w, x3, a[F + "gamma"], a[F + "beta"], a[F + "scale"], a["b1_cols"], a[F + "b2"], out)


def columns(bias):
    blocks = -(-bias.shape[0] // P)
    filled = np.zeros(blocks * P, bias.dtype)
    filled[:bias.shape[0]] = bias
    return np.ascontiguousarray(filled.reshape(blocks, P).T)


def kernel(**inputs):
    import concourse.bacc as bacc
    from concourse.bass_utils import run_bass_kernel_spmd

    a = dict(inputs)
    turned = lambda m: np.ascontiguousarray(m.T)
    ssm = a.pop("L0_xattn_ssm_kernel")
    a["ssm_reversed"] = np.zeros((ssm.shape[0], D + P), ssm.dtype)
    a["ssm_reversed"][:, :D] = ssm[:, ::-1]
    a["router_t"] = turned(a.pop("L0_ffn_router_w"))
    for new, old in (("wq_t", "Wq"), ("wg_t", "Wg"), ("wkv_t", "Wkv"), ("wo_t", "Wo")):
        a[new] = turned(a.pop("L1_xattn_" + old))
    for new, old in (("s_gate_b_cols", "L0_ffn_s_gate_b"), ("s_up_b_cols", "L0_ffn_s_up_b"), ("bg_cols", "L1_xattn_bg")):
        a[new] = columns(a.pop(old))
    a["b1_cols"] = turned(a.pop("L1_ffn_b1"))
    a["L1_ffn_mu"] = a["L1_ffn_mu"].reshape(D, ES)

    nc = bacc.Bacc("TRN2", target_bir_lowering=False, num_devices=1)
    arrays, args = {}, {}
    for name, value in a.items():
        value = np.ascontiguousarray(value)
        arrays[f"in_{name}"] = value
        args[name] = nc.dram_tensor(f"in_{name}", value.shape, mybir.dt.from_np(value.dtype), kind="ExternalInput").ap()
    out = nc.dram_tensor("out", (T, D), F32, kind="ExternalOutput").ap()
    transformer(nc, args, out)
    result = run_bass_kernel_spmd(nc, [arrays], core_ids=[0])
    return result.results[0]["out"].reshape(B, N, D)
```

```python
from contextlib import ExitStack, contextmanager

import numpy as np

import concourse.bass as bass
from concourse import mybir

F32, F16, I32 = mybir.dt.float32, mybir.dt.float16, mybir.dt.int32
ACT = mybir.ActivationFunctionType
ALU = mybir.AluOpType
AX = mybir.AxisListType

P = 128
B, N, D = 8, 256, 512
T = B * N
TT = T // P
KD = D // P
CH = 4 * P
NCH = T // CH
SSM_H, SSM_I = 32, 8
PAIRS = SSM_I * (SSM_I + 1) // 2
GH = 16
GROUPS = SSM_H // GH
LN_EPS = 1e-5


@contextmanager
def phase(nc):
    with nc.cleanup_on_exit(), ExitStack() as stack:
        yield stack


def opener(nc, stack):
    def sb(name, shape, dt=F32):
        return stack.enter_context(nc.sbuf_tensor(name, shape, dt))

    def ps(name, shape, dt=F32):
        return stack.enter_context(nc.psum_tensor(name, shape, dt))

    def sem(name):
        return nc.alloc_semaphore(name)
    return sb, ps, sem


def mixed(a, b):
    at = [((i + 0.5) / len(a), 0, o) for i, o in enumerate(a)] + [((i + 0.5) / len(b), 1, o) for i, o in enumerate(b)]
    return [o for _, _, o in sorted(at, key=lambda v: v[:2])]


def pair_at(i):
    return i * SSM_I - i * (i - 1) // 2


class LayerNorm:

    def __init__(self, sb, sem, name, tiles=4):
        self.tiles = tiles
        self.stats = sb(f"{name}_stats", [P, tiles, 6])
        self.mean, self.var = sb(f"{name}_mean", [P, tiles]), sb(f"{name}_var", [P, tiles])
        self.gap, self.spread = sb(f"{name}_gap", [P, tiles]), sb(f"{name}_spread", [P, tiles])
        self.std, self.rstd = sb(f"{name}_std", [P, tiles]), sb(f"{name}_rstd", [P, tiles])
        self.stats_done, self.parts_done = sem(f"{name}_stats_done"), sem(f"{name}_parts_done")
        self.gap_squared, self.var_done = sem(f"{name}_gap_squared"), sem(f"{name}_var_done")
        self.std_done, self.rstd_done = sem(f"{name}_std_done"), sem(f"{name}_rstd_done")

    def statistics(self, nc, dve, rows, c):
        for t in range(self.tiles):
            self.tile(nc, rows, t)
        self.finish(nc, dve, c)

    def tile(self, nc, rows, t):
        nc.vector.bn_stats(self.stats[:, t, :], rows[:, t, :]).then_inc(self.stats_done, 1)

    def finish(self, nc, dve, c):
        self.variance(nc, dve, c)
        self.inverse(nc, dve, c)

    def variance(self, nc, dve, c):
        even_mean, even_m2 = self.stats[:, :, 1], self.stats[:, :, 2]
        odd_mean, odd_m2 = self.stats[:, :, 4], self.stats[:, :, 5]
        dve.wait_ge(self.stats_done, (c + 1) * self.tiles)
        nc.vector.tensor_tensor(self.mean[:, :], even_mean, odd_mean, ALU.add).then_inc(self.parts_done, 1)
        nc.vector.tensor_tensor(self.gap[:, :], even_mean, odd_mean, ALU.subtract).then_inc(self.parts_done, 1)
        nc.vector.tensor_tensor(self.spread[:, :], even_m2, odd_m2, ALU.add).then_inc(self.parts_done, 1)
        dve.wait_ge(self.parts_done, (c + 1) * 3)
        nc.vector.tensor_scalar(self.mean[:, :], self.mean[:, :], 0.5, None, ALU.mult).then_inc(self.gap_squared, 1)
        nc.vector.scalar_tensor_tensor(self.gap[:, :], self.gap[:, :], 0.25, self.gap[:, :], ALU.mult, ALU.mult
                                       ).then_inc(self.gap_squared, 1)
        nc.vector.tensor_scalar(self.spread[:, :], self.spread[:, :], 1.0 / D, LN_EPS, ALU.mult, ALU.add
                                ).then_inc(self.gap_squared, 1)
        dve.wait_ge(self.gap_squared, (c + 1) * 3)
        nc.vector.tensor_tensor(self.var[:, :], self.gap[:, :], self.spread[:, :], ALU.add).then_inc(self.var_done, 1)

    def inverse(self, nc, dve, c):
        dve.wait_ge(self.std_done, c + 1)
        nc.vector.reciprocal(self.rstd[:, :], self.std[:, :]).then_inc(self.rstd_done, 1)
        dve.wait_ge(self.rstd_done, c + 1)

    def root(self, nc, act, c):
        act.wait_ge(self.var_done, c + 1)
        nc.scalar.activation(self.std[:, :], self.var[:, :], ACT.Sqrt).then_inc(self.std_done, 1)


def constants(nc, k, g_xattn, g_ffn):
    with phase(nc) as st:
        sb, ps, sem = opener(nc, st)
        ident_zeroed, ident_ready = sem("ident_zeroed"), sem("ident_ready")
        gates_loaded, gates_ready = sem("gates_loaded"), sem("gates_ready")
        block = st.enter_context(nc.Block())

        @block.sync
        def _(sp):
            sp.dma_start(k.gates[:, 0:2], g_xattn.partition_broadcast(P)).then_inc(gates_loaded, 16)
            sp.dma_start(k.gates[:, 2:4], g_ffn.partition_broadcast(P)).then_inc(gates_loaded, 16)

        @block.gpsimd
        def _(pool):
            nc.gpsimd.memset(k.ident[:, :], 0.0).then_inc(ident_zeroed, 1)
            pool.wait_ge(ident_zeroed, 1)
            nc.gpsimd.affine_select(out=k.ident[:, :], in_=k.ident[:, :], compare_op=ALU.not_equal, fill=1.0,
                                    base=0, pattern=[[-1, P]], channel_multiplier=1).then_inc(ident_ready, 1)

        @block.scalar
        def _(act):
            act.wait_ge(gates_loaded, 32)
            nc.scalar.activation(k.tanh_gates[:, :], k.gates[:, :], ACT.Tanh).then_inc(gates_ready, 1)

        @block.vector
        def _(dve):
            dve.wait_ge(ident_ready, 1)
            nc.vector.tensor_copy(k.ident16[:, :], k.ident[:, :])


def conv_operands(nc, k, x, ctx, q_t, c_t):
    with phase(nc) as st:
        sb, ps, sem = opener(nc, st)
        x_in, c_in = sb("x_in", [P, 2, KD, D]), sb("c_in", [P, 2, KD, D])
        ln = LayerNorm(sb, sem, "x")
        tr = [ps(f"tr{n}", [P, D]) for n in range(8)]
        loaded = [sem(f"loaded{u}") for u in range(2)]
        normed = sem("normed")
        x_tr, c_tr = sem("x_tr"), sem("c_tr")
        x_out, c_out = sem("x_out"), sem("c_out")
        block = st.enter_context(nc.Block())
        x_d = x.rearrange("b (k p) d -> p (b k) d", p=P)
        c_d = ctx.rearrange("b (k p) d -> p (b k) d", p=P)

        @block.sync
        def _(sp):
            with sp.Fori(0, NCH // 2) as i:
                for u in range(2):
                    sp.wait_ge(x_out, i * 8 + 4 * (u + 1))
                    sp.dma_start(x_in[:, u], x_d[:, bass.ds(i * 8 + u * 4, 4), :]).then_inc(loaded[u], 16)
                    sp.dma_start(c_in[:, u], c_d[:, bass.ds(i * 8 + u * 4, 4), :]).then_inc(loaded[u], 16)

        @block.vector
        def _(dve):
            with dve.Fori(0, NCH // 2) as i:
                for u in range(2):
                    c = i * 2 + u
                    dve.wait_ge(loaded[u], (i + 1) * 32)
                    ln.statistics(nc, dve, x_in[:, u], c)
                    for t in range(4):
                        nc.vector.tensor_scalar(x_in[:, u, t, :], x_in[:, u, t, :], ln.mean[:, t:t + 1],
                                                ln.rstd[:, t:t + 1], ALU.subtract, ALU.mult).then_inc(normed, 1)
                    for t in range(4):
                        dve.wait_ge(x_tr, c * 4 + (t + 1))
                        dst = q_t[:, :, (t % 2) * 16:(t % 2) * 16 + 16, bass.ds(i * 4 + (2 * u + t // 2), 1), :]
                        nc.vector.tensor_copy(dst, tr[t][:, :].rearrange("p (k h o i) -> p k h o i", k=KD, o=1, i=SSM_I)
                                              ).then_inc(x_out, 1)

        @block.scalar
        def _(act):
            nc.scalar.preload_act_table(ACT.Sqrt)
            with act.Fori(0, NCH // 2) as i:
                for u in range(2):
                    c = i * 2 + u
                    ln.root(nc, act, c)
                    for t in range(4):
                        act.wait_ge(c_tr, c * 4 + (t + 1))
                        dst = c_t[:, :, (t % 2) * 16:(t % 2) * 16 + 16, bass.ds(i * 4 + (2 * u + t // 2), 1), :]
                        nc.scalar.activation(dst, tr[4 + t][:, :].rearrange("p (k h o i) -> p k h o i", k=KD, o=1, i=SSM_I),
                                             ACT.Copy).then_inc(c_out, 1)

        @block.tensor
        def _(pe):
            with pe.Fori(0, NCH // 2) as i:
                for u in range(2):
                    c = i * 2 + u
                    pe.wait_ge(loaded[u], (i + 1) * 32)
                    for t in range(4):
                        pe.wait_ge(c_out, c * 4 + (t + 1))
                        for b in range(KD):
                            last = nc.tensor.transpose(tr[4 + t][:, b * P:(b + 1) * P], c_in[:, u, t, b * P:(b + 1) * P], k.ident[:, :])
                        last.then_inc(c_tr, 1)
                    for t in range(4):
                        pe.wait_ge(normed, c * 4 + (t + 1))
                        pe.wait_ge(x_out, c * 4 + (t + 5))
                        for b in range(KD):
                            last = nc.tensor.transpose(tr[t][:, b * P:(b + 1) * P], x_in[:, u, t, b * P:(b + 1) * P], k.ident[:, :])
                        last.then_inc(x_tr, 1)

        @block.gpsimd
        def _(pool):
            nc.gpsimd.nop().then_inc(c_out, 4)
            nc.gpsimd.nop().then_inc(x_out, 8)



def conv_phase(nc, k, q_t, c_t, ssm_reversed, ssm_d, x, x1):
    assert GH * SSM_I == P
    STEPS = SSM_H // 2
    GSTEPS = GH // 2
    with phase(nc) as st:
        sb, ps, sem = opener(nc, st)
        d_all = sb("d_all", [P, SSM_H])
        toep = sb("toep", [P, 2, 2, D])
        toep_hi, toep_lo = sb("toep_hi", [P, 2, 2, D], F16), sb("toep_lo", [P, 2, 2, D], F16)
        prod = sb("prod", [P, KD, 2 * B, PAIRS])
        prod_hi = sb("prod_hi", [P, 2, KD, 2 * B, PAIRS], F16)
        prod_lo = sb("prod_lo", [P, 2, KD, 2 * B, PAIRS], F16)
        y = sb("y", [P, 2, KD, 2 * B, PAIRS])
        terms = sb("terms", [P, SSM_I, KD, 2 * B, SSM_I])
        sums = sb("sums", [P, 2, KD, B, GH, SSM_I])
        x_rows, gated = sb("x_rows", [P, B, D]), sb("gated", [P, B, D])
        conv = ps("conv", [P, 2, KD, D])
        d_loaded = sem("d_loaded")
        toep_loaded = [sem(f"toep_loaded{u}") for u in range(2)]
        toep_summed = sem("toep_summed")
        toep_hi_done, toep_lo_done = sem("toep_hi_done"), sem("toep_lo_done")
        prod_done, prod_hi_done, prod_lo_done = sem("prod_done"), sem("prod_hi_done"), sem("prod_lo_done")
        conv_done, conv_read = sem("conv_done"), sem("conv_read")
        weighed, half_sums, summed = sem("weighed"), sem("half_sums"), sem("summed")
        sum_done, sum_read = sem("sum_done"), sem("sum_read")
        x_loaded, x_added, x_stored = sem("x_loaded"), sem("x_added"), sem("x_stored")
        block = st.enter_context(nc.Block())
        x_g = x.rearrange("b (g r) d -> g r b d", g=GROUPS)
        x1_g = x1.rearrange("b (g r) d -> g r b d", g=GROUPS)

        def toeplitz(s, u):
            return bass.AP(tensor=ssm_reversed.tensor, offset=s * (2 * (P + D)),
                           ap=[[1, P], [P + D, 2], [1, D]])

        @block.sync
        def _(sp):
            sp.dma_start(d_all[:, :], ssm_d.partition_broadcast(P)).then_inc(d_loaded, 16)

            def load_toeplitz(s):
                sp.wait_ge(toep_lo_done, s + 1)
                sp.dma_start(toep[:, s % 2], toeplitz(s, s % 2)).then_inc(toep_loaded[s % 2], 16)

            def store(g):
                for b in range(B):
                    sp.wait_ge(x_added, g * B + b + 1)
                    sp.dma_start(x1_g[g, :, b, :], gated[:, b, :]).then_inc(x_stored, 16)

            for g in range(GROUPS):
                for j in range(GSTEPS):
                    load_toeplitz(g * GSTEPS + j)
                    if j == 1 and g:
                        store(g - 1)
                    if j == 1:
                        sp.dma_start(x_rows[:, :, :], x_g[g]).then_inc(x_loaded, 16)
            store(GROUPS - 1)
            sp.wait_ge(x_stored, GROUPS * B * 16)

        @block.vector
        def _(dve):
            dve.wait_ge(d_loaded, 16)

            def make_products(g, j):
                s, u = g * GSTEPS + j, j % 2
                dve.wait_ge(toep_loaded[u], g * (GSTEPS * 8) + (j // 2 + 1) * 16)
                for e in range(2):
                    nc.vector.scalar_tensor_tensor(toep[:, u, e, D - P:D], k.ident[:, ::-1], d_all[:, bass.ds(s * 2 + e, 1)],
                                                   toep[:, u, e, D - P:D], ALU.mult, ALU.add).then_inc(toep_summed, 1)
                dve.wait_ge(prod_hi_done, s + 1)
                dve.wait_ge(prod_lo_done, s + 1)
                ch = c_t[:, :, bass.ds(s * 2, 2), :, :].rearrange("p k h b i -> p k (h b) i")
                for i in range(SSM_I):
                    n = SSM_I - i
                    nc.vector.tensor_tensor(prod[:, :, :, pair_at(i):pair_at(i) + n],
                                            ch[:, :, :, i:i + 1].to_broadcast([P, KD, 2 * B, n]),
                                            ch[:, :, :, i:SSM_I], ALU.mult).then_inc(prod_done, 1)

            def weigh(g, j):
                s = g * GSTEPS + j
                dve.wait_ge(conv_read, s * 2 + 6)
                dve.wait_ge(summed, s * 2 + 2)
                q = q_t[:, :, bass.ds(s * 2, 2), :, :].rearrange("p k h b i -> p k (h b) i")
                for i in range(SSM_I):
                    n = SSM_I - i
                    last = nc.vector.tensor_tensor(terms[:, i, :, :, i:SSM_I], y[:, j % 2, :, :, pair_at(i):pair_at(i) + n],
                                                   q[:, :, :, i:i + 1].to_broadcast([P, KD, 2 * B, n]), ALU.mult)
                    if i < SSM_I - 1:
                        dst = terms[:, i + 1:SSM_I, :, :, i].rearrange("p i k b -> p k b i")
                        last = nc.vector.tensor_tensor(dst, y[:, j % 2, :, :, pair_at(i) + 1:pair_at(i) + n],
                                                       q[:, :, :, i + 1:SSM_I], ALU.mult)
                last.then_inc(weighed, 1)
                dve.wait_ge(weighed, s + 3)
                flat = terms[:, :, :, :, :].rearrange("p i k b j -> p i (k b j)")
                nc.vector.tensor_tensor(flat[:, 0:4], flat[:, 0:4], flat[:, 4:8], ALU.add).then_inc(half_sums, 1)
                dve.wait_ge(half_sums, s + 1)
                for e in range(2):
                    dst = sums[:, :, :, :, 2 * j + e].rearrange("p i k b j -> p (i k) b j")
                    src = terms[:, :, :, e * B:(e + 1) * B, :].rearrange("p i k b j -> p (i k) b j")
                    nc.vector.tensor_tensor(dst, src[:, 0:2 * KD], src[:, 2 * KD:4 * KD], ALU.add).then_inc(summed, 1)

            make_products(0, 0)
            make_products(0, 1)
            for g in range(GROUPS):
                for j in range(GSTEPS):
                    if j + 2 < GSTEPS or g + 1 < GROUPS:
                        make_products(g + (j + 2) // GSTEPS, (j + 2) % GSTEPS)
                    if j == 0:
                        dve.wait_ge(sum_done, (g + 1) * B)
                    weigh(g, j)

        @block.scalar
        def _(act):
            nc.scalar.preload_act_table(ACT.Copy)
            nc.scalar.nop().then_inc(prod_hi_done, 1)
            nc.scalar.nop().then_inc(sum_read, B)
            nc.scalar.nop().then_inc(conv_read, 4)

            def copy_out(g, j):
                s = g * GSTEPS + j
                act.wait_ge(weighed, s + 1)
                for e in range(2):
                    act.wait_ge(conv_done, s * 2 + (e + 1))
                    nc.scalar.activation(y[:, j % 2, :, e * B:(e + 1) * B, :].rearrange("p k b r -> p k (b r)"),
                                         conv[:, e, :, 0:B * PAIRS], ACT.Copy).then_inc(conv_read, 1)

            def split(s):
                u = s % 2
                act.wait_ge(toep_summed, (s + 1) * 2)
                if s >= 2:
                    act.wait_ge(conv_done, (s - 1) * 2)
                nc.scalar.activation(toep_hi[:, u], toep[:, u, :, ::-1], ACT.Copy).then_inc(toep_hi_done, 1)
                act.wait_ge(prod_done, (s + 1) * SSM_I)
                nc.scalar.activation(prod_hi[:, u].rearrange("p k b r -> p (k b r)"),
                                     prod[:, :, :, :].rearrange("p k b r -> p (k b r)"), ACT.Copy).then_inc(prod_hi_done, 1)

            split(0)
            split(1)
            for g in range(GROUPS):
                for j in range(GSTEPS):
                    copy_out(g, j)
                    if g * GSTEPS + j + 2 < STEPS:
                        split(g * GSTEPS + j + 2)
                if g:
                    act.wait_ge(x_stored, g * B * 16)
                for b in range(B):
                    act.wait_ge(sum_done, (g + 1) * B + (b + 1))
                    nc.scalar.activation(gated[:, b, :], conv[:, b // KD, b % KD, :], ACT.Copy,
                                         scale=k.tanh_gates[:, 0:1]).then_inc(sum_read, 1)

        @block.gpsimd
        def _(pool):
            nc.gpsimd.nop().then_inc(toep_lo_done, 2)
            nc.gpsimd.nop().then_inc(prod_lo_done, 1)
            nc.gpsimd.nop().then_inc(weighed, 2)
            nc.gpsimd.nop().then_inc(summed, 2)
            nc.gpsimd.nop().then_inc(sum_done, B)

            def rest(s):
                u = s % 2
                pool.wait_ge(toep_hi_done, s + 1)
                if s >= 2:
                    pool.wait_ge(conv_read, s * 2)
                nc.gpsimd.tensor_tensor(toep_lo[:, u], toep[:, u, :, ::-1], toep_hi[:, u], ALU.subtract).then_inc(toep_lo_done, 1)
                pool.wait_ge(prod_hi_done, s + 2)
                nc.gpsimd.tensor_tensor(prod_lo[:, u].rearrange("p k b r -> p (k b r)"),
                                        prod[:, :, :, :].rearrange("p k b r -> p (k b r)"),
                                        prod_hi[:, u].rearrange("p k b r -> p (k b r)"), ALU.subtract).then_inc(prod_lo_done, 1)

            def add_rows(g):
                pool.wait_ge(x_loaded, (g + 1) * 16)
                for b in range(B):
                    pool.wait_ge(sum_read, (g + 1) * B + b + 1)
                    nc.gpsimd.tensor_tensor(gated[:, b, :], gated[:, b, :], x_rows[:, b, :], ALU.add).then_inc(x_added, 1)

            for g in range(GROUPS):
                for j in range(GSTEPS):
                    rest(g * GSTEPS + j)
                    if g and j == 1:
                        add_rows(g - 1)
            add_rows(GROUPS - 1)

        @block.tensor
        def _(pe):
            for g in range(GROUPS):
                for j in range(GSTEPS):
                    s, u = g * GSTEPS + j, j % 2
                    pe.wait_ge(toep_lo_done, s + 3)
                    pe.wait_ge(prod_lo_done, s + 2)
                    if j == 0:
                        pe.wait_ge(sum_read, (g + 1) * B)
                    for e in range(2):
                        pe.wait_ge(conv_read, s * 2 + (e + 3))
                        for m in range(KD):
                            out = conv[:, e, m, 0:B * PAIRS]
                            for n in range(m + 1):
                                t = slice((m - n) * P, (m - n + 1) * P)
                                hi = prod_hi[:, u, n, e * B:(e + 1) * B, :]
                                lo = prod_lo[:, u, n, e * B:(e + 1) * B, :]
                                nc.tensor.matmul(out, toep_hi[:, u, e, t], hi, start=(n == 0), stop=False)
                                nc.tensor.matmul(out, toep_hi[:, u, e, t], lo, start=False, stop=False)
                                last = nc.tensor.matmul(out, toep_lo[:, u, e, t], hi, start=False, stop=(n == m))
                        last.then_inc(conv_done, 1)
                pe.wait_ge(conv_read, (g + 1) * GH + 4)
                pe.wait_ge(summed, (g + 1) * GH + 2)
                for b in range(B):
                    for m in range(KD):
                        out = conv[:, b // KD, b % KD, m * P:(m + 1) * P]
                        for i in range(2):
                            last = nc.tensor.matmul(out, sums[:, i, m, b].rearrange("p h j -> p (h j)"), k.ident[:, :],
                                                    is_transpose=True, start=(i == 0), stop=(i == 1))
                    last.then_inc(sum_done, 1)


E, I_MOE = 8, 352
I_SH = 704
MK = -(-I_MOE // P)
SK = -(-I_SH // P)
TILES = (2 * T + E * (P - 1)) // P
SLOTS = TILES * P


def rows_of(width, m):
    return min(P, width - m * P)


def shared_phase(nc, k, w, x1, xn_out, x1s, router_t, gate, up, s_gate, s_gate_b, s_up, s_up_b, s_down, s_down_b):
    with phase(nc) as st:
        sb, ps, sem = opener(nc, st)
        ln = LayerNorm(sb, sem, "x1")
        x_in = sb("x1_in", [P, 2, 4, D])
        xn = sb("xn", [P, 4, D])
        xt_hi, xt_lo = sb("xt_hi", [P, KD, CH], F16), sb("xt_lo", [P, KD, CH], F16)
        sg_hi, sg_lo = sb("sg_hi", [P, KD, I_SH], F16), sb("sg_lo", [P, KD, I_SH], F16)
        su_hi, su_lo = sb("su_hi", [P, KD, I_SH], F16), sb("su_lo", [P, KD, I_SH], F16)
        sd_hi, sd_lo = sb("sd_hi", [P, SK, D], F16), sb("sd_lo", [P, SK, D], F16)
        rw, rw_hi, rw_lo = sb("rw", [P, KD, E]), sb("rw_hi", [P, KD, E], F16), sb("rw_lo", [P, KD, E], F16)
        bg, bu, bd = sb("bg", [P, SK]), sb("bu", [P, SK]), sb("bd", [P, D])
        stage = sb("stage", [P, 2, KD * I_MOE])
        silu, h = sb("silu", [P, 2, CH]), sb("h", [P, 2, CH])
        h_hi, h_lo = sb("h_hi", [P, SK, CH], F16), sb("h_lo", [P, SK, CH], F16)
        summed = sb("ffn_sum", [P, D])
        tr = ps("tr", [P, KD, CH])
        gu = ps("gu", [P, 2, 2, CH])

        small_loaded = sem("small_loaded")
        stage_loaded = [sem(f"stage_loaded{u}") for u in range(2)]
        x_loaded = [sem(f"x1_loaded{u}") for u in range(2)]
        sw_hi, sw_lo = sem("sw_hi"), sem("sw_lo")
        ew_hi, ew_lo = sem("ew_hi"), sem("ew_lo")
        normed, xn_stored, turned = sem("xn_normed"), sem("xn_stored"), sem("turned")
        xt_hi_done, xt_lo_done = sem("xt_hi_done"), sem("xt_lo_done")
        routed, logits_read = sem("routed"), sem("logits_read")
        gu_done, silu_done, h_done = sem("gu_done"), sem("silu_done"), sem("h_done")
        h_hi_done, h_lo_done = sem("h_hi_done"), sem("h_lo_done")
        down_done, bias_added, out_done, out_stored = sem("down_done"), sem("bias_added"), sem("out_done"), sem("out_stored")
        block = st.enter_context(nc.Block())
        x1_d, x1s_d, xn_d = (a.rearrange("(c k p) d -> p (c k) d", p=P, k=4) for a in (x1, x1s, xn_out))

        pieces = []
        for hi, lo, m in ((sg_hi, sg_lo, s_gate), (su_hi, su_lo, s_up)):
            for b in range(0, KD, 2):
                pieces.append((hi[:, b:b + 2, :], lo[:, b:b + 2, :], m[b * P:(b + 2) * P, :].rearrange("(k p) n -> p k n", p=P), P))
        whole = I_SH // P
        for b in range(0, whole, 2):
            e = min(b + 2, whole)
            pieces.append((sd_hi[:, b:e, :], sd_lo[:, b:e, :], s_down[b * P:e * P, :].rearrange("(k p) n -> p k n", p=P), P))
        rest = I_SH - whole * P
        pieces.append((sd_hi[0:rest, whole:SK, :], sd_lo[0:rest, whole:SK, :],
                       s_down[whole * P:I_SH, :].rearrange("(k p) n -> p k n", k=1), rest))
        NP = len(pieces)
        assert NP % 2 == 0

        def staged(piece, u):
            hi, _, _, rows = piece
            k_, n = hi.shape[1], hi.shape[2]
            return stage[0:rows, u, 0:k_ * n].rearrange("p (k n) -> p k n", n=n)

        @block.sync
        def _(sp):
            def load_x(c, u):
                sp.wait_ge(out_stored, c * 16 + 16)
                sp.dma_start(x_in[:, u], x1_d[:, bass.ds(c * 4, 4), :]).then_inc(x_loaded[u], 16)

            load_x(0, 0)
            sp.dma_start(rw[:, :, :], router_t.rearrange("(k p) e -> p k e", p=P)).then_inc(small_loaded, 16)
            sp.dma_start(bd[:, :], s_down_b.partition_broadcast(P)).then_inc(small_loaded, 16)
            for dst, b in ((bg, s_gate_b), (bu, s_up_b)):
                sp.dma_start(dst[:, :], b).then_inc(small_loaded, 16)
            for n, piece in enumerate(pieces):
                if n >= 2:
                    sp.wait_ge(sw_lo, n - 1)
                sp.dma_start(staged(piece, n % 2), piece[2]).then_inc(stage_loaded[n % 2], 16)
            sp.wait_ge(sw_lo, NP)

            def chunk(c, u, last):
                if not last:
                    load_x(c + 1, 1 - u)
                sp.wait_ge(normed, (c + 1) * 4)
                sp.dma_start(xn_d[:, bass.ds(c * 4, 4), :], xn[:, :, :]).then_inc(xn_stored, 16)
                for q in range(4):
                    sp.wait_ge(ew_lo, c * 4 + (q + 1))
                    src = (gate, up)[q % 2][bass.ds(c * 2 + q // 2, 1), :, :].rearrange("o (k p) i -> p (o k) i", p=P)
                    sp.dma_start(stage[:, q % 2, :].rearrange("p (k i) -> p k i", k=KD), src).then_inc(stage_loaded[q % 2], 16)
                sp.wait_ge(out_done, (c + 2) * 4)
                sp.dma_start(x1s_d[:, bass.ds(c * 4, 4), :], x_in[:, u]).then_inc(out_stored, 16)

            for c in range(NCH):
                chunk(c, c % 2, c == NCH - 1)
            sp.wait_ge(out_stored, (NCH + 2) * 16)
            sp.wait_ge(xn_stored, (NCH + 1) * 16)

        @block.scalar
        def _(act):
            nc.scalar.nop().then_inc(xn_stored, 16)
            ln.root(nc, act, 0)
            for n, piece in enumerate(pieces):
                act.wait_ge(stage_loaded[n % 2], (n // 2 + 1) * 16)
                nc.scalar.activation(piece[0], staged(piece, n % 2), ACT.Copy).then_inc(sw_hi, 1)

            def chunk(c, last):
                for b in range(KD):
                    act.wait_ge(turned, c * KD + (b + 1))
                    nc.scalar.activation(xt_hi[:, b, :], tr[:, b, :], ACT.Copy).then_inc(xt_hi_done, 1)
                for m in range(SK):
                    r, u = rows_of(I_SH, m), m % 2
                    act.wait_ge(gu_done, c * SK + (m + 1))
                    act.wait_ge(h_done, c * SK + (m + 1))
                    nc.scalar.activation(silu[0:r, u, :], gu[0:r, u, 0, :], ACT.Silu, bias=bg[0:r, m:m + 1]).then_inc(silu_done, 1)
                    if m < 4:
                        split_expert(c, m)
                    act.wait_ge(h_done, c * SK + (m + 3))
                    nc.scalar.activation(h_hi[0:r, m, :], h[0:r, u, :], ACT.Copy).then_inc(h_hi_done, 1)
                if not last:
                    ln.root(nc, act, c + 1)

            def split_expert(c, q):
                act.wait_ge(stage_loaded[q % 2], c * 32 + (NP // 2 + q // 2 + 1) * 16)
                dst = (w.gate_hi, w.up_hi)[q % 2][:, bass.ds(c * 2 + q // 2, 1), :, :].rearrange("p o k i -> p (o k i)")
                nc.scalar.activation(dst, stage[:, q % 2, :], ACT.Copy).then_inc(ew_hi, 1)

            for c in range(NCH):
                chunk(c, c == NCH - 1)

        @block.gpsimd
        def _(pool):
            nc.gpsimd.nop().then_inc(out_stored, 32)
            nc.gpsimd.nop().then_inc(ew_lo, 2)
            nc.gpsimd.nop().then_inc(h_done, 2)
            nc.gpsimd.nop().then_inc(logits_read, 1)
            nc.gpsimd.nop().then_inc(out_done, 4)

            def chunk(c):
                for m in range(SK):
                    r, u = rows_of(I_SH, m), m % 2
                    pool.wait_ge(h_hi_done, c * SK + (m + 1))
                    nc.gpsimd.tensor_tensor(h_lo[0:r, m, :], h[0:r, u, :], h_hi[0:r, m, :], ALU.subtract).then_inc(h_lo_done, 1)
                    if m < 4:
                        q = m
                        pool.wait_ge(ew_hi, c * 4 + (q + 1))
                        hi, lo = ((w.gate_hi, w.gate_lo), (w.up_hi, w.up_lo))[q % 2]
                        hi, lo = (a[:, bass.ds(c * 2 + q // 2, 1), :, :].rearrange("p o k i -> p (o k i)") for a in (hi, lo))
                        nc.gpsimd.tensor_tensor(lo, stage[:, q % 2, :], hi, ALU.subtract).then_inc(ew_lo, 1)

            for c in range(NCH):
                chunk(c)

        @block.vector
        def _(dve):
            def normalise(c, u):
                dve.wait_ge(x_loaded[u], (c // 2 + 1) * 16)
                ln.statistics(nc, dve, x_in[:, u], c)
                dve.wait_ge(xn_stored, (c + 1) * 16)
                for t in range(4):
                    nc.vector.tensor_scalar(xn[:, t, :], x_in[:, u, t, :], ln.mean[:, t:t + 1], ln.rstd[:, t:t + 1],
                                            ALU.subtract, ALU.mult).then_inc(normed, 1)

            normalise(0, 0)
            dve.wait_ge(small_loaded, 16 * 4)
            for n, piece in enumerate(pieces):
                dve.wait_ge(sw_hi, n + 1)
                nc.vector.tensor_tensor(piece[1], staged(piece, n % 2), piece[0], ALU.subtract).then_inc(sw_lo, 1)
            nc.vector.tensor_copy(rw_hi[:, :, :], rw[:, :, :]).then_inc(sw_lo, 1)
            dve.wait_ge(sw_lo, NP + 1)
            nc.vector.tensor_tensor(rw_lo[:, :, :], rw[:, :, :], rw_hi[:, :, :], ALU.subtract).then_inc(sw_lo, 1)

            def chunk(c, u, last):
                for b in range(KD):
                    dve.wait_ge(xt_hi_done, c * KD + (b + 1))
                    nc.vector.tensor_tensor(xt_lo[:, b, :], tr[:, b, :], xt_hi[:, b, :], ALU.subtract).then_inc(xt_lo_done, 1)
                dve.wait_ge(routed, c + 1)
                nc.vector.tensor_copy(k.logits[:, bass.ds(c * 4, 4), :], tr[:, 0, 0:4 * E].rearrange("p (t e) -> p t e", e=E)
                                      ).then_inc(logits_read, 1)
                for m in range(SK):
                    r, v = rows_of(I_SH, m), m % 2
                    dve.wait_ge(silu_done, c * SK + (m + 1))
                    if not (isinstance(c, int) and c == 0 and m < 2):
                        dve.wait_ge(h_lo_done, c * SK + (m - 1))
                    nc.vector.scalar_tensor_tensor(h[0:r, v, :], gu[0:r, v, 1, :], bu[0:r, m:m + 1], silu[0:r, v, :],
                                                   ALU.add, ALU.mult).then_inc(h_done, 1)
                if not last:
                    normalise(c + 1, 1 - u)
                for t in range(4):
                    dve.wait_ge(down_done, c * 4 + (t + 1))
                    dve.wait_ge(out_done, c * 4 + (t + 4))
                    nc.vector.tensor_tensor(summed[:, :], tr[:, t, :], bd[:, :], ALU.add).then_inc(bias_added, 1)
                    dve.wait_ge(bias_added, c * 4 + (t + 1))
                    nc.vector.scalar_tensor_tensor(x_in[:, u, t, :], summed[:, :], k.tanh_gates[:, 2:3], x_in[:, u, t, :],
                                                   ALU.mult, ALU.add).then_inc(out_done, 1)

            for c in range(NCH):
                chunk(c, c % 2, c == NCH - 1)

        @block.tensor
        def _(pe):
            def chunk(c, u):
                for b in range(KD):
                    for t in range(4):
                        if b == 0:
                            pe.wait_ge(normed, c * 4 + (t + 1))
                        if t == 0:
                            if not (isinstance(c, int) and c == 0):
                                pe.wait_ge(bias_added, (c - 1) * 4 + (b + 1))
                        last = nc.tensor.transpose(tr[:, b, t * P:(t + 1) * P], xn[:, t, b * P:(b + 1) * P], k.ident[:, :])
                    last.then_inc(turned, 1)
                if isinstance(c, int) and c == 0:
                    pe.wait_ge(sw_lo, NP + 2)
                pe.wait_ge(xt_lo_done, (c + 1) * KD)
                for t in range(4):
                    tok = slice(t * P, (t + 1) * P)
                    for b in range(KD):
                        for n, (x_, r_) in enumerate(((xt_hi, rw_hi), (xt_hi, rw_lo), (xt_lo, rw_hi))):
                            last = nc.tensor.matmul(tr[:, 0, t * E:(t + 1) * E], x_[:, b, tok], r_[:, b, :],
                                                    start=(b == 0 and n == 0), stop=(b == KD - 1 and n == 2))
                last.then_inc(routed, 1)
                for m in range(SK):
                    r, v = rows_of(I_SH, m), m % 2
                    cols = slice(m * P, m * P + r)
                    pe.wait_ge(h_done, c * SK + (m + 1))
                    for o, (hi, lo) in enumerate(((sg_hi, sg_lo), (su_hi, su_lo))):
                        for b in range(KD):
                            nc.tensor.matmul(gu[0:r, v, o, :], hi[:, b, cols], xt_hi[:, b, :], start=(b == 0), stop=False)
                            nc.tensor.matmul(gu[0:r, v, o, :], hi[:, b, cols], xt_lo[:, b, :], start=False, stop=False)
                            last = nc.tensor.matmul(gu[0:r, v, o, :], lo[:, b, cols], xt_hi[:, b, :], start=False, stop=(b == KD - 1))
                    last.then_inc(gu_done, 1)
                pe.wait_ge(logits_read, c + 2)
                pe.wait_ge(h_lo_done, (c + 1) * SK)
                for t in range(4):
                    tok = slice(t * P, (t + 1) * P)
                    for m in range(SK):
                        r = rows_of(I_SH, m)
                        nc.tensor.matmul(tr[:, t, :], h_hi[0:r, m, tok], sd_hi[0:r, m, :], start=(m == 0), stop=False)
                        nc.tensor.matmul(tr[:, t, :], h_hi[0:r, m, tok], sd_lo[0:r, m, :], start=False, stop=False)
                        last = nc.tensor.matmul(tr[:, t, :], h_lo[0:r, m, tok], sd_hi[0:r, m, :], start=False, stop=(m == SK - 1))
                    last.then_inc(down_done, 1)

            for c in range(NCH):
                chunk(c, c % 2)



def route_phase(nc, k, w, down, slot_token):
    C = 2 * TT
    with phase(nc) as st:
        sb, ps, sem = opener(nc, st)
        small = [P, TT, E]
        first_i, steps_i, tiles_i = sb("first_i", [P, E], I32), sb("steps_i", [P, TT], I32), sb("tiles_i", [P, TILES], I32)
        first, steps, tiles_f = sb("first", [P, E]), sb("steps", [P, TT]), sb("tiles_f", [P, TILES])
        token = sb("token", [P, TT], I32)
        zeros = sb("zeros", [TILES, P], I32)
        before, ones = sb("before", [P, P], F16), sb("ones", [P, P], F16)
        best = [sb(f"best{n}", [P, TT]) for n in range(2)]
        tie = [sb(f"tie{n}", small) for n in range(2)]
        tie_best = [sb(f"tie_best{n}", [P, TT]) for n in range(2)]
        pick = [sb(f"pick{n}", small) for n in range(2)]
        rest = sb("rest", small)
        picked = sb("picked", [P, 2 * TT, E], F16)
        gap, e2, den = sb("r_gap", [P, TT]), sb("r_e2", [P, TT]), sb("r_den", [P, TT])
        over, tiles_of, tiles_to = sb("over", [P, E, TT]), sb("tiles_of", [P, E]), sb("tiles_to", [P, E])
        one8, start = sb("one8", [P, E]), sb("start", [P, E])
        place, placed = sb("place", small), [sb(f"placed{n}", small) for n in range(2)]
        slot_f = sb("slot_f", [P, 2, TT])
        past, texp_f = sb("past", [P, TILES, E]), sb("texp_f", [P, TILES])
        stage = sb("d_stage", [P, 2, MK, D])
        rank, total = ps("rank", [P, TT * E]), ps("total", [P, E])
        consts_made, before_zeroed = sem("consts_made"), sem("before_zeroed")
        zero_stored = sem("zero_stored")
        chain = sem("route_chain")
        e2_done, picked_done, ranked = sem("e2_done"), sem("picked_done"), sem("ranked")
        gap_done, slots_done, scattered, listed = sem("gap_done"), sem("slots_done"), sem("scattered"), sem("listed")
        stage_loaded = [sem(f"d_stage_loaded{u}") for u in range(2)]
        d_hi, d_lo = sem("d_hi"), sem("d_lo")
        block = st.enter_context(nc.Block())
        whole = I_MOE // P
        tail = I_MOE - whole * P

        @block.sync
        def _(sp):
            sp.wait_ge(consts_made, 1)
            sp.dma_start(slot_token.rearrange("(t p) o -> t (p o)", p=P), zeros[:, :]).then_inc(zero_stored, 16)
            for e in range(E):
                if e >= 2:
                    sp.wait_ge(d_lo, 2 * (e - 1))
                u = e % 2
                sp.dma_start(stage[:, u, 0:whole, :], down[e, 0:whole * P, :].rearrange("(k p) n -> p k n", p=P)).then_inc(stage_loaded[u], 16)
                sp.dma_start(stage[0:tail, u, whole, :], down[e, whole * P:I_MOE, :]).then_inc(stage_loaded[u], 16)
            sp.wait_ge(scattered, C * 16)
            with nc.allow_non_contiguous_dma(reason="one token number a slot"):
                sp.dma_start(k.slot_token[:, :], slot_token.rearrange("(t p) o -> p (t o)", p=P)).then_inc(listed, 16)
            sp.wait_ge(listed, 16)

        @block.gpsimd
        def _(pool):
            nc.gpsimd.memset(zeros[:, :], 0).then_inc(consts_made, 1)
            nc.gpsimd.memset(before[:, :], 1.0).then_inc(before_zeroed, 1)
            nc.gpsimd.memset(ones[:, :], 1.0)
            nc.gpsimd.memset(picked[:, 0:TT, :], 0.0)
            nc.gpsimd.memset(one8[:, :], 1.0)
            nc.gpsimd.iota(first_i[:, :], pattern=[[-1, E]], base=E, channel_multiplier=0)
            nc.gpsimd.iota(steps_i[:, :], pattern=[[P, TT]], base=0, channel_multiplier=0)
            nc.gpsimd.iota(tiles_i[:, :], pattern=[[1, TILES]], base=0, channel_multiplier=0)
            nc.gpsimd.iota(token[:, :], pattern=[[P, TT]], base=0, channel_multiplier=1)
            pool.wait_ge(before_zeroed, 1)
            nc.gpsimd.affine_select(out=before[:, :], in_=before[:, :], compare_op=ALU.is_gt, fill=0.0,
                                    base=0, pattern=[[1, P]], channel_multiplier=-1).then_inc(consts_made, 1)
            pool.wait_ge(zero_stored, 16)
            pool.wait_ge(slots_done, 1)
            for t in range(TT):
                for n in range(2):
                    nc.gpsimd.indirect_dma_start(slot_token, bass.IndirectOffsetOnAxis(ap=k.slots[:, n, t:t + 1], axis=0),
                                                 token[:, t:t + 1], None).then_inc(scattered, 16)

        @block.scalar
        def _(act):
            nc.scalar.preload_act_table(ACT.Exp)
            act.wait_ge(gap_done, 1)
            nc.scalar.activation(e2[:, :], gap[:, :], ACT.Exp).then_inc(e2_done, 1)
            for e in range(E):
                act.wait_ge(stage_loaded[e % 2], (e // 2 + 1) * 32)
                nc.scalar.activation(w.down_hi[:, e, 0:whole, :], stage[:, e % 2, 0:whole, :], ACT.Copy).then_inc(d_hi, 1)
                nc.scalar.activation(w.down_hi[0:tail, e, whole, :], stage[0:tail, e % 2, whole, :], ACT.Copy).then_inc(d_hi, 1)

        @block.tensor
        def _(pe):
            pe.wait_ge(picked_done, 1)
            nc.tensor.matmul(rank[:, :], before[:, :], picked[:, TT:2 * TT, :], start=True, stop=False)
            for s in range(1, TT):
                nc.tensor.matmul(rank[:, :], ones[:, :], picked[:, TT - s:2 * TT - s, :], start=False, stop=(s == TT - 1))
            for t in range(TT):
                last = nc.tensor.matmul(total[:, :], ones[:, :], picked[:, TT + t, :], start=(t == 0), stop=(t == TT - 1))
            last.then_inc(ranked, 1)

        @block.vector
        def _(dve):
            done = [0]

            def then(*made):
                for m in made:
                    m.then_inc(chain, 1)
                done[0] += len(made)
                dve.wait_ge(chain, done[0])

            V = nc.vector
            over_e = lambda a: a[:, :].unsqueeze(2).to_broadcast([P, TT, E])
            dve.wait_ge(consts_made, 2)
            then(V.tensor_copy(first[:, :], first_i[:, :]), V.tensor_copy(steps[:, :], steps_i[:, :]),
                 V.tensor_copy(tiles_f[:, :], tiles_i[:, :]))
            scores = k.logits
            for n in range(2):
                then(V.tensor_reduce(best[n][:, :], scores[:, :, :], AX.X, ALU.max))
                then(V.tensor_tensor(tie[n][:, :, :], scores[:, :, :], over_e(best[n]), ALU.is_equal))
                then(V.tensor_tensor(tie[n][:, :, :], tie[n][:, :, :], first[:, :].unsqueeze(1).to_broadcast(small), ALU.mult))
                then(V.tensor_reduce(tie_best[n][:, :], tie[n][:, :, :], AX.X, ALU.max))
                then(V.tensor_tensor(pick[n][:, :, :], tie[n][:, :, :], over_e(tie_best[n]), ALU.is_equal))
                if n == 0:
                    then(V.scalar_tensor_tensor(rest[:, :, :].rearrange("p t e -> p (t e)"), pick[0][:, :, :].rearrange("p t e -> p (t e)"),
                                                -3e38, scores[:, :, :].rearrange("p t e -> p (t e)"), ALU.mult, ALU.add))
                    scores = rest
            V.tensor_tensor(picked[:, TT:2 * TT, :], pick[0][:, :, :], pick[1][:, :, :], ALU.add).then_inc(picked_done, 1)
            V.tensor_tensor(gap[:, :], best[1][:, :], best[0][:, :], ALU.subtract).then_inc(gap_done, 1)
            dve.wait_ge(e2_done, 1)
            then(V.tensor_scalar(den[:, :], e2[:, :], 1.0, None, ALU.add))
            then(V.reciprocal(den[:, :], den[:, :]))
            then(V.tensor_scalar(k.mix[:, 0, :], den[:, :], k.tanh_gates[:, 2:3], None, ALU.mult))
            then(V.tensor_tensor(k.mix[:, 1, :], k.mix[:, 0, :], e2[:, :], ALU.mult))
            dve.wait_ge(ranked, 1)
            then(V.tensor_tensor(over[:, :, :], total[:, :].unsqueeze(2).to_broadcast([P, E, TT]),
                                 steps[:, :].unsqueeze(1).to_broadcast([P, E, TT]), ALU.is_gt))
            then(V.tensor_reduce(tiles_of[:, :], over[:, :, :], AX.X, ALU.add))
            then(V.tensor_tensor_scan(tiles_to[:, :], one8[:, :], tiles_of[:, :], 0.0, ALU.mult, ALU.add))
            then(V.tensor_tensor(start[:, :], tiles_to[:, :], tiles_of[:, :], ALU.subtract),
                 V.tensor_tensor(past[:, :, :], tiles_to[:, :].unsqueeze(1).to_broadcast([P, TILES, E]),
                                 tiles_f[:, :].unsqueeze(2).to_broadcast([P, TILES, E]), ALU.is_le))
            then(V.tensor_scalar(start[:, :], start[:, :], float(P), None, ALU.mult),
                 V.tensor_reduce(texp_f[:, :], past[:, :, :], AX.X, ALU.add))
            then(V.tensor_tensor(place[:, :, :], rank[:, :].rearrange("p (t e) -> p t e", e=E),
                                 start[:, :].unsqueeze(1).to_broadcast(small), ALU.add),
                 V.tensor_scalar(k.tile_expert[:, :], texp_f[:, :], float(E - 1), None, ALU.min))
            then(*(V.tensor_tensor(placed[n][:, :, :], place[:, :, :], pick[n][:, :, :], ALU.mult) for n in range(2)))
            then(*(V.tensor_reduce(slot_f[:, n, :], placed[n][:, :, :], AX.X, ALU.add) for n in range(2)))
            V.tensor_copy(k.slots[:, :, :], slot_f[:, :, :]).then_inc(slots_done, 1)
            for e in range(E):
                dve.wait_ge(d_hi, 2 * e + 2)
                V.tensor_tensor(w.down_lo[:, e, 0:whole, :], stage[:, e % 2, 0:whole, :], w.down_hi[:, e, 0:whole, :], ALU.subtract).then_inc(d_lo, 1)
                V.tensor_tensor(w.down_lo[0:tail, e, whole, :], stage[0:tail, e % 2, whole, :], w.down_hi[0:tail, e, whole, :],
                                ALU.subtract).then_inc(d_lo, 1)




def expert_phase(nc, k, w, xn, y_out):
    U = 3
    assert TILES % U == 0
    MT = MK - 1
    TAIL = I_MOE - MT * P
    with phase(nc) as st:
        sb, ps, sem = opener(nc, st)
        rows = sb("e_rows", [P, U, D])
        xt_hi, xt_lo = sb("e_xt_hi", [P, U, D], F16), sb("e_xt_lo", [P, U, D], F16)
        silu, h = sb("e_silu", [P, U, I_MOE]), sb("e_h", [P, U, I_MOE])
        h_hi, h_lo = sb("e_h_hi", [P, U, MK, P], F16), sb("e_h_lo", [P, U, MK, P], F16)
        y = sb("e_y", [P, U, D])
        turn, h_turn = ps("e_turn", [P, D]), ps("e_h_turn", [P, MK, P])
        gate_ps, up_ps, out_ps = ps("e_gate", [P, 2, D]), ps("e_up", [P, 2, D]), ps("e_out", [P, 2, D])
        gathered = [sem(f"gathered{u}") for u in range(U)]
        stored = [sem(f"e_stored{u}") for u in range(U)]
        turned, xt_hi_done, xt_lo_done = sem("e_turned"), sem("e_xt_hi_done"), sem("e_xt_lo_done")
        expanded, silu_done, h_done = sem("e_expanded"), sem("e_silu_done"), sem("e_h_done")
        h_turned, h_hi_done, h_lo_done = sem("e_h_turned"), sem("e_h_hi_done"), sem("e_h_lo_done")
        contracted, y_done = sem("e_contracted"), sem("e_y_done")
        block = st.enter_context(nc.Block())
        BODY = 2 * U
        PEEL = 9
        LOOPS = (TILES - PEEL) // BODY
        assert PEEL + LOOPS * BODY == TILES

        def over_tiles(eng, step):
            for n in range(PEEL):
                step(n, n // U, n, n, 0)
            with eng.Fori(0, LOOPS) as i:
                for j in range(PEEL, PEEL + BODY):
                    step(i * BODY + j, i * 2 + j // U, j, PEEL, 0)
            for n in range(TILES, TILES + 3):
                step(n, n // U, n, PEEL, n - TILES + 1)

        @block.gpsimd
        def _(pool):
            for n in range(TILES):
                if n >= U:
                    pool.wait_ge(turned, n - U + 1)
                nc.gpsimd.indirect_dma_start(rows[:, n % U, :], None, xn,
                                             bass.IndirectOffsetOnAxis(ap=k.slot_token[:, n:n + 1], axis=0)
                                             ).then_inc(gathered[n % U], 16)

        @block.tensor
        def _(pe):
            def step(n, rounds, r, early, late):
                if not late:
                    u = r % U
                    pe.wait_ge(gathered[u], rounds * 16 + 16)
                    if early >= 1:
                        pe.wait_ge(xt_lo_done, n)
                    for c in range(KD):
                        last = nc.tensor.transpose(turn[:, c * P:(c + 1) * P], rows[:, u, c * P:(c + 1) * P], k.ident[:, :])
                    last.then_inc(turned, 1)
                if early >= 1 and late <= 1:
                    u, b = (r - 1) % U, (r - 1) % 2
                    expert = nc.tensor.value_load(k.tile_expert[0:1, bass.ds(n - 1, 1)], min_val=0, max_val=E - 1)
                    pe.wait_ge(xt_lo_done, n)
                    if early >= 3:
                        pe.wait_ge(h_done, n - 2)
                    for dst, hi, lo in ((gate_ps, w.gate_hi, w.gate_lo), (up_ps, w.up_hi, w.up_lo)):
                        out = dst[:, b, 0:I_MOE]
                        for c in range(KD):
                            x_hi, x_lo = (a[:, u, c * P:(c + 1) * P] for a in (xt_hi, xt_lo))
                            w_hi, w_lo = (a[:, bass.ds(expert, 1), c, :].rearrange("p o i -> p (o i)") for a in (hi, lo))
                            nc.tensor.matmul(out, x_hi, w_hi, start=(c == 0), stop=False)
                            nc.tensor.matmul(out, x_lo, w_hi, start=False, stop=False)
                            last = nc.tensor.matmul(out, x_hi, w_lo, start=False, stop=(c == KD - 1))
                    last.then_inc(expanded, 1)
                if early >= 2 and late <= 2:
                    u = (r - 2) % U
                    pe.wait_ge(h_done, n - 1)
                    if early >= 3:
                        pe.wait_ge(h_lo_done, (n - 2) * 2)
                    for q in range(MK):
                        i_ = slice(q * P, min((q + 1) * P, I_MOE))
                        last = nc.tensor.transpose(h_turn[0:i_.stop - i_.start, q, :], h[:, u, i_], k.ident[:, :])
                    last.then_inc(h_turned, 1)
                if early >= 3:
                    u, b = (r - 3) % U, (r - 3) % 2
                    expert = nc.tensor.value_load(k.tile_expert[0:1, bass.ds(n - 3, 1)], min_val=0, max_val=E - 1)
                    pe.wait_ge(h_lo_done, (n - 2) * 2)
                    if early >= 5:
                        pe.wait_ge(y_done, n - 4)
                    for q in range(MK):
                        n_ = min(P, I_MOE - q * P)
                        a_hi, a_lo = (a[0:n_, u, q, :] for a in (h_hi, h_lo))
                        w_hi, w_lo = (a[0:n_, bass.ds(expert, 1), q, :].rearrange("p o d -> p (o d)") for a in (w.down_hi, w.down_lo))
                        nc.tensor.matmul(out_ps[:, b, :], a_hi, w_hi, start=(q == 0), stop=False)
                        nc.tensor.matmul(out_ps[:, b, :], a_lo, w_hi, start=False, stop=False)
                        last = nc.tensor.matmul(out_ps[:, b, :], a_hi, w_lo, start=False, stop=(q == MK - 1))
                    last.then_inc(contracted, 1)
            over_tiles(pe, step)

        parts = ((slice(0, P), slice(0, MT)), (slice(0, TAIL), slice(MT, MK)))

        @block.scalar
        def _(act):
            nc.scalar.preload_act_table(ACT.Silu)

            def step(n, rounds, r, early, late):
                if not late:
                    act.wait_ge(turned, n + 1)
                    if early >= 3:
                        act.wait_ge(expanded, n - 2)
                    nc.scalar.activation(xt_hi[:, r % U, :], turn[:, :], ACT.Copy).then_inc(xt_hi_done, 1)
                if early >= 1 and late <= 1:
                    act.wait_ge(expanded, n)
                    nc.scalar.activation(silu[:, (r - 1) % U, :], gate_ps[:, (r - 1) % 2, 0:I_MOE], ACT.Silu).then_inc(silu_done, 1)
                if early >= 2 and late <= 2:
                    act.wait_ge(h_turned, n - 1)
                    if early >= 5:
                        act.wait_ge(contracted, n - 4)
                    for rows_, blocks in parts:
                        nc.scalar.activation(h_hi[rows_, (r - 2) % U, blocks, :], h_turn[rows_, blocks, :], ACT.Copy).then_inc(h_hi_done, 1)
            over_tiles(act, step)

        @block.vector
        def _(dve):
            def step(n, rounds, r, early, late):
                if not late:
                    dve.wait_ge(xt_hi_done, n + 1)
                    nc.vector.tensor_tensor(xt_lo[:, r % U, :], turn[:, :], xt_hi[:, r % U, :], ALU.subtract).then_inc(xt_lo_done, 1)
                if early >= 1 and late <= 1:
                    dve.wait_ge(silu_done, n)
                    if early >= 4:
                        dve.wait_ge(h_turned, n - 3)
                    nc.vector.tensor_tensor(h[:, (r - 1) % U, :], up_ps[:, (r - 1) % 2, 0:I_MOE], silu[:, (r - 1) % U, :],
                                            ALU.mult).then_inc(h_done, 1)
                if early >= 2 and late <= 2:
                    dve.wait_ge(h_hi_done, (n - 1) * 2)
                    for rows_, blocks in parts:
                        nc.vector.tensor_tensor(h_lo[rows_, (r - 2) % U, blocks, :], h_turn[rows_, blocks, :],
                                                h_hi[rows_, (r - 2) % U, blocks, :], ALU.subtract).then_inc(h_lo_done, 1)
                if early >= 3:
                    u, b = (r - 3) % U, (r - 3) % 2
                    dve.wait_ge(contracted, n - 2)
                    if early >= 6:
                        dve.wait_ge(stored[u], rounds * 16 - 16)
                    nc.vector.tensor_copy(y[:, u, :], out_ps[:, b, :]).then_inc(y_done, 1)
            over_tiles(dve, step)

        @block.sync
        def _(sp):
            with sp.Fori(0, TILES // U) as i:
                for u in range(U):
                    sp.wait_ge(y_done, i * U + (u + 1))
                    sp.dma_start(y_out[bass.ds((i * U + u) * P, P), :], y[:, u, :]).then_inc(stored[u], 16)
            for u in range(U):
                sp.wait_ge(stored[u], TILES // U * 16)


HEADS1 = 16
HD1 = D // HEADS1
QUAD = P // HD1
XATTN_EPS = 1e-6
RING = 8
KV_SCALE = 1.0 / N


def xattn_phase(nc, k, x1s, y_rows, ctx, wq_t, wg_t, bg_cols, wkv_t, wo_t, x3):
    with phase(nc) as st:
        sb, ps, sem = opener(nc, st)
        X_BUFS = 3
        ln = LayerNorm(sb, sem, "x2")
        wq, wg, wkv, wo = (tuple(sb(f"{n}_{q}", [P, KD, m], F16) for q in ("hi", "lo"))
                           for n, m in (("wq", D), ("wg", D), ("wkv", 2 * D), ("wo", D)))
        stage = sb("a_stage", [P, 2, 2, 2 * D])
        bg = sb("a_bg", [P, KD])
        mask = sb("a_mask", [P, 2 * P])
        ctx_in, x2 = sb("a_ctx", [P, 4, D]), sb("a_x2", [P, X_BUFS, 4, D])
        y_in = sb("a_y", [P, 4, 2, D])
        xn = sb("a_xn", [P, 4, D])
        ct = tuple(sb(f"a_ct_{q}", [P, KD, CH], F16) for q in ("hi", "lo"))
        xt = tuple(sb(f"a_xt_{q}", [P, KD, CH], F16) for q in ("hi", "lo"))
        low, low_exp = sb("a_low", [P, 2, D]), sb("a_low_exp", [P, 2, D])
        feat = sb("a_feat", [P, 2, D])
        k_hi, k_lo = sb("a_k_hi", [P, 4, D], F16), sb("a_k_lo", [P, 4, D], F16)
        q_hi, q_lo = sb("a_q_hi", [P, KD, CH], F16), sb("a_q_lo", [P, KD, CH], F16)
        v_hi, v_lo = sb("a_v_hi", [P, 4, KD, 2 * P], F16), sb("a_v_lo", [P, 4, KD, P], F16)
        gate = sb("a_gate", [P, KD, CH])
        kv = sb("a_kv", [P, 2, KD, 2, P])
        kv_hi, kv_lo = sb("a_kv_hi", [P, 2, KD, 2, P], F16), sb("a_kv_lo", [P, 2, KD, 2, P], F16)
        denom, mixed_ = sb("a_denom", [P, 2, N]), sb("a_mixed", [P, 2, N])
        a_hi, a_lo = sb("a_a_hi", [P, KD, CH], F16), sb("a_a_lo", [P, KD, CH], F16)
        ring = ps("a_ring", [P, RING, D])

        w_loaded = [sem(f"a_w_loaded{u}") for u in range(2)]
        small_loaded, mask_made, mask_scaled, bg_negated = (sem(f"a_{n}") for n in ("small_loaded", "mask_made", "mask_scaled", "bg_negated"))
        w_hi, w_lo = sem("a_w_hi"), sem("a_w_lo")
        ctx_loaded, x_loaded = sem("a_ctx_loaded"), [sem(f"a_x_loaded{u}") for u in range(X_BUFS)]
        y_loaded = [sem(f"a_y_loaded{u}") for u in range(4)]
        first_added, combined, normed = sem("a_first_added"), sem("a_combined"), sem("a_normed")
        c_turned, c_hi, c_lo = sem("a_c_turned"), sem("a_c_hi"), sem("a_c_lo")
        x_turned, x_hi, x_lo = sem("a_x_turned"), sem("a_x_hi"), sem("a_x_lo")
        k_done, v_done, q_done, g_done, gate_done = (sem(f"a_{n}") for n in ("k_done", "v_done", "q_done", "g_done", "gate_done"))
        sum_done, mix_done, out_done, out_read = (sem(f"a_{n}") for n in ("sum_done", "mix_done", "out_done", "out_read"))
        v_hi_done, low_done, low_exp_done = sem("a_v_hi_done"), sem("a_low_done"), sem("a_low_exp_done")
        feat_done, feat_hi, feat_lo = sem("a_feat_done"), sem("a_feat_hi"), sem("a_feat_lo")
        v_lo_done, gate_exp = sem("a_v_lo_done"), sem("a_gate_exp")
        kv_done, kv_hi_done, kv_lo_done = sem("a_kv_done"), sem("a_kv_hi_done"), sem("a_kv_lo_done")
        denom_done, recip_done, mixed_done = sem("a_denom_done"), sem("a_recip_done"), sem("a_mixed_done")
        a_hi_done, a_lo_done, stored = sem("a_a_hi_done"), sem("a_a_lo_done"), sem("a_stored")
        block = st.enter_context(nc.Block())
        x1s_d, x3_d, ctx_d = (a.rearrange("(c k p) d -> p (c k) d", p=P, k=4) for a in (x1s, x3, ctx))

        pieces = [(m, dst, b) for m, dst in ((wkv_t, wkv), (wq_t, wq), (wg_t, wg), (wo_t, wo)) for b in (0, 2)]
        NP = len(pieces)

        def staged(n):
            cols = pieces[n][1][0].shape[2]
            return stage[:, n % 2, :, 0:cols]

        def ops(c, op, count):
            return [(c, op, n) for n in range(count)] if c < NCH else []

        def projections(c, first, second, last, count):
            return [(c, op, n) for n in range(count) for op in (first, second, last)] if c < NCH else []

        def weights(first, end):
            return [(0, "WS", n) for n in range(first, end)]

        schedule = (ops(0, "TC", 4) + weights(0, 2) + ops(0, "CB", 4) + ops(0, "NA", 1) + ops(0, "NB", 1)
                    + mixed(projections(0, "K", "V", "KF", 4), ops(0, "TX", 4) + weights(2, NP)))
        for c in range(NCH):
            schedule += mixed(projections(c, "Q", "G", "QF", KD), ops(c + 1, "TC", 4) + ops(c + 1, "CB", 4))
            schedule += ops(c, "SM", 4) + ops(c, "SS", 2)
            schedule += ops(c + 1, "NA", 1) + mixed(projections(c + 1, "K", "V", "KF", 4), ops(c, "AT", 2 * KD))
            schedule += ops(c + 1, "NB", 1) + mixed(ops(c, "OUT", 4), ops(c + 1, "TX", 4))

        READ = {"TC": (c_lo, 4), "TX": (x_lo, 4), "K": (feat_done, 8), "Q": (feat_done, 8), "V": (v_lo_done, 4), "G": (gate_exp, 4),
                "SM": (kv_done, 4), "AT": (mixed_done, 8), "OUT": (out_read, 4)}
        SECOND = {"KF": "K", "QF": "Q"}
        uses, home, previous = [], {}, {}
        for at in schedule:
            if at[1] in READ:
                home[at] = len(uses) % RING
                if len(uses) >= RING:
                    previous[at] = uses[-RING]
                uses.append(at)
            elif at[1] in SECOND:
                home[at] = home[at[0], SECOND[at[1]], at[2]]

        def run(step):
            for at in schedule:
                step(*at, home.get(at))

        @block.sync
        def _(sp):
            def load_rows(c):
                if c >= X_BUFS:
                    sp.wait_ge(stored, (c - X_BUFS + 1) * 4 * 16)
                sp.dma_start(x2[:, c % X_BUFS], x1s_d[:, c * 4:c * 4 + 4, :]).then_inc(x_loaded[c % X_BUFS], 16)

            sp.dma_start(ctx_in[:, :, :], ctx_d[:, 0:4, :]).then_inc(ctx_loaded, 16)
            sp.dma_start(bg[:, :], bg_cols).then_inc(small_loaded, 16)
            for n, (m, dst, b) in enumerate(pieces):
                if n >= 2:
                    sp.wait_ge(w_lo, n - 1)
                sp.dma_start(staged(n), m[b * P:(b + 2) * P, :].rearrange("(k p) n -> p k n", p=P)).then_inc(w_loaded[n % 2], 16)
                if n == 1:
                    load_rows(0)
            for c in range(NCH):
                if c < NCH - 1:
                    sp.wait_ge(c_turned, 4 * c + 4)
                    sp.dma_start(ctx_in[:, :, :], ctx_d[:, c * 4 + 4:c * 4 + 8, :]).then_inc(ctx_loaded, 16)
                    load_rows(c + 1)
                for t in range(4):
                    sp.wait_ge(out_read, c * 4 + t + 1)
                    sp.dma_start(x3_d[:, c * 4 + t, :], x2[:, c % X_BUFS, t]).then_inc(stored, 16)
            sp.wait_ge(stored, NCH * 4 * 16)
        @block.gpsimd
        def _(pool):
            nc.gpsimd.memset(v_hi[:, :, :, P:2 * P], 1.0).then_inc(mask_made, 1)
            nc.gpsimd.memset(mask[:, :], 0.0).then_inc(mask_made, 1)
            pool.wait_ge(mask_made, 2)
            for rep in range(2):
                m = mask[:, rep * P:(rep + 1) * P].rearrange("p (j i) -> p j i", i=HD1)
                nc.gpsimd.affine_select(out=m, in_=m, compare_op=ALU.is_gt, fill=KV_SCALE, base=0,
                                        pattern=[[HD1, QUAD], [0, HD1]], channel_multiplier=-1).then_inc(mask_made, 1)
            pool.wait_ge(mask_made, 4)
            for rep in range(2):
                m = mask[:, rep * P:(rep + 1) * P].rearrange("p (j i) -> p j i", i=HD1)
                nc.gpsimd.affine_select(out=m, in_=m, compare_op=ALU.is_gt, fill=0.0, base=HD1,
                                        pattern=[[HD1, QUAD], [0, HD1]], channel_multiplier=-1).then_inc(mask_made, 1)

            def gather(c, t):
                n = c * 4 + t
                if c:
                    pool.wait_ge(combined, n - 3)
                for e in range(2):
                    nc.gpsimd.indirect_dma_start(y_in[:, t, e, :], None, y_rows,
                                                 bass.IndirectOffsetOnAxis(ap=k.slots[:, e, n:n + 1], axis=0)
                                                 ).then_inc(y_loaded[t], 16)

            for t in range(4):
                gather(0, t)

            def step(c, op, n, bank):
                if op == "KF":
                    pool.wait_ge(feat_hi, c * 8 + n + 1)
                    nc.gpsimd.tensor_tensor(k_lo[:, n, :], feat[:, n % 2, :], k_hi[:, n, :], ALU.subtract).then_inc(feat_lo, 1)
                    if c < NCH - 1:
                        gather(c + 1, n)
                if op == "QF":
                    pool.wait_ge(feat_hi, c * 8 + n + 5)
                    nc.gpsimd.tensor_tensor(q_lo[:, n, :], feat[:, n % 2, :], q_hi[:, n, :], ALU.subtract).then_inc(feat_lo, 1)
                if op == "AT":
                    b, m = divmod(n, KD)
                    pool.wait_ge(a_hi_done, c * 8 + n + 1)
                    nc.gpsimd.tensor_tensor(a_lo[:, m, b * N:(b + 1) * N], mixed_[:, n % 2, :], a_hi[:, m, b * N:(b + 1) * N],
                                            ALU.subtract).then_inc(a_lo_done, 1)
            run(step)

        @block.scalar
        def _(act):
            A = nc.scalar.activation

            def step(c, op, n, bank):
                if op == "TC":
                    act.wait_ge(c_turned, c * 4 + n + 1)
                    if c:
                        act.wait_ge(v_done, c * 4)
                    A(ct[0][:, :, n * P:(n + 1) * P], ring[:, bank, :].rearrange("p (k i) -> p k i", i=P), ACT.Copy).then_inc(c_hi, 1)
                if op == "TX":
                    act.wait_ge(x_turned, c * 4 + n + 1)
                    if c:
                        act.wait_ge(g_done, c * 4)
                    A(xt[0][:, :, n * P:(n + 1) * P], ring[:, bank, :].rearrange("p (k i) -> p k i", i=P), ACT.Copy).then_inc(x_hi, 1)
                if op == "WS":
                    act.wait_ge(w_loaded[n % 2], (n // 2 + 1) * 16)
                    _, dst, b = pieces[n]
                    A(dst[0][:, b:b + 2, :], staged(n), ACT.Copy).then_inc(w_hi, 1)
                if op == "NA":
                    ln.root(nc, act, c)
                if op == "K":
                    act.wait_ge(low_done, c * 8 + n + 1)
                    A(low_exp[:, n % 2, :], low[:, n % 2, :], ACT.Exp).then_inc(low_exp_done, 1)
                if op == "V":
                    act.wait_ge(v_done, c * 4 + n + 1)
                    if c:
                        act.wait_ge(sum_done, c * 4)
                    A(v_hi[:, n, :, 0:P], ring[:, bank, :].rearrange("p (m i) -> p m i", i=P), ACT.Copy).then_inc(v_hi_done, 1)
                if op == "KF":
                    act.wait_ge(feat_done, c * 8 + n + 1)
                    A(k_hi[:, n, :], feat[:, n % 2, :], ACT.Copy).then_inc(feat_hi, 1)
                if op == "Q":
                    act.wait_ge(low_done, c * 8 + n + 5)
                    A(low_exp[:, n % 2, :], low[:, n % 2, :], ACT.Exp).then_inc(low_exp_done, 1)
                if op == "G":
                    act.wait_ge(g_done, c * 4 + n + 1)
                    if c:
                        act.wait_ge(denom_done, c * 8)
                    A(gate[:, n, :], ring[:, bank, :], ACT.Exp, bias=bg[:, n:n + 1], scale=-1.0).then_inc(gate_exp, 1)
                if op == "QF":
                    act.wait_ge(feat_done, c * 8 + n + 5)
                    if c:
                        act.wait_ge(mix_done, c * 8)
                    A(q_hi[:, n, :], feat[:, n % 2, :], ACT.Copy).then_inc(feat_hi, 1)
                if op == "SS":
                    act.wait_ge(kv_done, c * 4 + n * 2 + 2)
                    A(kv_hi[:, n], kv[:, n], ACT.Copy).then_inc(kv_hi_done, 1)
                if op == "AT":
                    b, m = divmod(n, KD)
                    act.wait_ge(mixed_done, c * 8 + n + 1)
                    if c:
                        act.wait_ge(out_done, c * 4)
                    A(a_hi[:, m, b * N:(b + 1) * N], mixed_[:, n % 2, :], ACT.Copy).then_inc(a_hi_done, 1)
            act.wait_ge(small_loaded, 16)
            act.wait_ge(bg_negated, 1)
            run(step)

        @block.vector
        def _(dve):
            V = nc.vector

            def low_part(bank, f):
                if f >= 2:
                    dve.wait_ge(low_exp_done, f - 1)
                V.tensor_scalar(low[:, f % 2, :], ring[:, bank, :], 0.0, None, ALU.min).then_inc(low_done, 1)

            def feature(bank, f):
                dve.wait_ge(low_exp_done, f + 1)
                if f >= 2:
                    dve.wait_ge(feat_lo, f - 1)
                V.scalar_tensor_tensor(feat[:, f % 2, :], ring[:, bank, :], 0.0, low_exp[:, f % 2, :], ALU.max, ALU.add).then_inc(feat_done, 1)

            def step(c, op, n, bank):
                if op == "CB":
                    u, at = c % X_BUFS, c * 4 + n
                    if n == 0:
                        dve.wait_ge(x_loaded[u], (c // X_BUFS + 1) * 16)
                    dve.wait_ge(y_loaded[n], (c + 1) * 32)
                    V.scalar_tensor_tensor(x2[:, u, n, :], y_in[:, n, 0, :], k.mix[:, 0, at:at + 1], x2[:, u, n, :],
                                           ALU.mult, ALU.add).then_inc(first_added, 1)
                    dve.wait_ge(first_added, at + 1)
                    V.scalar_tensor_tensor(x2[:, u, n, :], y_in[:, n, 1, :], k.mix[:, 1, at:at + 1], x2[:, u, n, :],
                                           ALU.mult, ALU.add).then_inc(combined, 1)
                    dve.wait_ge(combined, at + 1)
                    ln.tile(nc, x2[:, u], n)
                if op == "NA":
                    if c:
                        dve.wait_ge(normed, c * 4)
                    ln.variance(nc, dve, c)
                if op == "NB":
                    ln.inverse(nc, dve, c)
                    if c:
                        dve.wait_ge(x_turned, c * 4)
                    for t in range(4):
                        V.tensor_scalar(xn[:, t, :], x2[:, c % X_BUFS, t, :], ln.mean[:, t:t + 1], ln.rstd[:, t:t + 1],
                                        ALU.subtract, ALU.mult).then_inc(normed, 1)
                if op in ("TC", "TX"):
                    hi_done, lo_done, dst = (c_hi, c_lo, ct) if op == "TC" else (x_hi, x_lo, xt)
                    tok = slice(n * P, (n + 1) * P)
                    dve.wait_ge(hi_done, c * 4 + n + 1)
                    V.tensor_tensor(dst[1][:, :, tok], ring[:, bank, :].rearrange("p (k i) -> p k i", i=P), dst[0][:, :, tok],
                                    ALU.subtract).then_inc(lo_done, 1)
                if op == "WS":
                    dve.wait_ge(w_hi, n + 1)
                    _, dst, b = pieces[n]
                    V.tensor_tensor(dst[1][:, b:b + 2, :], staged(n), dst[0][:, b:b + 2, :], ALU.subtract).then_inc(w_lo, 1)
                if op == "K":
                    dve.wait_ge(k_done, c * 4 + n + 1)
                    low_part(bank, c * 8 + n)
                if op == "V":
                    dve.wait_ge(v_hi_done, c * 4 + n + 1)
                    V.tensor_tensor(v_lo[:, n], ring[:, bank, :].rearrange("p (m i) -> p m i", i=P), v_hi[:, n, :, 0:P],
                                    ALU.subtract).then_inc(v_lo_done, 1)
                if op == "KF":
                    feature(bank, c * 8 + n)
                if op == "Q":
                    dve.wait_ge(q_done, c * 4 + n + 1)
                    low_part(bank, c * 8 + 4 + n)
                if op == "QF":
                    feature(bank, c * 8 + 4 + n)
                    dve.wait_ge(gate_exp, c * 4 + n + 1)
                    V.tensor_scalar(gate[:, n, :], gate[:, n, :], 1.0, None, ALU.add).then_inc(gate_done, 1)
                if op == "SM":
                    b, half = divmod(n, 2)
                    dve.wait_ge(sum_done, c * 4 + n + 1)
                    if c:
                        dve.wait_ge(kv_lo_done, c * 2)
                    V.tensor_tensor(kv[:, b, 2 * half:2 * half + 2].rearrange("p m s i -> p m (s i)"),
                                    ring[:, bank, :].rearrange("p (q i) -> p q i", q=2),
                                    mask[:, :].unsqueeze(1).to_broadcast([P, 2, 2 * P]), ALU.mult).then_inc(kv_done, 1)
                if op == "SS":
                    dve.wait_ge(kv_hi_done, c * 2 + n + 1)
                    V.tensor_tensor(kv_lo[:, n], kv[:, n], kv_hi[:, n], ALU.subtract).then_inc(kv_lo_done, 1)
                if op == "AT":
                    b, m = divmod(n, KD)
                    at = c * 8 + n
                    dve.wait_ge(mix_done, at + 1)
                    dve.wait_ge(gate_done, c * 4 + m + 1)
                    if at >= 2:
                        dve.wait_ge(mixed_done, at - 1)
                    V.scalar_tensor_tensor(denom[:, n % 2, :], ring[:, bank, N:2 * N], XATTN_EPS * KV_SCALE, gate[:, m, b * N:(b + 1) * N],
                                           ALU.add, ALU.mult).then_inc(denom_done, 1)
                    dve.wait_ge(denom_done, at + 1)
                    V.reciprocal(denom[:, n % 2, :], denom[:, n % 2, :]).then_inc(recip_done, 1)
                    dve.wait_ge(recip_done, at + 1)
                    if at >= 2:
                        dve.wait_ge(a_lo_done, at - 1)
                    V.tensor_tensor(mixed_[:, n % 2, :], ring[:, bank, 0:N], denom[:, n % 2, :], ALU.mult).then_inc(mixed_done, 1)
                if op == "OUT":
                    dve.wait_ge(out_done, c * 4 + n + 1)
                    dve.wait_ge(normed, c * 4 + n + 1)
                    V.scalar_tensor_tensor(x2[:, c % X_BUFS, n, :], ring[:, bank, :], k.tanh_gates[:, 1:2], x2[:, c % X_BUFS, n, :],
                                           ALU.mult, ALU.add).then_inc(out_read, 1)
            dve.wait_ge(mask_made, 6)
            dve.wait_ge(small_loaded, 16)
            V.tensor_scalar(bg[:, :], bg[:, :], -1.0, None, ALU.mult).then_inc(bg_negated, 1)
            run(step)

        @block.tensor
        def _(pe):
            mm = nc.tensor.matmul

            def three(out, a, b, first, last):
                mm(out, a[0], b[0], start=first, stop=False)
                mm(out, a[0], b[1], start=False, stop=False)
                return mm(out, a[1], b[0], start=False, stop=last)

            def turn(bank, src, t):
                for b in range(KD):
                    last = nc.tensor.transpose(ring[:, bank, b * P:(b + 1) * P], src[:, t, b * P:(b + 1) * P], k.ident[:, :])
                return last

            def step(c, op, n, bank):
                if (c, op, n) in previous:
                    pc, pop, pn = previous[c, op, n]
                    read, per = READ[pop]
                    pe.wait_ge(read, pc * per + pn + (5 if pop == "Q" else 1))
                if op == "TC":
                    pe.wait_ge(ctx_loaded, (c + 1) * 16)
                    turn(bank, ctx_in, n).then_inc(c_turned, 1)
                if op == "TX":
                    pe.wait_ge(normed, c * 4 + n + 1)
                    turn(bank, xn, n).then_inc(x_turned, 1)
                if op in ("K", "V"):
                    o = op == "V"
                    pe.wait_ge(c_lo, c * 4 + n + 1)
                    pe.wait_ge(w_lo, 2)
                    for b in range(KD):
                        last = three(ring[:, bank, :], [a[:, b, n * P:(n + 1) * P] for a in ct],
                                     [a[:, b, o * D:(o + 1) * D] for a in wkv], b == 0, b == KD - 1)
                    last.then_inc(v_done if o else k_done, 1)
                if op in ("Q", "G"):
                    wt, made = (wq, q_done) if op == "Q" else (wg, g_done)
                    pe.wait_ge(x_lo, c * 4 + 4)
                    pe.wait_ge(w_lo, 4 if op == "Q" else 6)
                    for b in range(KD):
                        last = three(ring[:, bank, :], [a[:, b, n * P:(n + 1) * P] for a in wt], [a[:, b, :] for a in xt], b == 0, b == KD - 1)
                    last.then_inc(made, 1)
                if op == "SM":
                    b, half = divmod(n, 2)
                    pe.wait_ge(feat_lo, c * 8 + 4)
                    pe.wait_ge(v_lo_done, c * 4 + 4)
                    pe.wait_ge(mask_made, 1)
                    for q in range(2):
                        m = half * 2 + q
                        full, half_ = slice(q * N, (q + 1) * N), slice(q * N, q * N + P)
                        for t in (2 * b, 2 * b + 1):
                            kh, kl = (a[:, t, m * P:(m + 1) * P] for a in (k_hi, k_lo))
                            mm(ring[:, bank, full], kh, v_hi[:, t, m, :], start=(t == 2 * b), stop=False)
                            mm(ring[:, bank, half_], kh, v_lo[:, t, m, :], start=False, stop=False)
                            last = mm(ring[:, bank, full], kl, v_hi[:, t, m, :], start=False, stop=(t == 2 * b + 1))
                    last.then_inc(sum_done, 1)
                if op == "AT":
                    b, m = divmod(n, KD)
                    pe.wait_ge(feat_lo, c * 8 + 8)
                    pe.wait_ge(kv_lo_done, c * 2 + b + 1)
                    qs = [a[:, m, b * N:(b + 1) * N] for a in (q_hi, q_lo)]
                    for o in range(2):
                        last = three(ring[:, bank, o * N:(o + 1) * N], [a[:, b, m, o, :] for a in (kv_hi, kv_lo)], qs, True, True)
                    last.then_inc(mix_done, 1)
                if op == "OUT":
                    pe.wait_ge(a_lo_done, c * 8 + (n // 2 + 1) * 4)
                    pe.wait_ge(w_lo, NP)
                    for m in range(KD):
                        last = three(ring[:, bank, :], [a[:, m, n * P:(n + 1) * P] for a in (a_hi, a_lo)],
                                     [a[:, m, :] for a in wo], m == 0, m == KD - 1)
                    last.then_inc(out_done, 1)
            run(step)


EXPERTS2, SLOTS2, HID2 = 16, 128, 128
ES = EXPERTS2 * SLOTS2
NJ = ES // D
JE = D // SLOTS2
L2_EPS = 1e-12


def soft_weights_phase(nc, k, w, mu, w1):
    with phase(nc) as st:
        sb, ps, sem = opener(nc, st)
        raw = sb("mu_raw", [P, NJ, KD, D])
        square = sb("mu_square", [P, 2, KD, D])
        ones = sb("mu_ones", [P, P])
        norm = sb("mu_norm", [P, 2, D])
        stage = sb("w_stage", [P, EXPERTS2, KD, HID2])
        total = ps("mu_total", [P, 2, D])
        loaded = [sem(f"mu_loaded{j}") for j in range(NJ)]
        ones_made, squared, summed = sem("mu_ones_made"), sem("mu_squared"), sem("mu_summed")
        rooted, floored, inverted, scaled, mu_hi = (sem(f"mu_{n}") for n in ("rooted", "floored", "inverted", "scaled", "hi"))
        w_loaded = [sem(f"w1_loaded{n}") for n in range(EXPERTS2)]
        w_hi, w_lo = sem("w1_hi"), sem("w1_lo")
        block = st.enter_context(nc.Block())
        mu_d, w1_d = mu.rearrange("(k p) s -> p k s", p=P), w1.rearrange("e (k p) h -> p e k h", p=P)
        PER = EXPERTS2 // NJ

        @block.sync
        def _(sp):
            for j in range(NJ):
                sp.dma_start(raw[:, j], mu_d[:, :, j * D:(j + 1) * D]).then_inc(loaded[j], 16)
                for n in range(j * PER, (j + 1) * PER):
                    sp.dma_start(stage[:, n], w1_d[:, n]).then_inc(w_loaded[n], 16)

        @block.gpsimd
        def _(pool):
            nc.gpsimd.memset(ones[:, :], 1.0).then_inc(ones_made, 1)
            for n in range(EXPERTS2):
                pool.wait_ge(w_hi, n + 1)
                nc.gpsimd.tensor_tensor(w.w1[1][:, :, n, :], stage[:, n], w.w1[0][:, :, n, :], ALU.subtract).then_inc(w_lo, 1)

        @block.tensor
        def _(pe):
            pe.wait_ge(ones_made, 1)
            for j in range(NJ):
                pe.wait_ge(squared, j + 1)
                if j >= 2:
                    pe.wait_ge(rooted, j - 1)
                for c in range(KD):
                    last = nc.tensor.matmul(total[:, j % 2, :], ones[:, :], square[:, j % 2, c, :], start=(c == 0), stop=(c == KD - 1))
                last.then_inc(summed, 1)

        @block.scalar
        def _(act):
            nc.scalar.preload_act_table(ACT.Sqrt)

            def square_chunk(j):
                act.wait_ge(loaded[j], 16)
                if j >= 2:
                    act.wait_ge(summed, j - 1)
                nc.scalar.activation(square[:, j % 2], raw[:, j], ACT.Square).then_inc(squared, 1)

            square_chunk(0)
            for j in range(NJ):
                if j + 1 < NJ:
                    square_chunk(j + 1)
                act.wait_ge(summed, j + 1)
                if j >= 2:
                    act.wait_ge(scaled, j - 1)
                nc.scalar.activation(norm[:, j % 2, :], total[:, j % 2, :], ACT.Sqrt).then_inc(rooted, 1)
                for n in range(j * PER, (j + 1) * PER):
                    act.wait_ge(w_loaded[n], 16)
                    nc.scalar.activation(w.w1[0][:, :, n, :], stage[:, n], ACT.Copy).then_inc(w_hi, 1)
                act.wait_ge(scaled, j + 1)
                nc.scalar.activation(w.mu[0][:, :, j * D:(j + 1) * D], raw[:, j], ACT.Copy).then_inc(mu_hi, 1)

        @block.vector
        def _(dve):
            for j in range(NJ):
                u = j % 2
                dve.wait_ge(rooted, j + 1)
                nc.vector.tensor_scalar(norm[:, u, :], norm[:, u, :], L2_EPS, None, ALU.max).then_inc(floored, 1)
                dve.wait_ge(floored, j + 1)
                nc.vector.reciprocal(norm[:, u, :], norm[:, u, :]).then_inc(inverted, 1)
                dve.wait_ge(inverted, j + 1)
                nc.vector.tensor_tensor(raw[:, j], raw[:, j], norm[:, u, :].unsqueeze(1).to_broadcast([P, KD, D]), ALU.mult).then_inc(scaled, 1)
                dve.wait_ge(mu_hi, j + 1)
                nc.vector.tensor_tensor(w.mu[1][:, :, j * D:(j + 1) * D], raw[:, j], w.mu[0][:, :, j * D:(j + 1) * D], ALU.subtract)


def soft_moe_phase(nc, k, w, x3, gamma, beta, scale, b1_cols, w2, b2, out):
    with phase(nc) as st:
        sb, ps, sem = opener(nc, st)
        ln1, ln2 = LayerNorm(sb, sem, "s1", 2), LayerNorm(sb, sem, "s2", 2)
        gam, bet = sb("s_gamma", [P, D]), sb("s_beta", [P, D])
        scl, b1 = sb("s_scale", [P, 1]), sb("s_b1", [P, EXPERTS2])
        b2s = sb("s_b2", [EXPERTS2, D])
        x_in, x_ln, x_res = sb("s_x", [P, 2, D]), sb("s_xln", [P, 2, D]), sb("s_res", [P, 2, D])
        waste = sb("s_waste", [P, 2, D], F16)
        squares, l2, rs = sb("s_squares", [P, 2]), sb("s_l2", [P, 2]), sb("s_rs", [P, 2])
        xl = tuple(sb(f"s_xl_{q}", [P, 2, D], F16) for q in ("hi", "lo"))
        xt = tuple(sb(f"s_xt_{q}", [P, KD, N], F16) for q in ("hi", "lo"))
        lg = sb("s_lg", [P, 2, ES])
        top, low = sb("s_top", [P, 2, NJ]), sb("s_low", [P, 2])
        slot_top, slot_low = sb("s_slot_top", [P, 4, 2]), sb("s_slot_low", [P, 4, 2])
        slot_sum, slot_inv = sb("s_slot_sum", [P, 2, 2]), sb("s_slot_inv", [P, 2, 2])
        dt = sb("s_dt", [P, 2, 2, N])
        ed = tuple(sb(f"s_ed_{q}", [P, 2, ES], F16) for q in ("hi", "lo"))
        et = tuple(sb(f"s_et_{q}", [P, EXPERTS2, N], F16) for q in ("hi", "lo"))
        part = sb("s_part", [P, 2, EXPERTS2])
        part_t = sb("s_part_t", [EXPERTS2, 2, P])
        rn = sb("s_rn", [P, 2])
        si = tuple(sb(f"s_si_{q}", [P, 2, KD, D], F16) for q in ("hi", "lo"))
        w2_in = si[0][:, :, :, :].rearrange("p u k d -> p (u k d)").bitcast(F32).rearrange("p (u e d) -> p u e d", u=2, e=2)
        h32 = sb("s_h32", [P, 2, D])
        hp = tuple(sb(f"s_h_{q}", [P, 2, D], F16) for q in ("hi", "lo"))
        so = tuple(sb(f"s_so_{q}", [P, 2, D], F16) for q in ("hi", "lo"))
        ring = ps("s_ring", [P, 6, D])
        acc = ps("s_acc", [P, 2, D])

        names = ("small", "w2_hi", "w2_lo", "x_loaded", "res_loaded", "x1_done", "x_affine", "x_gamma", "xln_done", "squared",
                 "l2_done", "l2_floored", "l2_inverted", "rs_done", "xn_done", "xl_hi", "xl_lo", "turned", "xt_hi", "xt_lo",
                 "logits", "lg_out", "top_done", "top_all", "low_done", "d_turned", "slot_top_done", "slot_low_done", "dt_exp",
                 "slot_divided", "slot_inverted", "dt_done", "u_turned", "ed_hi", "ed_lo", "e_done", "part_done",
                 "zn_done", "zn_inv", "rn_done", "part_turned", "part_out", "et_turned", "et_hi", "et_lo",
                 "s_done", "si_hi", "si_lo", "h_done", "h_act", "h_hi", "h_lo", "o_done", "o_hi", "o_lo",
                 "c_done", "out_done", "stored")
        S = {n: sem(f"s_{n}") for n in names}
        w2_loaded = [sem(f"s_w2_loaded{u}") for u in range(2)]
        block = st.enter_context(nc.Block())
        x_d, out_d = (a.rearrange("(c p) d -> p c d", p=P) for a in (x3, out))

        def ops(op, first, end, nxt=0):
            return [(nxt, op, n) for n in range(first, end)]

        def contract(j):
            return [o for e in range(JE * j, JE * j + JE) for o in [(0, "O", e), (0, "OL", e)] + ([(0, "C", e - 1)] if e else [])]

        TURNS = ES * 2 // (4 * P)
        weights = ops("L", 0, 2, 1)
        for n in range(TURNS + 3):
            if n >= 3:
                weights += [(1, "U", n - 3)]
            if 1 <= n <= TURNS:
                weights += [(1, "F", n - 1)]
            if 2 <= n <= TURNS + 1:
                weights += [(1, "W", n - 2)]
            if n < TURNS:
                weights += [(1, "D", n)]
            if n % 2 == 0 and n + 2 < 2 * NJ:
                weights += ops("L", n + 2, n + 4, 1)
            if n >= TURNS + 3 - NJ:
                weights += ops("E", 2 * (n - TURNS - 3 + NJ), 2 * (n - TURNS - 3 + NJ) + 2, 1)
        norms = [(1, op, 0) for op in ("N1a", "N1b", "N2a", "N2b", "N3a", "N3b")]
        rows = ops("X", 0, 2, 1) + ops("XL", 0, 1, 1)
        HALF = JE * 3 // 2
        experts = (contract(1)[:HALF] + ops("H", 2, 3) + contract(1)[HALF:] + contract(2)[:HALF] + ops("H", 3, 4)
                   + contract(2)[HALF:] + contract(3) + ops("C", EXPERTS2 - 1, EXPERTS2))
        body = (mixed(mixed(ops("S", 0, 2 * KD), ops("T", 0, TURNS)), norms[:4])
                + ops("H", 0, 1) + norms[4:5] + ops("S", 2 * KD, 3 * KD) + ops("B", 0, 1) + norms[5:] + ops("H", 1, 2)
                + mixed(contract(0), ops("S", 3 * KD, 4 * KD)) + rows + mixed(experts, weights) + ops("OUT", 0, 1) + [(0, "skip", 0)])
        before = norms + rows + mixed(weights, ops("W2", 0, EXPERTS2 // 2, 1))
        last = [op for op in body if not op[0]]

        READ = {"X": ("xt_lo", 2), "L": ("lg_out", 2 * NJ), "D": ("dt_exp", TURNS), "U": ("ed_lo", TURNS), "T": ("et_lo", TURNS),
                "B": ("part_out", 1), "S": ("si_lo", NJ * KD), "H": ("h_act", NJ), "O": ("o_lo", EXPERTS2)}
        SECOND = {"F": "D", "OL": "O"}
        RING = 6

        def placed(ops_, uses):
            uses, result, home = list(uses), [], {}
            for nxt, op, n in ops_:
                bank = prev = None
                if op == "skip":
                    uses.append(uses[-RING])
                    continue
                if op in READ:
                    bank, prev = len(uses) % RING, uses[-RING]
                    uses.append((nxt, op, n))
                    home[nxt, op, n] = bank
                elif op in SECOND:
                    bank = home[nxt, SECOND[op], n]
                result.append((nxt, op, n, bank, prev))
            return result, [use and (use[0] - 1, *use[1:]) for use in uses[-RING:]]

        taken = sum(op in READ for _, op, _ in before)
        start, carry = placed(before, [None] * (2 * RING - taken % RING))
        first_ops, carry = placed(body, carry)
        loop_ops, loop_carry = placed(body, carry)
        last_ops, _ = placed(last, loop_carry)
        assert loop_carry == carry and sum(op in READ or op == "skip" for _, op, _ in body) % RING == 0

        def run(eng, step):
            def go(b, ops_):
                for nxt, op, n, bank, prev in ops_:
                    step(b + nxt, op, n, bank, prev and (b + prev[0], prev[1], prev[2]))
            go(-1, start)
            go(0, first_ops)
            with eng.Fori(1, B - 1) as b:
                go(b, loop_ops)
            go(B - 1, last_ops)

        def count(b, per_batch, n):
            return b * per_batch + (n + 1)

        def reusable(b, per_batch, n):
            return b * per_batch + max(n - 1, 0)

        def later(b):
            return not (isinstance(b, int) and b == 0)

        @block.sync
        def _(sp):
            for dst, src in ((gam, gamma), (bet, beta), (scl, scale)):
                sp.dma_start(dst[:, :], src.partition_broadcast(P)).then_inc(S["small"], 16)
            sp.dma_start(b1[:, :], b1_cols).then_inc(S["small"], 16)
            sp.dma_start(b2s[:, :], b2).then_inc(S["small"], 16)
            sp.dma_start(x_in[:, :, :], x_d[:, 0:2, :]).then_inc(S["x_loaded"], 16)

            def load_rows(b):
                sp.wait_ge(S["turned"], b * 2)
                sp.dma_start(x_in[:, :, :], x_d[:, bass.ds(b * 2, 2), :]).then_inc(S["x_loaded"], 16)

            def batch(b, ahead=True):
                if later(b):
                    sp.wait_ge(S["stored"], b * 16)
                sp.dma_start(x_res[:, :, :], x_d[:, bass.ds(b * 2, 2), :]).then_inc(S["res_loaded"], 16)
                if ahead:
                    load_rows(b + 2)
                sp.wait_ge(S["out_done"], b * 2 + 2)
                sp.dma_start(out_d[:, bass.ds(b * 2, 2), :], x_res[:, :, :]).then_inc(S["stored"], 16)

            w2_d = w2.rearrange("e h d -> h e d")
            for n in range(EXPERTS2 // 2):
                if n >= 2:
                    sp.wait_ge(S["w2_lo"], n - 1)
                sp.dma_start(w2_in[:, n % 2], w2_d[:, 2 * n:2 * n + 2, :]).then_inc(w2_loaded[n % 2], 16)
                if n == 1:
                    load_rows(1)
            batch(0)
            with sp.Fori(1, B - 2) as b:
                batch(b)
            batch(B - 2, ahead=False)
            batch(B - 1, ahead=False)
            sp.wait_ge(S["stored"], B * 16)

        @block.gpsimd
        def _(pool):
            def step(b, op, n, bank, prev):
                if op == "W2":
                    pool.wait_ge(S["w2_hi"], n + 1)
                    nc.gpsimd.tensor_tensor(w.w2[1][:, 2 * n:2 * n + 2, :], w2_in[:, n % 2], w.w2[0][:, 2 * n:2 * n + 2, :], ALU.subtract
                                            ).then_inc(S["w2_lo"], 1)
                if op == "N2b":
                    for t in range(2):
                        pool.wait_ge(S["x_affine"], count(b, 2, t))
                        nc.gpsimd.tensor_tensor(x_ln[:, t, :], x_ln[:, t, :], gam[:, :], ALU.mult).then_inc(S["x_gamma"], 1)
                    for t in range(2):
                        pool.wait_ge(S["x_gamma"], count(b, 2, t))
                        nc.gpsimd.tensor_tensor(x_ln[:, t, :], x_ln[:, t, :], bet[:, :], ALU.add).then_inc(S["xln_done"], 1)
                if op == "XL":
                    pool.wait_ge(S["xl_hi"], b + 1)
                    nc.gpsimd.tensor_tensor(xl[1][:, :, :], x_ln[:, :, :], xl[0][:, :, :], ALU.subtract).then_inc(S["xl_lo"], 1)
                if op == "H":
                    pool.wait_ge(S["h_hi"], count(b, NJ, n))
                    nc.gpsimd.tensor_tensor(hp[1][:, n % 2, :], h32[:, n % 2, :], hp[0][:, n % 2, :], ALU.subtract).then_inc(S["h_lo"], 1)
            pool.wait_ge(S["small"], 16 * 5)
            run(pool, step)

        @block.scalar
        def _(act):
            A = nc.scalar.activation

            def step(b, op, n, bank, prev):
                if op == "W2":
                    act.wait_ge(w2_loaded[n % 2], (n // 2 + 1) * 16)
                    A(w.w2[0][:, 2 * n:2 * n + 2, :], w2_in[:, n % 2], ACT.Copy).then_inc(S["w2_hi"], 1)
                if op == "N1a":
                    ln1.root(nc, act, b)
                if op == "N2a":
                    ln2.root(nc, act, b)
                if op == "N3a":
                    if later(b):
                        act.wait_ge(S["l2_done"], b)
                    for t in range(2):
                        act.wait_ge(S["xln_done"], count(b, 2, t))
                        A(waste[:, t, :], x_ln[:, t, :], ACT.Square, accum_out=squares[:, t:t + 1]).then_inc(S["squared"], 1)
                    act.wait_ge(S["squared"], count(b, 2, 1))
                    if later(b):
                        act.wait_ge(S["l2_inverted"], b)
                    A(l2[:, :], squares[:, :], ACT.Sqrt).then_inc(S["l2_done"], 1)
                if op == "XL":
                    if later(b):
                        act.wait_ge(S["s_done"], b * (NJ * KD))
                    A(xl[0][:, :, :], x_ln[:, :, :], ACT.Copy).then_inc(S["xl_hi"], 1)
                if op == "X":
                    act.wait_ge(S["turned"], count(b, 2, n))
                    if later(b):
                        act.wait_ge(S["logits"], b * (2 * NJ))
                    A(xt[0][:, :, n * P:(n + 1) * P], ring[:, bank, :].rearrange("p (k i) -> p k i", i=P), ACT.Copy).then_inc(S["xt_hi"], 1)
                if op == "L":
                    j, t = divmod(n, 2)
                    act.wait_ge(S["logits"], count(b, 2 * NJ, n))
                    if later(b):
                        act.wait_ge(S["et_turned"], b * TURNS)
                        act.wait_ge(S["part_done"], b * (2 * NJ))
                    A(lg[:, t, j * D:(j + 1) * D], ring[:, bank, :], ACT.Copy).then_inc(S["lg_out"], 1)
                if op == "F":
                    act.wait_ge(S["slot_low_done"], count(b, TURNS, n))
                    if later(b) or n >= 2:
                        act.wait_ge(S["u_turned"], reusable(b, TURNS, n))
                    for e in range(2):
                        last_ = A(dt[:, n % 2, e, :], ring[:, bank, e * N:(e + 1) * N], ACT.Exp, bias=slot_low[:, n % 4, e:e + 1],
                                  accum_out=slot_sum[:, n % 2, e:e + 1])
                    last_.then_inc(S["dt_exp"], 1)
                if op == "U":
                    act.wait_ge(S["u_turned"], count(b, TURNS, n))
                    if later(b):
                        act.wait_ge(S["s_done"], b * (NJ * KD))
                    A(ed[0][:, :, 2 * n * P:(2 * n + 2) * P], ring[:, bank, :].rearrange("p (t s) -> p t s", t=2), ACT.Copy
                      ).then_inc(S["ed_hi"], 1)
                if op == "E":
                    j, t = divmod(n, 2)
                    act.wait_ge(S["low_done"], b * 2 + 2)
                    act.wait_ge(S["d_turned"], count(b, TURNS, 2 * j + 1))
                    A(lg[:, t, j * D:(j + 1) * D], lg[:, t, j * D:(j + 1) * D], ACT.Exp, bias=low[:, t:t + 1]).then_inc(S["e_done"], 1)
                if op == "T":
                    act.wait_ge(S["et_turned"], count(b, TURNS, n))
                    if later(b):
                        act.wait_ge(S["c_done"], b * EXPERTS2)
                    A(et[0][:, 2 * n:2 * n + 2, :], ring[:, bank, :].rearrange("p (e i) -> p e i", e=2), ACT.Copy).then_inc(S["et_hi"], 1)
                if op == "S":
                    j, m = divmod(n, KD)
                    act.wait_ge(S["s_done"], count(b, NJ * KD, n))
                    if isinstance(b, int) and b == 0 and n == 0:
                        act.wait_ge(S["w2_lo"], EXPERTS2 // 2)
                    if later(b) or j >= 2:
                        act.wait_ge(S["h_done"], reusable(b, NJ, j))
                    A(si[0][:, j % 2, m, :], ring[:, bank, :], ACT.Copy, scale=1.0 / N).then_inc(S["si_hi"], 1)
                if op == "H":
                    act.wait_ge(S["h_done"], count(b, NJ, n))
                    if later(b) or n >= 2:
                        act.wait_ge(S["h_lo"], reusable(b, NJ, n))
                    for e in range(JE):
                        last_ = A(h32[:, n % 2, e * SLOTS2:(e + 1) * SLOTS2], ring[:, bank, e * SLOTS2:(e + 1) * SLOTS2], ACT.Gelu,
                                  bias=b1[:, n * JE + e:n * JE + e + 1])
                    last_.then_inc(S["h_act"], 1)
                if op == "O":
                    act.wait_ge(S["o_done"], count(b, EXPERTS2, n))
                    if later(b) or n >= 2:
                        act.wait_ge(S["c_done"], reusable(b, EXPERTS2, n))
                    A(so[0][:, n % 2, :], ring[:, bank, :], ACT.Copy).then_inc(S["o_hi"], 1)
            act.wait_ge(S["small"], 16 * 5)
            run(act, step)

        @block.vector
        def _(dve):
            V = nc.vector

            def step(b, op, n, bank, prev):
                if op == "N1a":
                    dve.wait_ge(S["x_loaded"], b * 16 + 16)
                    for t in range(2):
                        ln1.tile(nc, x_in, t)
                    ln1.variance(nc, dve, b)
                if op == "N1b":
                    ln1.inverse(nc, dve, b)
                    if later(b):
                        dve.wait_ge(S["xl_lo"], b)
                        dve.wait_ge(S["xn_done"], b * 2)
                    for t in range(2):
                        V.tensor_scalar(x_ln[:, t, :], x_in[:, t, :], ln1.mean[:, t:t + 1], ln1.rstd[:, t:t + 1], ALU.subtract,
                                        ALU.mult).then_inc(S["x1_done"], 1)
                if op == "N2a":
                    dve.wait_ge(S["x1_done"], b * 2 + 2)
                    for t in range(2):
                        ln2.tile(nc, x_ln, t)
                    ln2.variance(nc, dve, b)
                if op == "N2b":
                    ln2.inverse(nc, dve, b)
                    for t in range(2):
                        V.tensor_scalar(x_ln[:, t, :], x_ln[:, t, :], ln2.mean[:, t:t + 1], ln2.rstd[:, t:t + 1], ALU.subtract,
                                        ALU.mult).then_inc(S["x_affine"], 1)
                if op == "N3b":
                    dve.wait_ge(S["l2_done"], b + 1)
                    V.tensor_scalar(l2[:, :], l2[:, :], L2_EPS, None, ALU.max).then_inc(S["l2_floored"], 1)
                    dve.wait_ge(S["l2_floored"], b + 1)
                    V.reciprocal(rs[:, :], l2[:, :]).then_inc(S["l2_inverted"], 1)
                    dve.wait_ge(S["l2_inverted"], b + 1)
                    V.tensor_scalar(rs[:, :], rs[:, :], scl[:, 0:1], None, ALU.mult).then_inc(S["rs_done"], 1)
                    dve.wait_ge(S["rs_done"], b + 1)
                    dve.wait_ge(S["xln_done"], b * 2 + 2)
                    for t in range(2):
                        V.tensor_scalar(x_in[:, t, :], x_ln[:, t, :], rs[:, t:t + 1], None, ALU.mult).then_inc(S["xn_done"], 1)
                if op == "X":
                    dve.wait_ge(S["xt_hi"], count(b, 2, n))
                    tok = slice(n * P, (n + 1) * P)
                    V.tensor_tensor(xt[1][:, :, tok], ring[:, bank, :].rearrange("p (k i) -> p k i", i=P), xt[0][:, :, tok], ALU.subtract
                                    ).then_inc(S["xt_lo"], 1)
                if op == "L":
                    j, t = divmod(n, 2)
                    dve.wait_ge(S["lg_out"], count(b, 2 * NJ, n))
                    V.tensor_reduce(top[:, t, j:j + 1], lg[:, t, j * D:(j + 1) * D], AX.X, ALU.max).then_inc(S["top_done"], 1)
                    if j == NJ - 1:
                        dve.wait_ge(S["top_done"], count(b, 2 * NJ, n))
                        V.tensor_reduce(low[:, t:t + 1], top[:, t, :], AX.X, ALU.max).then_inc(S["top_all"], 1)
                        dve.wait_ge(S["top_all"], count(b, 2, t))
                        V.tensor_scalar(low[:, t:t + 1], low[:, t:t + 1], -1.0, None, ALU.mult).then_inc(S["low_done"], 1)
                if op == "D":
                    dve.wait_ge(S["d_turned"], count(b, TURNS, n))
                    V.tensor_reduce(slot_top[:, n % 4, :], ring[:, bank, :].rearrange("p (e i) -> p e i", e=2), AX.X, ALU.max
                                    ).then_inc(S["slot_top_done"], 1)
                    dve.wait_ge(S["slot_top_done"], count(b, TURNS, n))
                    V.tensor_scalar(slot_low[:, n % 4, :], slot_top[:, n % 4, :], -1.0, None, ALU.mult).then_inc(S["slot_low_done"], 1)
                if op == "W":
                    dve.wait_ge(S["dt_exp"], count(b, TURNS, n))
                    V.tensor_scalar(slot_inv[:, n % 2, :], slot_sum[:, n % 2, :], 1.0 / N, None, ALU.mult).then_inc(S["slot_divided"], 1)
                    dve.wait_ge(S["slot_divided"], count(b, TURNS, n))
                    V.reciprocal(slot_inv[:, n % 2, :], slot_inv[:, n % 2, :]).then_inc(S["slot_inverted"], 1)
                    dve.wait_ge(S["slot_inverted"], count(b, TURNS, n))
                    for e in range(2):
                        last_ = V.tensor_scalar(dt[:, n % 2, e, :], dt[:, n % 2, e, :], slot_inv[:, n % 2, e:e + 1], None, ALU.mult)
                    last_.then_inc(S["dt_done"], 1)
                if op == "U":
                    dve.wait_ge(S["ed_hi"], count(b, TURNS, n))
                    s = slice(2 * n * P, (2 * n + 2) * P)
                    V.tensor_tensor(ed[1][:, :, s], ring[:, bank, :].rearrange("p (t s) -> p t s", t=2), ed[0][:, :, s], ALU.subtract
                                    ).then_inc(S["ed_lo"], 1)
                if op == "E":
                    j, t = divmod(n, 2)
                    dve.wait_ge(S["e_done"], count(b, 2 * NJ, n))
                    if later(b) and n == 0:
                        dve.wait_ge(S["part_turned"], b)
                    V.tensor_reduce(part[:, t, j * JE:(j + 1) * JE], lg[:, t, j * D:(j + 1) * D].rearrange("p (e i) -> p e i", i=SLOTS2),
                                    AX.X, ALU.add).then_inc(S["part_done"], 1)
                if op == "B":
                    dve.wait_ge(S["part_done"], (b + 1) * (2 * NJ))
                    if later(b):
                        dve.wait_ge(S["out_done"], b * 2)
                        dve.wait_ge(S["c_done"], b * EXPERTS2)
                    V.tensor_reduce(rn[:, :], part[:, :, :], AX.X, ALU.add).then_inc(S["zn_done"], 1)
                    dve.wait_ge(S["zn_done"], b + 1)
                    V.reciprocal(rn[:, :], rn[:, :]).then_inc(S["zn_inv"], 1)
                    dve.wait_ge(S["zn_inv"], b + 1)
                    V.tensor_scalar(rn[:, :], rn[:, :], k.tanh_gates[:, 3:4], None, ALU.mult).then_inc(S["rn_done"], 1)
                    dve.wait_ge(S["part_turned"], b + 1)
                    V.tensor_copy(part_t[:, :, :], ring[0:EXPERTS2, bank, 0:2 * P].rearrange("p (t i) -> p t i", i=P)).then_inc(S["part_out"], 1)
                if op == "T":
                    dve.wait_ge(S["et_hi"], count(b, TURNS, n))
                    V.tensor_tensor(et[1][:, 2 * n:2 * n + 2, :], ring[:, bank, :].rearrange("p (e i) -> p e i", e=2),
                                    et[0][:, 2 * n:2 * n + 2, :], ALU.subtract).then_inc(S["et_lo"], 1)
                if op == "S":
                    j, m = divmod(n, KD)
                    dve.wait_ge(S["si_hi"], count(b, NJ * KD, n))
                    V.scalar_tensor_tensor(si[1][:, j % 2, m, :], ring[:, bank, :], 1.0 / N, si[0][:, j % 2, m, :], ALU.mult, ALU.subtract
                                           ).then_inc(S["si_lo"], 1)
                if op == "H":
                    dve.wait_ge(S["h_act"], count(b, NJ, n))
                    if later(b) or n >= 2:
                        dve.wait_ge(S["o_done"], b * EXPERTS2 + max(n - 1, 0) * JE)
                    V.tensor_copy(hp[0][:, n % 2, :], h32[:, n % 2, :]).then_inc(S["h_hi"], 1)
                if op == "OL":
                    dve.wait_ge(S["o_hi"], count(b, EXPERTS2, n))
                    V.tensor_tensor(so[1][:, n % 2, :], ring[:, bank, :], so[0][:, n % 2, :], ALU.subtract).then_inc(S["o_lo"], 1)
                if op == "OUT":
                    dve.wait_ge(S["c_done"], (b + 1) * EXPERTS2)
                    dve.wait_ge(S["res_loaded"], b * 16 + 16)
                    dve.wait_ge(S["rn_done"], b + 1)
                    for t in range(2):
                        V.scalar_tensor_tensor(x_res[:, t, :], acc[:, t, :], rn[:, t:t + 1], x_res[:, t, :], ALU.mult, ALU.add
                                               ).then_inc(S["out_done"], 1)
            dve.wait_ge(S["small"], 16 * 5)
            run(dve, step)

        @block.tensor
        def _(pe):
            mm = nc.tensor.matmul

            def three(out_, a, b_, first, last_):
                mm(out_, a[0], b_[0], start=first, stop=False)
                mm(out_, a[0], b_[1], start=False, stop=False)
                return mm(out_, a[1], b_[0], start=False, stop=last_)

            def step(b, op, n, bank, prev):
                if prev:
                    name, per = READ[prev[1]]
                    pe.wait_ge(S[name], count(prev[0], per, prev[2]))
                if op == "X":
                    pe.wait_ge(S["xn_done"], count(b, 2, n))
                    for c in range(KD):
                        last_ = nc.tensor.transpose(ring[:, bank, c * P:(c + 1) * P], x_in[:, n, c * P:(c + 1) * P], k.ident[:, :])
                    last_.then_inc(S["turned"], 1)
                if op == "L":
                    j, t = divmod(n, 2)
                    pe.wait_ge(S["xt_lo"], count(b, 2, t))
                    tok = slice(t * P, (t + 1) * P)
                    for c in range(KD):
                        last_ = three(ring[:, bank, :], [a[:, c, tok] for a in xt], [a[:, c, j * D:(j + 1) * D] for a in w.mu],
                                      c == 0, c == KD - 1)
                    last_.then_inc(S["logits"], 1)
                if op == "D":
                    pe.wait_ge(S["lg_out"], count(b, 2 * NJ, 2 * (n // 2) + 1))
                    for e in range(2):
                        for t in range(2):
                            at = (e * 2 + t) * P
                            last_ = nc.tensor.transpose(ring[:, bank, at:at + P], lg[:, t, (2 * n + e) * P:(2 * n + e + 1) * P], k.ident[:, :])
                    last_.then_inc(S["d_turned"], 1)
                if op == "U":
                    pe.wait_ge(S["dt_done"], count(b, TURNS, n))
                    for t in range(2):
                        for e in range(2):
                            at = (t * 2 + e) * P
                            last_ = nc.tensor.transpose(ring[:, bank, at:at + P], dt[:, n % 2, e, t * P:(t + 1) * P], k.ident[:, :])
                    last_.then_inc(S["u_turned"], 1)
                if op == "T":
                    pe.wait_ge(S["e_done"], count(b, 2 * NJ, 2 * (n // 2) + 1))
                    for e in range(2):
                        for t in range(2):
                            at = (e * 2 + t) * P
                            last_ = nc.tensor.transpose(ring[:, bank, at:at + P], lg[:, t, (2 * n + e) * P:(2 * n + e + 1) * P], k.ident[:, :])
                    last_.then_inc(S["et_turned"], 1)
                if op == "B":
                    pe.wait_ge(S["part_done"], (b + 1) * (2 * NJ))
                    for t in range(2):
                        last_ = nc.tensor.transpose(ring[0:EXPERTS2, bank, t * P:(t + 1) * P], part[:, t, :], k.ident[:, :])
                    last_.then_inc(S["part_turned"], 1)
                if op == "S":
                    j, m = divmod(n, KD)
                    pe.wait_ge(S["xl_lo"], b + 1)
                    pe.wait_ge(S["ed_lo"], count(b, TURNS, 2 * j + 1))
                    for t in range(2):
                        last_ = three(ring[:, bank, :], [a[:, t, m * P:(m + 1) * P] for a in xl],
                                      [a[:, t, j * D:(j + 1) * D] for a in ed], t == 0, t == 1)
                    last_.then_inc(S["s_done"], 1)
                if op == "H":
                    pe.wait_ge(S["si_lo"], b * (NJ * KD) + (n + 1) * KD)
                    for e in range(JE):
                        s = slice(e * SLOTS2, (e + 1) * SLOTS2)
                        for c in range(KD):
                            last_ = three(ring[:, bank, s], [a[:, c, n * JE + e, :] for a in w.w1], [a[:, n % 2, c, s] for a in si],
                                          c == 0, c == KD - 1)
                    last_.then_inc(S["h_done"], 1)
                if op == "O":
                    j, e = divmod(n, JE)
                    pe.wait_ge(S["h_lo"], count(b, NJ, j))
                    if isinstance(b, int) and b == 0 and n == 0:
                        pe.wait_ge(S["w2_lo"], EXPERTS2 // 2)
                    s = slice(e * SLOTS2, (e + 1) * SLOTS2)
                    three(ring[:, bank, :], [a[:, j % 2, s] for a in hp], [a[:, n, :] for a in w.w2], True, True).then_inc(S["o_done"], 1)
                if op == "C":
                    if n == 0:
                        pe.wait_ge(S["part_out"], b + 1)
                        if later(b):
                            pe.wait_ge(S["out_done"], b * 2)
                        for t in range(2):
                            mm(acc[:, t, :], part_t[:, t, :], b2s[:, :], start=True, stop=False)
                        pe.wait_ge(S["et_lo"], (b + 1) * TURNS)
                    pe.wait_ge(S["o_lo"], count(b, EXPERTS2, n))
                    for t in range(2):
                        last_ = three(acc[:, t, :], [a[:, n, t * P:(t + 1) * P] for a in et], [a[:, n % 2, :] for a in so],
                                      False, n == EXPERTS2 - 1)
                    last_.then_inc(S["c_done"], 1)
            pe.wait_ge(S["small"], 16 * 5)
            run(pe, step)



class OnChip:
    pass


def transformer(nc, a, out):
    F, X = "L0_ffn_", "L1_xattn_"

    def scratch(name, shape, dt=F32):
        return nc.dram_tensor(name, shape, dt).ap()

    x1, xn, x1s, x3 = (scratch(name, (T, D)) for name in ("after_conv", "normed_rows", "after_shared", "after_xattn"))
    expert_rows, slot_token = scratch("expert_rows", (SLOTS, D)), scratch("slot_token_rows", (SLOTS, 1), I32)
    flat = {name: a[name].rearrange("b n d -> (b n) d") for name in ("x", "ctx_2048")}
    with ExitStack() as whole:
        sb, _, _ = opener(nc, whole)
        k = OnChip()
        k.ident, k.ident16 = sb("ident", [P, P]), sb("ident16", [P, P], F16)
        k.gates, k.tanh_gates = sb("gates", [P, 4]), sb("tanh_gates", [P, 4])
        constants(nc, k, a["g_xattn"], a["g_ffn"])

        with ExitStack() as st:
            sb, _, _ = opener(nc, st)
            q_t, c_t = (sb(name, [P, KD, SSM_H, B, SSM_I]) for name in ("q_t", "c_t"))
            conv_operands(nc, k, a["x"], a["ctx_2048"], q_t, c_t)
            conv_phase(nc, k, q_t, c_t, a["ssm_reversed"], a["L0_xattn_D"], a["x"], x1.rearrange("(b n) d -> b n d", n=N))

        with ExitStack() as routed:
            sb, _, _ = opener(nc, routed)
            k.slots, k.mix = sb("slots", [P, 2, TT], I32), sb("mix", [P, 2, TT])
            with ExitStack() as st:
                sb, _, _ = opener(nc, st)
                w = OnChip()
                k.logits = sb("router_logits", [P, TT, E])
                k.tile_expert, k.slot_token = sb("tile_expert", [P, TILES], I32), sb("slot_token", [P, TILES], I32)
                w.gate_hi, w.gate_lo, w.up_hi, w.up_lo = (sb(f"w_{n}", [P, E, KD, I_MOE], F16) for n in ("gate_hi", "gate_lo", "up_hi", "up_lo"))
                shared_phase(nc, k, w, x1, xn, x1s, a["router_t"], a[F + "gate_w"], a[F + "up_w"], a[F + "s_gate_w"],
                             a["s_gate_b_cols"], a[F + "s_up_w"], a["s_up_b_cols"], a[F + "s_down_w"], a[F + "s_down_b"])
                w.down_hi, w.down_lo = (sb(f"w_down_{q}", [P, E, MK, D], F16) for q in ("hi", "lo"))
                route_phase(nc, k, w, a[F + "down_w"], slot_token)
                expert_phase(nc, k, w, xn, expert_rows)
            xattn_phase(nc, k, x1s, expert_rows, flat["ctx_2048"], a["wq_t"], a["wg_t"], a["bg_cols"], a["wkv_t"], a["wo_t"], x3)

        with ExitStack() as st:
            sb, _, _ = opener(nc, st)
            w = OnChip()
            w.mu = tuple(sb(f"w_mu_{q}", [P, KD, ES], F16) for q in ("hi", "lo"))
            w.w1 = tuple(sb(f"w_w1_{q}", [P, KD, EXPERTS2, HID2], F16) for q in ("hi", "lo"))
            w.w2 = tuple(sb(f"w_w2_{q}", [P, EXPERTS2, D], F16) for q in ("hi", "lo"))
            F = "L1_ffn_"
            soft_weights_phase(nc, k, w, a[F + "mu"], a[F + "W1"])
            soft_moe_phase(nc, k, w, x3, a[F + "gamma"], a[F + "beta"], a[F + "scale"], a["b1_cols"], a[F + "W2"], a[F + "b2"], out)


def columns(bias):
    blocks = -(-bias.shape[0] // P)
    filled = np.zeros(blocks * P, bias.dtype)
    filled[:bias.shape[0]] = bias
    return np.ascontiguousarray(filled.reshape(blocks, P).T)


def kernel(**inputs):
    import concourse.bacc as bacc
    from concourse.bass_utils import run_bass_kernel_spmd

    a = dict(inputs)
    turned = lambda m: np.ascontiguousarray(m.T)
    ssm = a.pop("L0_xattn_ssm_kernel")
    a["ssm_reversed"] = np.zeros((ssm.shape[0], D + P), ssm.dtype)
    a["ssm_reversed"][:, :D] = ssm[:, ::-1]
    a["router_t"] = turned(a.pop("L0_ffn_router_w"))
    for new, old in (("wq_t", "Wq"), ("wg_t", "Wg"), ("wkv_t", "Wkv"), ("wo_t", "Wo")):
        a[new] = turned(a.pop("L1_xattn_" + old))
    for new, old in (("s_gate_b_cols", "L0_ffn_s_gate_b"), ("s_up_b_cols", "L0_ffn_s_up_b"), ("bg_cols", "L1_xattn_bg")):
        a[new] = columns(a.pop(old))
    a["b1_cols"] = turned(a.pop("L1_ffn_b1"))
    a["L1_ffn_mu"] = a["L1_ffn_mu"].reshape(D, ES)

    nc = bacc.Bacc("TRN2", target_bir_lowering=False, num_devices=1)
    arrays, args = {}, {}
    for name, value in a.items():
        value = np.ascontiguousarray(value)
        arrays[f"in_{name}"] = value
        args[name] = nc.dram_tensor(f"in_{name}", value.shape, mybir.dt.from_np(value.dtype), kind="ExternalInput").ap()
    out = nc.dram_tensor("out", (T, D), F32, kind="ExternalOutput").ap()
    transformer(nc, args, out)
    result = run_bass_kernel_spmd(nc, [arrays], core_ids=[0])
    return result.results[0]["out"].reshape(B, N, D)
```

```python
from contextlib import ExitStack, contextmanager

import numpy as np

import concourse.bass as bass
from concourse import mybir

F32, F16, I32 = mybir.dt.float32, mybir.dt.float16, mybir.dt.int32
ACT = mybir.ActivationFunctionType
ALU = mybir.AluOpType
AX = mybir.AxisListType

P = 128
B, N, D = 8, 256, 512
T = B * N
TT = T // P
KD = D // P
CH = 4 * P
NCH = T // CH
SSM_H, SSM_I = 32, 8
PAIRS = SSM_I * (SSM_I + 1) // 2
GH = 16
GROUPS = SSM_H // GH
LN_EPS = 1e-5


@contextmanager
def phase(nc):
    with nc.cleanup_on_exit(), ExitStack() as stack:
        yield stack


def opener(nc, stack):
    def sb(name, shape, dt=F32):
        return stack.enter_context(nc.sbuf_tensor(name, shape, dt))

    def ps(name, shape, dt=F32):
        return stack.enter_context(nc.psum_tensor(name, shape, dt))

    def sem(name):
        return nc.alloc_semaphore(name)
    return sb, ps, sem


def mixed(a, b):
    at = [((i + 0.5) / len(a), 0, o) for i, o in enumerate(a)] + [((i + 0.5) / len(b), 1, o) for i, o in enumerate(b)]
    return [o for _, _, o in sorted(at, key=lambda v: v[:2])]


def pair_at(i):
    return i * SSM_I - i * (i - 1) // 2


class LayerNorm:

    def __init__(self, sb, sem, name, tiles=4):
        self.tiles = tiles
        self.stats = sb(f"{name}_stats", [P, tiles, 6])
        self.mean, self.var = sb(f"{name}_mean", [P, tiles]), sb(f"{name}_var", [P, tiles])
        self.gap, self.spread = sb(f"{name}_gap", [P, tiles]), sb(f"{name}_spread", [P, tiles])
        self.std, self.rstd = sb(f"{name}_std", [P, tiles]), sb(f"{name}_rstd", [P, tiles])
        self.stats_done, self.parts_done = sem(f"{name}_stats_done"), sem(f"{name}_parts_done")
        self.gap_squared, self.var_done = sem(f"{name}_gap_squared"), sem(f"{name}_var_done")
        self.std_done, self.rstd_done = sem(f"{name}_std_done"), sem(f"{name}_rstd_done")

    def statistics(self, nc, dve, rows, c):
        for t in range(self.tiles):
            self.tile(nc, rows, t)
        self.finish(nc, dve, c)

    def tile(self, nc, rows, t):
        nc.vector.bn_stats(self.stats[:, t, :], rows[:, t, :]).then_inc(self.stats_done, 1)

    def finish(self, nc, dve, c):
        self.variance(nc, dve, c)
        self.inverse(nc, dve, c)

    def variance(self, nc, dve, c):
        even_mean, even_m2 = self.stats[:, :, 1], self.stats[:, :, 2]
        odd_mean, odd_m2 = self.stats[:, :, 4], self.stats[:, :, 5]
        dve.wait_ge(self.stats_done, (c + 1) * self.tiles)
        nc.vector.tensor_tensor(self.mean[:, :], even_mean, odd_mean, ALU.add).then_inc(self.parts_done, 1)
        nc.vector.tensor_tensor(self.gap[:, :], even_mean, odd_mean, ALU.subtract).then_inc(self.parts_done, 1)
        nc.vector.tensor_tensor(self.spread[:, :], even_m2, odd_m2, ALU.add).then_inc(self.parts_done, 1)
        dve.wait_ge(self.parts_done, (c + 1) * 3)
        nc.vector.tensor_scalar(self.mean[:, :], self.mean[:, :], 0.5, None, ALU.mult).then_inc(self.gap_squared, 1)
        nc.vector.scalar_tensor_tensor(self.gap[:, :], self.gap[:, :], 0.25, self.gap[:, :], ALU.mult, ALU.mult
                                       ).then_inc(self.gap_squared, 1)
        nc.vector.tensor_scalar(self.spread[:, :], self.spread[:, :], 1.0 / D, LN_EPS, ALU.mult, ALU.add
                                ).then_inc(self.gap_squared, 1)
        dve.wait_ge(self.gap_squared, (c + 1) * 3)
        nc.vector.tensor_tensor(self.var[:, :], self.gap[:, :], self.spread[:, :], ALU.add).then_inc(self.var_done, 1)

    def inverse(self, nc, dve, c):
        dve.wait_ge(self.std_done, c + 1)
        nc.vector.reciprocal(self.rstd[:, :], self.std[:, :]).then_inc(self.rstd_done, 1)
        dve.wait_ge(self.rstd_done, c + 1)

    def root(self, nc, act, c):
        act.wait_ge(self.var_done, c + 1)
        nc.scalar.activation(self.std[:, :], self.var[:, :], ACT.Sqrt).then_inc(self.std_done, 1)


def constants(nc, k, g_xattn, g_ffn):
    with phase(nc) as st:
        sb, ps, sem = opener(nc, st)
        ident_zeroed, ident_ready = sem("ident_zeroed"), sem("ident_ready")
        gates_loaded, gates_ready = sem("gates_loaded"), sem("gates_ready")
        block = st.enter_context(nc.Block())

        @block.sync
        def _(sp):
            sp.dma_start(k.gates[:, 0:2], g_xattn.partition_broadcast(P)).then_inc(gates_loaded, 16)
            sp.dma_start(k.gates[:, 2:4], g_ffn.partition_broadcast(P)).then_inc(gates_loaded, 16)

        @block.gpsimd
        def _(pool):
            nc.gpsimd.memset(k.ident[:, :], 0.0).then_inc(ident_zeroed, 1)
            pool.wait_ge(ident_zeroed, 1)
            nc.gpsimd.affine_select(out=k.ident[:, :], in_=k.ident[:, :], compare_op=ALU.not_equal, fill=1.0,
                                    base=0, pattern=[[-1, P]], channel_multiplier=1).then_inc(ident_ready, 1)

        @block.scalar
        def _(act):
            act.wait_ge(gates_loaded, 32)
            nc.scalar.activation(k.tanh_gates[:, :], k.gates[:, :], ACT.Tanh).then_inc(gates_ready, 1)


def conv_operands(nc, k, x, ctx, q_t, c_t):
    with phase(nc) as st:
        sb, ps, sem = opener(nc, st)
        x_in, c_in = sb("x_in", [P, 2, KD, D]), sb("c_in", [P, 2, KD, D])
        ln = LayerNorm(sb, sem, "x")
        tr = [ps(f"tr{n}", [P, D]) for n in range(8)]
        loaded = [sem(f"loaded{u}") for u in range(2)]
        normed = sem("normed")
        x_tr, c_tr = sem("x_tr"), sem("c_tr")
        x_out, c_out = sem("x_out"), sem("c_out")
        block = st.enter_context(nc.Block())
        x_d = x.rearrange("b (k p) d -> p (b k) d", p=P)
        c_d = ctx.rearrange("b (k p) d -> p (b k) d", p=P)

        @block.sync
        def _(sp):
            with sp.Fori(0, NCH // 2) as i:
                for u in range(2):
                    sp.wait_ge(x_out, i * 8 + 4 * (u + 1))
                    sp.dma_start(x_in[:, u], x_d[:, bass.ds(i * 8 + u * 4, 4), :]).then_inc(loaded[u], 16)
                    sp.dma_start(c_in[:, u], c_d[:, bass.ds(i * 8 + u * 4, 4), :]).then_inc(loaded[u], 16)

        @block.vector
        def _(dve):
            with dve.Fori(0, NCH // 2) as i:
                for u in range(2):
                    c = i * 2 + u
                    dve.wait_ge(loaded[u], (i + 1) * 32)
                    ln.statistics(nc, dve, x_in[:, u], c)
                    for t in range(4):
                        nc.vector.tensor_scalar(x_in[:, u, t, :], x_in[:, u, t, :], ln.mean[:, t:t + 1],
                                                ln.rstd[:, t:t + 1], ALU.subtract, ALU.mult).then_inc(normed, 1)
                    for t in range(4):
                        dve.wait_ge(x_tr, c * 4 + (t + 1))
                        dst = q_t[:, :, (t % 2) * 16:(t % 2) * 16 + 16, bass.ds(i * 4 + (2 * u + t // 2), 1), :]
                        nc.vector.tensor_copy(dst, tr[t][:, :].rearrange("p (k h o i) -> p k h o i", k=KD, o=1, i=SSM_I)
                                              ).then_inc(x_out, 1)

        @block.scalar
        def _(act):
            nc.scalar.preload_act_table(ACT.Sqrt)
            with act.Fori(0, NCH // 2) as i:
                for u in range(2):
                    c = i * 2 + u
                    ln.root(nc, act, c)
                    for t in range(4):
                        act.wait_ge(c_tr, c * 4 + (t + 1))
                        dst = c_t[:, :, (t % 2) * 16:(t % 2) * 16 + 16, bass.ds(i * 4 + (2 * u + t // 2), 1), :]
                        nc.scalar.activation(dst, tr[4 + t][:, :].rearrange("p (k h o i) -> p k h o i", k=KD, o=1, i=SSM_I),
                                             ACT.Copy).then_inc(c_out, 1)

        @block.tensor
        def _(pe):
            with pe.Fori(0, NCH // 2) as i:
                for u in range(2):
                    c = i * 2 + u
                    pe.wait_ge(loaded[u], (i + 1) * 32)
                    for t in range(4):
                        pe.wait_ge(c_out, c * 4 + (t + 1))
                        for b in range(KD):
                            last = nc.tensor.transpose(tr[4 + t][:, b * P:(b + 1) * P], c_in[:, u, t, b * P:(b + 1) * P], k.ident[:, :])
                        last.then_inc(c_tr, 1)
                    for t in range(4):
                        pe.wait_ge(normed, c * 4 + (t + 1))
                        pe.wait_ge(x_out, c * 4 + (t + 5))
                        for b in range(KD):
                            last = nc.tensor.transpose(tr[t][:, b * P:(b + 1) * P], x_in[:, u, t, b * P:(b + 1) * P], k.ident[:, :])
                        last.then_inc(x_tr, 1)

        @block.gpsimd
        def _(pool):
            nc.gpsimd.nop().then_inc(c_out, 4)
            nc.gpsimd.nop().then_inc(x_out, 8)



def conv_phase(nc, k, q_t, c_t, ssm_reversed, ssm_d, x, x1):
    assert GH * SSM_I == P
    STEPS = SSM_H // 2
    GSTEPS = GH // 2
    with phase(nc) as st:
        sb, ps, sem = opener(nc, st)
        d_all = sb("d_all", [P, SSM_H])
        toep = sb("toep", [P, 2, 2, D])
        toep_hi, toep_lo = sb("toep_hi", [P, 2, 2, D], F16), sb("toep_lo", [P, 2, 2, D], F16)
        prod = sb("prod", [P, KD, 2 * B, PAIRS])
        prod_hi = sb("prod_hi", [P, 2, KD, 2 * B, PAIRS], F16)
        prod_lo = sb("prod_lo", [P, 2, KD, 2 * B, PAIRS], F16)
        y = sb("y", [P, 2, KD, 2 * B, PAIRS])
        terms = sb("terms", [P, SSM_I, KD, 2 * B, SSM_I])
        sums = sb("sums", [P, 2, KD, B, GH, SSM_I])
        x_rows, gated = sb("x_rows", [P, B, D]), sb("gated", [P, B, D])
        conv = ps("conv", [P, 2, KD, D])
        d_loaded = sem("d_loaded")
        toep_loaded = [sem(f"toep_loaded{u}") for u in range(2)]
        toep_summed = sem("toep_summed")
        toep_hi_done, toep_lo_done = sem("toep_hi_done"), sem("toep_lo_done")
        prod_done, prod_hi_done, prod_lo_done = sem("prod_done"), sem("prod_hi_done"), sem("prod_lo_done")
        conv_done, conv_read = sem("conv_done"), sem("conv_read")
        weighed, half_sums, half_sums_pool, summed = sem("weighed"), sem("half_sums"), sem("half_sums_pool"), sem("summed")
        BY_DVE = 2
        flat = terms[:, :, :, :, :].rearrange("p i k b j -> p i (k b j)")
        sum_done, sum_read = sem("sum_done"), sem("sum_read")
        x_loaded, x_added, x_stored = sem("x_loaded"), sem("x_added"), sem("x_stored")
        block = st.enter_context(nc.Block())
        x_g = x.rearrange("b (g r) d -> g r b d", g=GROUPS)
        x1_g = x1.rearrange("b (g r) d -> g r b d", g=GROUPS)

        def toeplitz(s, u):
            return bass.AP(tensor=ssm_reversed.tensor, offset=s * (2 * (P + D)),
                           ap=[[1, P], [P + D, 2], [1, D]])

        @block.sync
        def _(sp):
            sp.dma_start(d_all[:, :], ssm_d.partition_broadcast(P)).then_inc(d_loaded, 16)

            def load_toeplitz(s):
                sp.wait_ge(toep_lo_done, s + 1)
                sp.dma_start(toep[:, s % 2], toeplitz(s, s % 2)).then_inc(toep_loaded[s % 2], 16)

            def store(g):
                for b in range(B):
                    sp.wait_ge(x_added, g * B + b + 1)
                    sp.dma_start(x1_g[g, :, b, :], gated[:, b, :]).then_inc(x_stored, 16)

            for g in range(GROUPS):
                for j in range(GSTEPS):
                    load_toeplitz(g * GSTEPS + j)
                    if j == 1 and not g:
                        sp.dma_start(x_rows[:, :, :], x_g[g]).then_inc(x_loaded, 16)
                if g:
                    store(g - 1)
                    sp.dma_start(x_rows[:, :, :], x_g[g]).then_inc(x_loaded, 16)
            store(GROUPS - 1)
            sp.wait_ge(x_stored, GROUPS * B * 16)

        @block.vector
        def _(dve):
            dve.wait_ge(d_loaded, 16)

            def make_products(g, j):
                s, u = g * GSTEPS + j, j % 2
                dve.wait_ge(toep_loaded[u], g * (GSTEPS * 8) + (j // 2 + 1) * 16)
                for e in range(2):
                    nc.vector.scalar_tensor_tensor(toep[:, u, e, D - P:D], k.ident[:, ::-1], d_all[:, bass.ds(s * 2 + e, 1)],
                                                   toep[:, u, e, D - P:D], ALU.mult, ALU.add).then_inc(toep_summed, 1)
                dve.wait_ge(prod_hi_done, s + 1)
                dve.wait_ge(prod_lo_done, s + 1)
                ch = c_t[:, :, bass.ds(s * 2, 2), :, :].rearrange("p k h b i -> p k (h b) i")
                for i in range(SSM_I):
                    n = SSM_I - i
                    nc.vector.tensor_tensor(prod[:, :, :, pair_at(i):pair_at(i) + n],
                                            ch[:, :, :, i:i + 1].to_broadcast([P, KD, 2 * B, n]),
                                            ch[:, :, :, i:SSM_I], ALU.mult).then_inc(prod_done, 1)

            def weigh(g, j):
                s = g * GSTEPS + j
                dve.wait_ge(conv_read, s * 2 + 6)
                dve.wait_ge(summed, s * 2 + 2)
                q = q_t[:, :, bass.ds(s * 2, 2), :, :].rearrange("p k h b i -> p k (h b) i")
                for i in range(SSM_I):
                    n = SSM_I - i
                    last = nc.vector.tensor_tensor(terms[:, i, :, :, i:SSM_I], y[:, j % 2, :, :, pair_at(i):pair_at(i) + n],
                                                   q[:, :, :, i:i + 1].to_broadcast([P, KD, 2 * B, n]), ALU.mult)
                    if i < SSM_I - 1:
                        dst = terms[:, i + 1:SSM_I, :, :, i].rearrange("p i k b -> p k b i")
                        last = nc.vector.tensor_tensor(dst, y[:, j % 2, :, :, pair_at(i) + 1:pair_at(i) + n],
                                                       q[:, :, :, i + 1:SSM_I], ALU.mult)
                last.then_inc(weighed, 1)
                dve.wait_ge(weighed, s + 3)
                nc.vector.tensor_tensor(flat[:, 0:BY_DVE], flat[:, 0:BY_DVE], flat[:, 4:4 + BY_DVE], ALU.add).then_inc(half_sums, 1)

            def sum_up(g, j):
                s = g * GSTEPS + j
                dve.wait_ge(half_sums, s + 1)
                dve.wait_ge(half_sums_pool, s + 1)
                for e in range(2):
                    dst = sums[:, :, :, :, 2 * j + e].rearrange("p i k b j -> p (i k) b j")
                    src = terms[:, :, :, e * B:(e + 1) * B, :].rearrange("p i k b j -> p (i k) b j")
                    nc.vector.tensor_tensor(dst, src[:, 0:2 * KD], src[:, 2 * KD:4 * KD], ALU.add).then_inc(summed, 1)

            for g in range(GROUPS):
                make_products(g, 0)
                make_products(g, 1)
                if g:
                    dve.wait_ge(sum_done, (g + 1) * B)
                for j in range(GSTEPS):
                    if j + 2 < GSTEPS:
                        make_products(g, j + 2)
                    if j:
                        sum_up(g, j - 1)
                    weigh(g, j)
                sum_up(g, GSTEPS - 1)

        @block.scalar
        def _(act):
            nc.scalar.preload_act_table(ACT.Copy)
            nc.scalar.nop().then_inc(prod_hi_done, 1)
            nc.scalar.nop().then_inc(sum_read, B)
            nc.scalar.nop().then_inc(conv_read, 4)

            def copy_out(g, j):
                s = g * GSTEPS + j
                act.wait_ge(weighed, s + 1)
                for e in range(2):
                    act.wait_ge(conv_done, s * 2 + (e + 1))
                    nc.scalar.activation(y[:, j % 2, :, e * B:(e + 1) * B, :].rearrange("p k b r -> p k (b r)"),
                                         conv[:, e, :, 0:B * PAIRS], ACT.Copy).then_inc(conv_read, 1)

            def split(s):
                u = s % 2
                act.wait_ge(toep_summed, (s + 1) * 2)
                if s >= 2:
                    act.wait_ge(conv_done, (s - 1) * 2)
                nc.scalar.activation(toep_hi[:, u], toep[:, u, :, ::-1], ACT.Copy).then_inc(toep_hi_done, 1)
                act.wait_ge(prod_done, (s + 1) * SSM_I)
                nc.scalar.activation(prod_hi[:, u].rearrange("p k b r -> p (k b r)"),
                                     prod[:, :, :, :].rearrange("p k b r -> p (k b r)"), ACT.Copy).then_inc(prod_hi_done, 1)

            def read_sums(g, first, end):
                for b in range(first, end):
                    act.wait_ge(sum_done, (g + 1) * B + (b + 1))
                    nc.scalar.activation(gated[:, b, :], conv[:, b // KD, b % KD, :], ACT.Copy,
                                         scale=k.tanh_gates[:, 0:1]).then_inc(sum_read, 1)

            for g in range(GROUPS):
                if g:
                    read_sums(g - 1, 0, B // 2)
                split(g * GSTEPS)
                if g:
                    read_sums(g - 1, B // 2, B)
                split(g * GSTEPS + 1)
                for j in range(GSTEPS):
                    copy_out(g, j)
                    if j + 2 < GSTEPS:
                        split(g * GSTEPS + j + 2)
                if g:
                    act.wait_ge(x_stored, g * B * 16)
            read_sums(GROUPS - 1, 0, B)

        @block.gpsimd
        def _(pool):
            nc.gpsimd.nop().then_inc(toep_lo_done, 2)
            nc.gpsimd.nop().then_inc(prod_lo_done, 1)
            nc.gpsimd.nop().then_inc(weighed, 2)
            nc.gpsimd.nop().then_inc(summed, 2)
            nc.gpsimd.nop().then_inc(sum_done, B)

            def rest(s):
                u = s % 2
                pool.wait_ge(toep_hi_done, s + 1)
                if s >= 2:
                    pool.wait_ge(conv_read, s * 2)
                nc.gpsimd.tensor_tensor(toep_lo[:, u], toep[:, u, :, ::-1], toep_hi[:, u], ALU.subtract).then_inc(toep_lo_done, 1)
                pool.wait_ge(prod_hi_done, s + 2)
                nc.gpsimd.tensor_tensor(prod_lo[:, u].rearrange("p k b r -> p (k b r)"),
                                        prod[:, :, :, :].rearrange("p k b r -> p (k b r)"),
                                        prod_hi[:, u].rearrange("p k b r -> p (k b r)"), ALU.subtract).then_inc(prod_lo_done, 1)

            def half_sum(s):
                pool.wait_ge(weighed, s + 3)
                nc.gpsimd.tensor_tensor(flat[:, BY_DVE:4], flat[:, BY_DVE:4], flat[:, 4 + BY_DVE:8], ALU.add).then_inc(half_sums_pool, 1)

            def add_rows(g, b):
                pool.wait_ge(x_loaded, (g + 1) * 16)
                pool.wait_ge(sum_read, (g + 1) * B + b + 1)
                nc.gpsimd.tensor_tensor(gated[:, b, :], gated[:, b, :], x_rows[:, b, :], ALU.add).then_inc(x_added, 1)

            for g in range(GROUPS):
                rest(g * GSTEPS)
                rest(g * GSTEPS + 1)
                for j in range(GSTEPS):
                    if j + 2 < GSTEPS:
                        rest(g * GSTEPS + j + 2)
                    half_sum(g * GSTEPS + j)
                    if g and j < B:
                        add_rows(g - 1, j)
            for b in range(B):
                add_rows(GROUPS - 1, b)

        @block.tensor
        def _(pe):
            for g in range(GROUPS):
                for j in range(GSTEPS):
                    s, u = g * GSTEPS + j, j % 2
                    pe.wait_ge(toep_lo_done, s + 3)
                    pe.wait_ge(prod_lo_done, s + 2)
                    if j == 0:
                        pe.wait_ge(sum_read, (g + 1) * B)
                    for e in range(2):
                        pe.wait_ge(conv_read, s * 2 + (e + 3))
                        for m in range(KD):
                            out = conv[:, e, m, 0:B * PAIRS]
                            for n in range(m + 1):
                                t = slice((m - n) * P, (m - n + 1) * P)
                                hi = prod_hi[:, u, n, e * B:(e + 1) * B, :]
                                lo = prod_lo[:, u, n, e * B:(e + 1) * B, :]
                                nc.tensor.matmul(out, toep_hi[:, u, e, t], hi, start=(n == 0), stop=False)
                                nc.tensor.matmul(out, toep_hi[:, u, e, t], lo, start=False, stop=False)
                                last = nc.tensor.matmul(out, toep_lo[:, u, e, t], hi, start=False, stop=(n == m))
                        last.then_inc(conv_done, 1)
                pe.wait_ge(conv_read, (g + 1) * GH + 4)
                pe.wait_ge(summed, (g + 1) * GH + 2)
                for b in range(B):
                    for m in range(KD):
                        out = conv[:, b // KD, b % KD, m * P:(m + 1) * P]
                        for i in range(2):
                            last = nc.tensor.matmul(out, sums[:, i, m, b].rearrange("p h j -> p (h j)"), k.ident[:, :],
                                                    is_transpose=True, start=(i == 0), stop=(i == 1))
                    last.then_inc(sum_done, 1)


E, I_MOE = 8, 352
I_SH = 704
MK = -(-I_MOE // P)
SK = -(-I_SH // P)
TILES = (2 * T + E * (P - 1)) // P
SLOTS = TILES * P


def rows_of(width, m):
    return min(P, width - m * P)


def shared_phase(nc, k, w, x1, xn_out, x1s, router_t, gate, up, s_gate, s_gate_b, s_up, s_up_b, s_down, s_down_b):
    with phase(nc) as st:
        sb, ps, sem = opener(nc, st)
        ln = LayerNorm(sb, sem, "x1")
        x_in = sb("x1_in", [P, 2, 4, D])
        xn = sb("xn", [P, 4, D])
        xt_hi, xt_lo = sb("xt_hi", [P, KD, CH], F16), sb("xt_lo", [P, KD, CH], F16)
        sg_hi, sg_lo = sb("sg_hi", [P, KD, I_SH], F16), sb("sg_lo", [P, KD, I_SH], F16)
        su_hi, su_lo = sb("su_hi", [P, KD, I_SH], F16), sb("su_lo", [P, KD, I_SH], F16)
        sd_hi, sd_lo = sb("sd_hi", [P, SK, D], F16), sb("sd_lo", [P, SK, D], F16)
        rw, rw_hi, rw_lo = sb("rw", [P, KD, E]), sb("rw_hi", [P, KD, E], F16), sb("rw_lo", [P, KD, E], F16)
        bg, bu, bd = sb("bg", [P, SK]), sb("bu", [P, SK]), sb("bd", [P, D])
        stage = sb("stage", [P, 2, KD * I_MOE])
        silu, h = sb("silu", [P, 2, CH]), sb("h", [P, 2, CH])
        h_hi, h_lo = sb("h_hi", [P, SK, CH], F16), sb("h_lo", [P, SK, CH], F16)
        summed = sb("ffn_sum", [P, D])
        tr = ps("tr", [P, KD, CH])
        gu = ps("gu", [P, 2, 2, CH])

        small_loaded = sem("small_loaded")
        stage_loaded = [sem(f"stage_loaded{u}") for u in range(2)]
        x_loaded = [sem(f"x1_loaded{u}") for u in range(2)]
        sw_hi, sw_lo = sem("sw_hi"), sem("sw_lo")
        ew_hi, ew_lo = sem("ew_hi"), sem("ew_lo")
        normed, xn_stored, turned = sem("xn_normed"), sem("xn_stored"), sem("turned")
        xt_hi_done, xt_lo_done = sem("xt_hi_done"), sem("xt_lo_done")
        routed, logits_read = sem("routed"), sem("logits_read")
        gu_done, silu_done, h_done = sem("gu_done"), sem("silu_done"), sem("h_done")
        h_hi_done, h_lo_done = sem("h_hi_done"), sem("h_lo_done")
        down_done, bias_added, out_done, out_stored = sem("down_done"), sem("bias_added"), sem("out_done"), sem("out_stored")
        block = st.enter_context(nc.Block())
        x1_d, x1s_d, xn_d = (a.rearrange("(c k p) d -> p (c k) d", p=P, k=4) for a in (x1, x1s, xn_out))

        pieces = []
        for hi, lo, m in ((sg_hi, sg_lo, s_gate), (su_hi, su_lo, s_up)):
            for b in range(0, KD, 2):
                pieces.append((hi[:, b:b + 2, :], lo[:, b:b + 2, :], m[b * P:(b + 2) * P, :].rearrange("(k p) n -> p k n", p=P), P))
        whole = I_SH // P
        for b in range(0, whole, 2):
            e = min(b + 2, whole)
            pieces.append((sd_hi[:, b:e, :], sd_lo[:, b:e, :], s_down[b * P:e * P, :].rearrange("(k p) n -> p k n", p=P), P))
        rest = I_SH - whole * P
        pieces.append((sd_hi[0:rest, whole:SK, :], sd_lo[0:rest, whole:SK, :],
                       s_down[whole * P:I_SH, :].rearrange("(k p) n -> p k n", k=1), rest))
        NP = len(pieces)
        assert NP % 2 == 0

        def staged(piece, u):
            hi, _, _, rows = piece
            k_, n = hi.shape[1], hi.shape[2]
            return stage[0:rows, u, 0:k_ * n].rearrange("p (k n) -> p k n", n=n)

        @block.sync
        def _(sp):
            def load_x(c, u):
                sp.wait_ge(out_stored, c * 16 + 16)
                sp.dma_start(x_in[:, u], x1_d[:, bass.ds(c * 4, 4), :]).then_inc(x_loaded[u], 16)

            load_x(0, 0)
            sp.dma_start(rw[:, :, :], router_t.rearrange("(k p) e -> p k e", p=P)).then_inc(small_loaded, 16)
            sp.dma_start(bd[:, :], s_down_b.partition_broadcast(P)).then_inc(small_loaded, 16)
            for dst, b in ((bg, s_gate_b), (bu, s_up_b)):
                sp.dma_start(dst[:, :], b).then_inc(small_loaded, 16)
            for n, piece in enumerate(pieces):
                if n >= 2:
                    sp.wait_ge(sw_lo, n + 1)
                sp.dma_start(staged(piece, n % 2), piece[2]).then_inc(stage_loaded[n % 2], 16)
            sp.wait_ge(sw_lo, NP + 2)

            def chunk(c, u, last):
                if not last:
                    load_x(c + 1, 1 - u)
                sp.wait_ge(normed, (c + 1) * 4)
                sp.dma_start(xn_d[:, bass.ds(c * 4, 4), :], xn[:, :, :]).then_inc(xn_stored, 16)
                for q in range(4):
                    sp.wait_ge(ew_lo, c * 4 + (q + 1))
                    src = (gate, up)[q % 2][bass.ds(c * 2 + q // 2, 1), :, :].rearrange("o (k p) i -> p (o k) i", p=P)
                    sp.dma_start(stage[:, q % 2, :].rearrange("p (k i) -> p k i", k=KD), src).then_inc(stage_loaded[q % 2], 16)
                sp.wait_ge(out_done, (c + 2) * 4)
                sp.dma_start(x1s_d[:, bass.ds(c * 4, 4), :], x_in[:, u]).then_inc(out_stored, 16)

            for c in range(NCH):
                chunk(c, c % 2, c == NCH - 1)
            sp.wait_ge(out_stored, (NCH + 2) * 16)
            sp.wait_ge(xn_stored, (NCH + 1) * 16)

        @block.scalar
        def _(act):
            nc.scalar.nop().then_inc(xn_stored, 16)
            ln.root(nc, act, 0)

            def split_turned(c):
                for b in range(KD):
                    act.wait_ge(turned, c * KD + (b + 1))
                    nc.scalar.activation(xt_hi[:, b, :], tr[:, b, :], ACT.Copy).then_inc(xt_hi_done, 1)

            split_turned(0)
            for n, piece in enumerate(pieces):
                act.wait_ge(stage_loaded[n % 2], (n // 2 + 1) * 16)
                nc.scalar.activation(piece[0], staged(piece, n % 2), ACT.Copy).then_inc(sw_hi, 1)

            def chunk(c, last):
                if c:
                    split_turned(c)
                for m in range(SK):
                    r, u = rows_of(I_SH, m), m % 2
                    act.wait_ge(gu_done, c * SK + (m + 1))
                    act.wait_ge(h_done, c * SK + (m + 1))
                    nc.scalar.activation(silu[0:r, u, :], gu[0:r, u, 0, :], ACT.Silu, bias=bg[0:r, m:m + 1]).then_inc(silu_done, 1)
                    if m < 4:
                        split_expert(c, m)
                    act.wait_ge(h_done, c * SK + (m + 3))
                    nc.scalar.activation(h_hi[0:r, m, :], h[0:r, u, :], ACT.Copy).then_inc(h_hi_done, 1)
                if not last:
                    ln.root(nc, act, c + 1)

            def split_expert(c, q):
                act.wait_ge(stage_loaded[q % 2], c * 32 + (NP // 2 + q // 2 + 1) * 16)
                dst = (w.gate_hi, w.up_hi)[q % 2][:, bass.ds(c * 2 + q // 2, 1), :, :].rearrange("p o k i -> p (o k i)")
                nc.scalar.activation(dst, stage[:, q % 2, :], ACT.Copy).then_inc(ew_hi, 1)

            for c in range(NCH):
                chunk(c, c == NCH - 1)

        @block.gpsimd
        def _(pool):
            nc.gpsimd.nop().then_inc(out_stored, 32)
            nc.gpsimd.nop().then_inc(ew_lo, 2)
            nc.gpsimd.nop().then_inc(h_done, 2)
            nc.gpsimd.nop().then_inc(logits_read, 1)
            nc.gpsimd.nop().then_inc(out_done, 4)

            def chunk(c):
                for m in range(SK):
                    r, u = rows_of(I_SH, m), m % 2
                    pool.wait_ge(h_hi_done, c * SK + (m + 1))
                    nc.gpsimd.tensor_tensor(h_lo[0:r, m, :], h[0:r, u, :], h_hi[0:r, m, :], ALU.subtract).then_inc(h_lo_done, 1)
                    if m < 4:
                        q = m
                        pool.wait_ge(ew_hi, c * 4 + (q + 1))
                        hi, lo = ((w.gate_hi, w.gate_lo), (w.up_hi, w.up_lo))[q % 2]
                        hi, lo = (a[:, bass.ds(c * 2 + q // 2, 1), :, :].rearrange("p o k i -> p (o k i)") for a in (hi, lo))
                        nc.gpsimd.tensor_tensor(lo, stage[:, q % 2, :], hi, ALU.subtract).then_inc(ew_lo, 1)

            for c in range(NCH):
                chunk(c)

        @block.vector
        def _(dve):
            def normalise(c, u):
                dve.wait_ge(x_loaded[u], (c // 2 + 1) * 16)
                ln.statistics(nc, dve, x_in[:, u], c)
                dve.wait_ge(xn_stored, (c + 1) * 16)
                for t in range(4):
                    nc.vector.tensor_scalar(xn[:, t, :], x_in[:, u, t, :], ln.mean[:, t:t + 1], ln.rstd[:, t:t + 1],
                                            ALU.subtract, ALU.mult).then_inc(normed, 1)

            normalise(0, 0)
            dve.wait_ge(small_loaded, 16 * 4)
            nc.vector.tensor_copy(rw_hi[:, :, :], rw[:, :, :]).then_inc(sw_lo, 1)
            dve.wait_ge(sw_lo, 1)
            nc.vector.tensor_tensor(rw_lo[:, :, :], rw[:, :, :], rw_hi[:, :, :], ALU.subtract).then_inc(sw_lo, 1)

            def rest_of_turned(c):
                for b in range(KD):
                    dve.wait_ge(xt_hi_done, c * KD + (b + 1))
                    nc.vector.tensor_tensor(xt_lo[:, b, :], tr[:, b, :], xt_hi[:, b, :], ALU.subtract).then_inc(xt_lo_done, 1)

            rest_of_turned(0)
            for n, piece in enumerate(pieces):
                dve.wait_ge(sw_hi, n + 1)
                nc.vector.tensor_tensor(piece[1], staged(piece, n % 2), piece[0], ALU.subtract).then_inc(sw_lo, 1)

            def chunk(c, u, last):
                if c:
                    rest_of_turned(c)
                dve.wait_ge(routed, c + 1)
                nc.vector.tensor_copy(k.logits[:, bass.ds(c * 4, 4), :], tr[:, 0, 0:4 * E].rearrange("p (t e) -> p t e", e=E)
                                      ).then_inc(logits_read, 1)
                for m in range(SK):
                    r, v = rows_of(I_SH, m), m % 2
                    dve.wait_ge(silu_done, c * SK + (m + 1))
                    if not (isinstance(c, int) and c == 0 and m < 2):
                        dve.wait_ge(h_lo_done, c * SK + (m - 1))
                    nc.vector.scalar_tensor_tensor(h[0:r, v, :], gu[0:r, v, 1, :], bu[0:r, m:m + 1], silu[0:r, v, :],
                                                   ALU.add, ALU.mult).then_inc(h_done, 1)
                if not last:
                    normalise(c + 1, 1 - u)
                for t in range(4):
                    dve.wait_ge(down_done, c * 4 + (t + 1))
                    dve.wait_ge(out_done, c * 4 + (t + 4))
                    nc.vector.tensor_tensor(summed[:, :], tr[:, t, :], bd[:, :], ALU.add).then_inc(bias_added, 1)
                    dve.wait_ge(bias_added, c * 4 + (t + 1))
                    nc.vector.scalar_tensor_tensor(x_in[:, u, t, :], summed[:, :], k.tanh_gates[:, 2:3], x_in[:, u, t, :],
                                                   ALU.mult, ALU.add).then_inc(out_done, 1)

            for c in range(NCH):
                chunk(c, c % 2, c == NCH - 1)

        @block.tensor
        def _(pe):
            def chunk(c, u):
                for b in range(KD):
                    for t in range(4):
                        if b == 0:
                            pe.wait_ge(normed, c * 4 + (t + 1))
                        if t == 0:
                            if not (isinstance(c, int) and c == 0):
                                pe.wait_ge(bias_added, (c - 1) * 4 + (b + 1))
                        last = nc.tensor.transpose(tr[:, b, t * P:(t + 1) * P], xn[:, t, b * P:(b + 1) * P], k.ident[:, :])
                    last.then_inc(turned, 1)
                for m in range(SK):
                    r, v = rows_of(I_SH, m), m % 2
                    cols = slice(m * P, m * P + r)
                    pe.wait_ge(h_done, c * SK + (m + 1))
                    for o, (hi, lo) in enumerate(((sg_hi, sg_lo), (su_hi, su_lo))):
                        if isinstance(c, int) and c == 0 and m == 0:
                            pe.wait_ge(sw_lo, 2 + (o + 1) * (KD // 2))
                        for b in range(KD):
                            if m == 0 and o == 0:
                                pe.wait_ge(xt_lo_done, c * KD + (b + 1))
                            nc.tensor.matmul(gu[0:r, v, o, :], hi[:, b, cols], xt_hi[:, b, :], start=(b == 0), stop=False)
                            nc.tensor.matmul(gu[0:r, v, o, :], hi[:, b, cols], xt_lo[:, b, :], start=False, stop=False)
                            last = nc.tensor.matmul(gu[0:r, v, o, :], lo[:, b, cols], xt_hi[:, b, :], start=False, stop=(b == KD - 1))
                    last.then_inc(gu_done, 1)
                    if m == 0:
                        for t in range(4):
                            tok = slice(t * P, (t + 1) * P)
                            for b in range(KD):
                                for n, (x_, r_) in enumerate(((xt_hi, rw_hi), (xt_hi, rw_lo), (xt_lo, rw_hi))):
                                    last = nc.tensor.matmul(tr[:, 0, t * E:(t + 1) * E], x_[:, b, tok], r_[:, b, :],
                                                            start=(b == 0 and n == 0), stop=(b == KD - 1 and n == 2))
                        last.then_inc(routed, 1)
                pe.wait_ge(logits_read, c + 2)
                if isinstance(c, int) and c == 0:
                    pe.wait_ge(sw_lo, NP + 2)
                for t in range(4):
                    tok = slice(t * P, (t + 1) * P)
                    for m in range(SK):
                        r = rows_of(I_SH, m)
                        if t == 0:
                            pe.wait_ge(h_lo_done, c * SK + (m + 1))
                        nc.tensor.matmul(tr[:, t, :], h_hi[0:r, m, tok], sd_hi[0:r, m, :], start=(m == 0), stop=False)
                        nc.tensor.matmul(tr[:, t, :], h_hi[0:r, m, tok], sd_lo[0:r, m, :], start=False, stop=False)
                        last = nc.tensor.matmul(tr[:, t, :], h_lo[0:r, m, tok], sd_hi[0:r, m, :], start=False, stop=(m == SK - 1))
                    last.then_inc(down_done, 1)

            for c in range(NCH):
                chunk(c, c % 2)



def route_phase(nc, k, w, down):
    C = 2 * TT
    with phase(nc) as st:
        sb, ps, sem = opener(nc, st)
        small = [P, TT, E]
        first_i, steps_i, tiles_i = sb("first_i", [P, E], I32), sb("steps_i", [P, TT], I32), sb("tiles_i", [P, TILES], I32)
        first, steps, tiles_f = sb("first", [P, E]), sb("steps", [P, TT]), sb("tiles_f", [P, TILES])
        token_i, edges_i, row_i = sb("token_i", [P, TT], I32), sb("edges_i", [P, TILES + 1], I32), sb("row_i", [P, P], I32)
        token, edges, row = sb("token", [P, TT]), sb("edges", [P, TILES + 1]), sb("row", [P, P])
        behind, in_tile = sb("behind", [P, C, TILES + 1], F16), sb("in_tile", [P, C, TILES], F16)
        behind_count, in_place = sb("behind_count", [P, C]), sb("in_place", [P, C])
        token_at = sb("token_at", [P, C, P], F16)
        before, ones = sb("before", [P, P], F16), sb("ones", [P, P], F16)
        best = [sb(f"best{n}", [P, TT]) for n in range(2)]
        tie = [sb(f"tie{n}", small) for n in range(2)]
        tie_best = [sb(f"tie_best{n}", [P, TT]) for n in range(2)]
        pick = [sb(f"pick{n}", small) for n in range(2)]
        rest = sb("rest", small)
        picked = sb("picked", [P, 2 * TT, E], F16)
        gap, e2, den = sb("r_gap", [P, TT]), sb("r_e2", [P, TT]), sb("r_den", [P, TT])
        over, tiles_of, tiles_to = sb("over", [P, E, TT]), sb("tiles_of", [P, E]), sb("tiles_to", [P, E])
        one8, start = sb("one8", [P, E]), sb("start", [P, E])
        place, placed = sb("place", small), [sb(f"placed{n}", small) for n in range(2)]
        slot_f = sb("slot_f", [P, 2, TT])
        past, texp_f = sb("past", [P, TILES, E]), sb("texp_f", [P, TILES])
        DOWN_BUFS, BY_POOL = 4, 6
        stage = sb("d_stage", [P, DOWN_BUFS, MK, D])
        rank, total, listing = ps("rank", [P, TT * E]), ps("total", [P, E]), ps("listing", [P, TILES])
        consts_made, before_zeroed = sem("consts_made"), sem("before_zeroed")
        chain = sem("route_chain")
        e2_done, picked_done, ranked = sem("e2_done"), sem("picked_done"), sem("ranked")
        gap_done, tokens_at, listed = sem("gap_done"), sem("tokens_at"), sem("listed")
        stage_loaded = [sem(f"d_stage_loaded{u}") for u in range(DOWN_BUFS)]
        d_hi, d_lo = sem("d_hi"), sem("d_lo")
        block = st.enter_context(nc.Block())
        whole = I_MOE // P
        tail = I_MOE - whole * P

        @block.sync
        def _(sp):
            for e in range(E):
                if e >= DOWN_BUFS:
                    sp.wait_ge(d_lo, 2 * (e - DOWN_BUFS + 1))
                u = e % DOWN_BUFS
                sp.dma_start(stage[:, u, 0:whole, :], down[e, 0:whole * P, :].rearrange("(k p) n -> p k n", p=P)).then_inc(stage_loaded[u], 16)
                sp.dma_start(stage[0:tail, u, whole, :], down[e, whole * P:I_MOE, :]).then_inc(stage_loaded[u], 16)
        @block.gpsimd
        def _(pool):
            nc.gpsimd.memset(before[:, :], 1.0).then_inc(before_zeroed, 1)
            nc.gpsimd.memset(ones[:, :], 1.0)
            nc.gpsimd.memset(picked[:, 0:TT, :], 0.0)
            nc.gpsimd.memset(one8[:, :], 1.0)
            nc.gpsimd.iota(first_i[:, :], pattern=[[-1, E]], base=E, channel_multiplier=0)
            nc.gpsimd.iota(steps_i[:, :], pattern=[[P, TT]], base=0, channel_multiplier=0)
            nc.gpsimd.iota(tiles_i[:, :], pattern=[[1, TILES]], base=0, channel_multiplier=0)
            nc.gpsimd.iota(token_i[:, :], pattern=[[P, TT]], base=0, channel_multiplier=1)
            nc.gpsimd.iota(edges_i[:, :], pattern=[[P, TILES + 1]], base=0, channel_multiplier=0)
            nc.gpsimd.iota(row_i[:, :], pattern=[[1, P]], base=-P, channel_multiplier=0)
            pool.wait_ge(before_zeroed, 1)
            nc.gpsimd.affine_select(out=before[:, :], in_=before[:, :], compare_op=ALU.is_gt, fill=0.0,
                                    base=0, pattern=[[1, P]], channel_multiplier=-1).then_inc(consts_made, 1)
            for e in range(BY_POOL):
                pool.wait_ge(d_hi, 2 * e + 2)
                nc.gpsimd.tensor_tensor(w.down_lo[:, e, 0:whole, :], stage[:, e % DOWN_BUFS, 0:whole, :], w.down_hi[:, e, 0:whole, :], ALU.subtract).then_inc(d_lo, 1)
                nc.gpsimd.tensor_tensor(w.down_lo[0:tail, e, whole, :], stage[0:tail, e % DOWN_BUFS, whole, :], w.down_hi[0:tail, e, whole, :],
                                        ALU.subtract).then_inc(d_lo, 1)

        @block.scalar
        def _(act):
            nc.scalar.preload_act_table(ACT.Exp)
            act.wait_ge(gap_done, 1)
            nc.scalar.activation(e2[:, :], gap[:, :], ACT.Exp).then_inc(e2_done, 1)
            for e in range(E):
                act.wait_ge(stage_loaded[e % DOWN_BUFS], (e // DOWN_BUFS + 1) * 32)
                nc.scalar.activation(w.down_hi[:, e, 0:whole, :], stage[:, e % DOWN_BUFS, 0:whole, :], ACT.Copy).then_inc(d_hi, 1)
                nc.scalar.activation(w.down_hi[0:tail, e, whole, :], stage[0:tail, e % DOWN_BUFS, whole, :], ACT.Copy).then_inc(d_hi, 1)

        @block.tensor
        def _(pe):
            pe.wait_ge(picked_done, 1)
            nc.tensor.matmul(rank[:, :], before[:, :], picked[:, TT:2 * TT, :], start=True, stop=False)
            for s in range(1, TT):
                nc.tensor.matmul(rank[:, :], ones[:, :], picked[:, TT - s:2 * TT - s, :], start=False, stop=(s == TT - 1))
            for t in range(TT):
                last = nc.tensor.matmul(total[:, :], ones[:, :], picked[:, TT + t, :], start=(t == 0), stop=(t == TT - 1))
            last.then_inc(ranked, 1)
            for c in range(C):
                pe.wait_ge(tokens_at, c + 1)
                last = nc.tensor.matmul(listing[:, :], token_at[:, c, :], in_tile[:, c, :], start=(c == 0), stop=(c == C - 1))
            last.then_inc(listed, 1)

        @block.vector
        def _(dve):
            done = [0]

            def then(*made):
                for m in made:
                    m.then_inc(chain, 1)
                done[0] += len(made)
                dve.wait_ge(chain, done[0])

            V = nc.vector
            over_e = lambda a: a[:, :].unsqueeze(2).to_broadcast([P, TT, E])
            dve.wait_ge(consts_made, 1)
            then(V.tensor_copy(first[:, :], first_i[:, :]), V.tensor_copy(steps[:, :], steps_i[:, :]),
                 V.tensor_copy(tiles_f[:, :], tiles_i[:, :]), V.tensor_copy(token[:, :], token_i[:, :]),
                 V.tensor_copy(edges[:, :], edges_i[:, :]), V.tensor_copy(row[:, :], row_i[:, :]))
            scores = k.logits
            for n in range(2):
                then(V.tensor_reduce(best[n][:, :], scores[:, :, :], AX.X, ALU.max))
                then(V.tensor_tensor(tie[n][:, :, :], scores[:, :, :], over_e(best[n]), ALU.is_equal))
                then(V.tensor_tensor(tie[n][:, :, :], tie[n][:, :, :], first[:, :].unsqueeze(1).to_broadcast(small), ALU.mult))
                then(V.tensor_reduce(tie_best[n][:, :], tie[n][:, :, :], AX.X, ALU.max))
                then(V.tensor_tensor(pick[n][:, :, :], tie[n][:, :, :], over_e(tie_best[n]), ALU.is_equal))
                if n == 0:
                    then(V.scalar_tensor_tensor(rest[:, :, :].rearrange("p t e -> p (t e)"), pick[0][:, :, :].rearrange("p t e -> p (t e)"),
                                                -3e38, scores[:, :, :].rearrange("p t e -> p (t e)"), ALU.mult, ALU.add))
                    scores = rest
            V.tensor_tensor(picked[:, TT:2 * TT, :], pick[0][:, :, :], pick[1][:, :, :], ALU.add).then_inc(picked_done, 1)
            V.tensor_tensor(gap[:, :], best[1][:, :], best[0][:, :], ALU.subtract).then_inc(gap_done, 1)
            dve.wait_ge(e2_done, 1)
            then(V.tensor_scalar(den[:, :], e2[:, :], 1.0, None, ALU.add))
            then(V.reciprocal(den[:, :], den[:, :]))
            then(V.tensor_scalar(k.mix[:, 0, :], den[:, :], k.tanh_gates[:, 2:3], None, ALU.mult))
            then(V.tensor_tensor(k.mix[:, 1, :], k.mix[:, 0, :], e2[:, :], ALU.mult))
            dve.wait_ge(ranked, 1)
            then(V.tensor_tensor(over[:, :, :], total[:, :].unsqueeze(2).to_broadcast([P, E, TT]),
                                 steps[:, :].unsqueeze(1).to_broadcast([P, E, TT]), ALU.is_gt))
            then(V.tensor_reduce(tiles_of[:, :], over[:, :, :], AX.X, ALU.add))
            then(V.tensor_tensor_scan(tiles_to[:, :], one8[:, :], tiles_of[:, :], 0.0, ALU.mult, ALU.add))
            then(V.tensor_tensor(start[:, :], tiles_to[:, :], tiles_of[:, :], ALU.subtract),
                 V.tensor_tensor(past[:, :, :], tiles_to[:, :].unsqueeze(1).to_broadcast([P, TILES, E]),
                                 tiles_f[:, :].unsqueeze(2).to_broadcast([P, TILES, E]), ALU.is_le))
            then(V.tensor_scalar(start[:, :], start[:, :], float(P), None, ALU.mult),
                 V.tensor_reduce(texp_f[:, :], past[:, :, :], AX.X, ALU.add))
            then(V.tensor_tensor(place[:, :, :], rank[:, :].rearrange("p (t e) -> p t e", e=E),
                                 start[:, :].unsqueeze(1).to_broadcast(small), ALU.add),
                 V.tensor_scalar(k.tile_expert[:, :], texp_f[:, :], float(E - 1), None, ALU.min))
            then(*(V.tensor_tensor(placed[n][:, :, :], place[:, :, :], pick[n][:, :, :], ALU.mult) for n in range(2)))
            then(*(V.tensor_reduce(slot_f[:, n, :], placed[n][:, :, :], AX.X, ALU.add) for n in range(2)))
            slot = slot_f[:, :, :].rearrange("p n t -> p (n t)")
            then(V.tensor_copy(k.slots[:, :, :], slot_f[:, :, :]),
                 V.tensor_tensor(behind[:, :, :], slot.unsqueeze(2).to_broadcast([P, C, TILES + 1]),
                                 edges[:, :].unsqueeze(1).to_broadcast([P, C, TILES + 1]), ALU.is_ge))
            then(V.tensor_reduce(behind_count[:, :], behind[:, :, :], AX.X, ALU.add),
                 V.tensor_tensor(in_tile[:, :, :], behind[:, :, 0:TILES], behind[:, :, 1:TILES + 1], ALU.subtract))
            then(V.scalar_tensor_tensor(in_place[:, :], behind_count[:, :], -float(P), slot, ALU.mult, ALU.add))
            for c in range(C):
                V.tensor_scalar(token_at[:, c, :], row[:, :], in_place[:, c:c + 1], token[:, c % TT:c % TT + 1], ALU.is_equal, ALU.mult
                                ).then_inc(tokens_at, 1)
            dve.wait_ge(listed, 1)
            V.tensor_copy(k.slot_token[:, :], listing[:, :])
            for e in range(BY_POOL, E):
                dve.wait_ge(d_hi, 2 * e + 2)
                V.tensor_tensor(w.down_lo[:, e, 0:whole, :], stage[:, e % DOWN_BUFS, 0:whole, :], w.down_hi[:, e, 0:whole, :], ALU.subtract)
                V.tensor_tensor(w.down_lo[0:tail, e, whole, :], stage[0:tail, e % DOWN_BUFS, whole, :], w.down_hi[0:tail, e, whole, :],
                                ALU.subtract)


def expert_phase(nc, k, w, xn, y_out):
    U = 3
    assert TILES % U == 0
    MT = MK - 1
    TAIL = I_MOE - MT * P
    with phase(nc) as st:
        sb, ps, sem = opener(nc, st)
        rows = sb("e_rows", [P, U, D])
        xt_hi, xt_lo = sb("e_xt_hi", [P, U, D], F16), sb("e_xt_lo", [P, U, D], F16)
        silu, h = sb("e_silu", [P, U, I_MOE]), sb("e_h", [P, U, I_MOE])
        h_hi, h_lo = sb("e_h_hi", [P, U, MK, P], F16), sb("e_h_lo", [P, U, MK, P], F16)
        y = sb("e_y", [P, U, D])
        turn, h_turn = ps("e_turn", [P, D]), ps("e_h_turn", [P, MK, P])
        gate_ps, up_ps, out_ps = ps("e_gate", [P, 2, D]), ps("e_up", [P, 2, D]), ps("e_out", [P, 2, D])
        gathered = [sem(f"gathered{u}") for u in range(U)]
        stored = [sem(f"e_stored{u}") for u in range(U)]
        turned, xt_hi_done, xt_lo_done = sem("e_turned"), sem("e_xt_hi_done"), sem("e_xt_lo_done")
        expanded, silu_done, h_done = sem("e_expanded"), sem("e_silu_done"), sem("e_h_done")
        h_turned, h_hi_done, h_lo_done = sem("e_h_turned"), sem("e_h_hi_done"), sem("e_h_lo_done")
        contracted, y_done = sem("e_contracted"), sem("e_y_done")
        block = st.enter_context(nc.Block())
        BODY = 2 * U
        PEEL = 9
        LOOPS = (TILES - PEEL) // BODY
        assert PEEL + LOOPS * BODY == TILES

        def over_tiles(eng, step):
            for n in range(PEEL):
                step(n, n // U, n, n, 0)
            with eng.Fori(0, LOOPS) as i:
                for j in range(PEEL, PEEL + BODY):
                    step(i * BODY + j, i * 2 + j // U, j, PEEL, 0)
            for n in range(TILES, TILES + 3):
                step(n, n // U, n, PEEL, n - TILES + 1)

        @block.gpsimd
        def _(pool):
            for n in range(TILES):
                if n >= U:
                    pool.wait_ge(turned, n - U + 1)
                nc.gpsimd.indirect_dma_start(rows[:, n % U, :], None, xn,
                                             bass.IndirectOffsetOnAxis(ap=k.slot_token[:, n:n + 1], axis=0)
                                             ).then_inc(gathered[n % U], 16)

        @block.tensor
        def _(pe):
            def step(n, rounds, r, early, late):
                if not late:
                    u = r % U
                    pe.wait_ge(gathered[u], rounds * 16 + 16)
                    if early >= 1:
                        pe.wait_ge(xt_lo_done, n)
                    for c in range(KD):
                        last = nc.tensor.transpose(turn[:, c * P:(c + 1) * P], rows[:, u, c * P:(c + 1) * P], k.ident[:, :])
                    last.then_inc(turned, 1)
                if early >= 1 and late <= 1:
                    u, b = (r - 1) % U, (r - 1) % 2
                    expert = nc.tensor.value_load(k.tile_expert[0:1, bass.ds(n - 1, 1)], min_val=0, max_val=E - 1)
                    pe.wait_ge(xt_lo_done, n)
                    if early >= 3:
                        pe.wait_ge(h_done, n - 2)
                    for dst, hi, lo in ((gate_ps, w.gate_hi, w.gate_lo), (up_ps, w.up_hi, w.up_lo)):
                        out = dst[:, b, 0:I_MOE]
                        for c in range(KD):
                            x_hi, x_lo = (a[:, u, c * P:(c + 1) * P] for a in (xt_hi, xt_lo))
                            w_hi, w_lo = (a[:, bass.ds(expert, 1), c, :].rearrange("p o i -> p (o i)") for a in (hi, lo))
                            nc.tensor.matmul(out, x_hi, w_hi, start=(c == 0), stop=False)
                            nc.tensor.matmul(out, x_lo, w_hi, start=False, stop=False)
                            last = nc.tensor.matmul(out, x_hi, w_lo, start=False, stop=(c == KD - 1))
                    last.then_inc(expanded, 1)
                if early >= 2 and late <= 2:
                    u = (r - 2) % U
                    pe.wait_ge(h_done, n - 1)
                    if early >= 3:
                        pe.wait_ge(h_lo_done, (n - 2) * 2)
                    for q in range(MK):
                        i_ = slice(q * P, min((q + 1) * P, I_MOE))
                        last = nc.tensor.transpose(h_turn[0:i_.stop - i_.start, q, :], h[:, u, i_], k.ident[:, :])
                    last.then_inc(h_turned, 1)
                if early >= 3:
                    u, b = (r - 3) % U, (r - 3) % 2
                    expert = nc.tensor.value_load(k.tile_expert[0:1, bass.ds(n - 3, 1)], min_val=0, max_val=E - 1)
                    pe.wait_ge(h_lo_done, (n - 2) * 2)
                    if early >= 5:
                        pe.wait_ge(y_done, n - 4)
                    for q in range(MK):
                        n_ = min(P, I_MOE - q * P)
                        a_hi, a_lo = (a[0:n_, u, q, :] for a in (h_hi, h_lo))
                        w_hi, w_lo = (a[0:n_, bass.ds(expert, 1), q, :].rearrange("p o d -> p (o d)") for a in (w.down_hi, w.down_lo))
                        nc.tensor.matmul(out_ps[:, b, :], a_hi, w_hi, start=(q == 0), stop=False)
                        nc.tensor.matmul(out_ps[:, b, :], a_lo, w_hi, start=False, stop=False)
                        last = nc.tensor.matmul(out_ps[:, b, :], a_hi, w_lo, start=False, stop=(q == MK - 1))
                    last.then_inc(contracted, 1)
            over_tiles(pe, step)

        parts = ((slice(0, P), slice(0, MT)), (slice(0, TAIL), slice(MT, MK)))

        @block.scalar
        def _(act):
            nc.scalar.preload_act_table(ACT.Silu)

            def step(n, rounds, r, early, late):
                if not late:
                    act.wait_ge(turned, n + 1)
                    if early >= 3:
                        act.wait_ge(expanded, n - 2)
                    nc.scalar.activation(xt_hi[:, r % U, :], turn[:, :], ACT.Copy).then_inc(xt_hi_done, 1)
                if early >= 1 and late <= 1:
                    act.wait_ge(expanded, n)
                    nc.scalar.activation(silu[:, (r - 1) % U, :], gate_ps[:, (r - 1) % 2, 0:I_MOE], ACT.Silu).then_inc(silu_done, 1)
                if early >= 2 and late <= 2:
                    act.wait_ge(h_turned, n - 1)
                    if early >= 5:
                        act.wait_ge(contracted, n - 4)
                    for rows_, blocks in parts:
                        nc.scalar.activation(h_hi[rows_, (r - 2) % U, blocks, :], h_turn[rows_, blocks, :], ACT.Copy).then_inc(h_hi_done, 1)
            over_tiles(act, step)

        @block.vector
        def _(dve):
            def step(n, rounds, r, early, late):
                if not late:
                    dve.wait_ge(xt_hi_done, n + 1)
                    nc.vector.tensor_tensor(xt_lo[:, r % U, :], turn[:, :], xt_hi[:, r % U, :], ALU.subtract).then_inc(xt_lo_done, 1)
                if early >= 1 and late <= 1:
                    dve.wait_ge(silu_done, n)
                    if early >= 4:
                        dve.wait_ge(h_turned, n - 3)
                    nc.vector.tensor_tensor(h[:, (r - 1) % U, :], up_ps[:, (r - 1) % 2, 0:I_MOE], silu[:, (r - 1) % U, :],
                                            ALU.mult).then_inc(h_done, 1)
                if early >= 2 and late <= 2:
                    dve.wait_ge(h_hi_done, (n - 1) * 2)
                    for rows_, blocks in parts:
                        nc.vector.tensor_tensor(h_lo[rows_, (r - 2) % U, blocks, :], h_turn[rows_, blocks, :],
                                                h_hi[rows_, (r - 2) % U, blocks, :], ALU.subtract).then_inc(h_lo_done, 1)
                if early >= 3:
                    u, b = (r - 3) % U, (r - 3) % 2
                    dve.wait_ge(contracted, n - 2)
                    if early >= 6:
                        dve.wait_ge(stored[u], rounds * 16 - 16)
                    nc.vector.tensor_copy(y[:, u, :], out_ps[:, b, :]).then_inc(y_done, 1)
            over_tiles(dve, step)

        @block.sync
        def _(sp):
            with sp.Fori(0, TILES // U) as i:
                for u in range(U):
                    sp.wait_ge(y_done, i * U + (u + 1))
                    sp.dma_start(y_out[bass.ds((i * U + u) * P, P), :], y[:, u, :]).then_inc(stored[u], 16)
            for u in range(U):
                sp.wait_ge(stored[u], TILES // U * 16)


HEADS1 = 16
HD1 = D // HEADS1
QUAD = P // HD1
XATTN_EPS = 1e-6
RING = 8
KV_SCALE = 1.0 / N


def xattn_phase(nc, k, x1s, y_rows, ctx, wq_t, wg_t, bg_cols, wkv_t, wo_t, x3):
    with phase(nc) as st:
        sb, ps, sem = opener(nc, st)
        X_BUFS = 3
        ln = LayerNorm(sb, sem, "x2")
        wq, wg, wkv, wo = (tuple(sb(f"{n}_{q}", [P, KD, m], F16) for q in ("hi", "lo"))
                           for n, m in (("wq", D), ("wg", D), ("wkv", 2 * D), ("wo", D)))
        stage = sb("a_stage", [P, 2, 2, 2 * D])
        bg = sb("a_bg", [P, KD])
        mask = sb("a_mask", [P, 2 * P])
        ctx_in, x2 = sb("a_ctx", [P, 4, D]), sb("a_x2", [P, X_BUFS, 4, D])
        y_in = sb("a_y", [P, 4, 2, D])
        xn = sb("a_xn", [P, 4, D])
        ct = tuple(sb(f"a_ct_{q}", [P, KD, CH], F16) for q in ("hi", "lo"))
        xt = tuple(sb(f"a_xt_{q}", [P, KD, CH], F16) for q in ("hi", "lo"))
        low, low_exp = sb("a_low", [P, 2, D]), sb("a_low_exp", [P, 2, D])
        feat = sb("a_feat", [P, 2, D])
        k_hi, k_lo = sb("a_k_hi", [P, 4, D], F16), sb("a_k_lo", [P, 4, D], F16)
        q_hi, q_lo = sb("a_q_hi", [P, KD, CH], F16), sb("a_q_lo", [P, KD, CH], F16)
        v_hi, v_lo = sb("a_v_hi", [P, 4, KD, 2 * P], F16), sb("a_v_lo", [P, 4, KD, P], F16)
        gate = sb("a_gate", [P, KD, CH])
        kv = sb("a_kv", [P, 2, KD, 2, P])
        kv_hi, kv_lo = sb("a_kv_hi", [P, 2, KD, 2, P], F16), sb("a_kv_lo", [P, 2, KD, 2, P], F16)
        denom, weighted = sb("a_denom", [P, 2, N]), sb("a_mixed", [P, 2, N])
        a_hi, a_lo = sb("a_a_hi", [P, KD, CH], F16), sb("a_a_lo", [P, KD, CH], F16)
        ring = ps("a_ring", [P, RING, D])

        w_loaded = [sem(f"a_w_loaded{u}") for u in range(2)]
        small_loaded, mask_made, mask_scaled, bg_negated = (sem(f"a_{n}") for n in ("small_loaded", "mask_made", "mask_scaled", "bg_negated"))
        w_hi, w_lo = sem("a_w_hi"), sem("a_w_lo")
        ctx_loaded, x_loaded = sem("a_ctx_loaded"), [sem(f"a_x_loaded{u}") for u in range(X_BUFS)]
        y_loaded = [sem(f"a_y_loaded{u}") for u in range(4)]
        first_added, combined, normed = sem("a_first_added"), sem("a_combined"), sem("a_normed")
        c_turned, c_hi, c_lo = sem("a_c_turned"), sem("a_c_hi"), sem("a_c_lo")
        x_turned, x_hi, x_lo = sem("a_x_turned"), sem("a_x_hi"), sem("a_x_lo")
        k_done, v_done, q_done, g_done, gate_done = (sem(f"a_{n}") for n in ("k_done", "v_done", "q_done", "g_done", "gate_done"))
        sum_done, mix_done, out_done, out_read = (sem(f"a_{n}") for n in ("sum_done", "mix_done", "out_done", "out_read"))
        v_hi_done, low_done, low_exp_done = sem("a_v_hi_done"), sem("a_low_done"), sem("a_low_exp_done")
        feat_done, feat_hi, feat_lo = sem("a_feat_done"), sem("a_feat_hi"), sem("a_feat_lo")
        v_lo_done, gate_exp = sem("a_v_lo_done"), sem("a_gate_exp")
        kv_done, kv_hi_done, kv_lo_done = sem("a_kv_done"), sem("a_kv_hi_done"), sem("a_kv_lo_done")
        denom_done, recip_done, weighted_done = sem("a_denom_done"), sem("a_recip_done"), sem("a_weighted_done")
        a_hi_done, a_lo_done, stored = sem("a_a_hi_done"), sem("a_a_lo_done"), sem("a_stored")
        block = st.enter_context(nc.Block())
        x1s_d, x3_d, ctx_d = (a.rearrange("(c k p) d -> p (c k) d", p=P, k=4) for a in (x1s, x3, ctx))

        pieces = [(m, dst, b) for m, dst in ((wkv_t, wkv), (wq_t, wq), (wg_t, wg), (wo_t, wo)) for b in (0, 2)]
        NP = len(pieces)

        def staged(n):
            cols = pieces[n][1][0].shape[2]
            return stage[:, n % 2, :, 0:cols]

        def ops(c, op, count):
            return [(c, op, n) for n in range(count)] if c < NCH else []

        def projections(c, first, second, last, count):
            return [(c, op, n) for n in range(count) for op in (first, second, last)] if c < NCH else []

        def weights(first, end):
            return [(0, "WS", n) for n in range(first, end)]

        schedule = (ops(0, "TC", 4) + weights(0, 2) + ops(0, "CB", 4) + ops(0, "NA", 1) + ops(0, "NB", 1)
                    + mixed(projections(0, "K", "V", "KF", 4), weights(2, 4) + ops(0, "TX", 4) + weights(4, NP)))
        for c in range(NCH):
            schedule += mixed(projections(c, "Q", "G", "QF", KD), [o for n in range(4) for o in ((c + 1, "TC", n), (c + 1, "CB", n)) if c + 1 < NCH])
            schedule += ops(c + 1, "NA", 1) + ops(c, "SM", 4) + ops(c, "SS", 2) + ops(c + 1, "NB", 1)
            schedule += mixed(projections(c + 1, "K", "V", "KF", 4), ops(c, "AT", 2 * KD))
            schedule += mixed(ops(c, "OUT", 4), ops(c + 1, "TX", 4))

        READ = {"TC": (c_lo, 4), "TX": (x_lo, 4), "K": (feat_done, 8), "Q": (feat_done, 8), "V": (v_lo_done, 4), "G": (gate_exp, 4),
                "SM": (kv_done, 4), "AT": (weighted_done, 8), "OUT": (out_read, 4)}
        SECOND = {"KF": "K", "QF": "Q"}
        uses, home, previous = [], {}, {}
        for at in schedule:
            if at[1] in READ:
                home[at] = len(uses) % RING
                if len(uses) >= RING:
                    previous[at] = uses[-RING]
                uses.append(at)
            elif at[1] in SECOND:
                home[at] = home[at[0], SECOND[at[1]], at[2]]

        def run(step):
            for at in schedule:
                step(*at, home.get(at))

        @block.sync
        def _(sp):
            def load_rows(c):
                if c >= X_BUFS:
                    sp.wait_ge(stored, (c - X_BUFS + 1) * 4 * 16)
                sp.dma_start(x2[:, c % X_BUFS], x1s_d[:, c * 4:c * 4 + 4, :]).then_inc(x_loaded[c % X_BUFS], 16)

            sp.dma_start(ctx_in[:, :, :], ctx_d[:, 0:4, :]).then_inc(ctx_loaded, 16)
            sp.dma_start(bg[:, :], bg_cols).then_inc(small_loaded, 16)
            for n, (m, dst, b) in enumerate(pieces):
                if n >= 2:
                    sp.wait_ge(w_lo, n - 1)
                sp.dma_start(staged(n), m[b * P:(b + 2) * P, :].rearrange("(k p) n -> p k n", p=P)).then_inc(w_loaded[n % 2], 16)
                if n == 1:
                    load_rows(0)
            for c in range(NCH):
                if c < NCH - 1:
                    sp.wait_ge(c_turned, 4 * c + 4)
                    sp.dma_start(ctx_in[:, :, :], ctx_d[:, c * 4 + 4:c * 4 + 8, :]).then_inc(ctx_loaded, 16)
                    load_rows(c + 1)
                for t in range(4):
                    sp.wait_ge(out_read, c * 4 + t + 1)
                    sp.dma_start(x3_d[:, c * 4 + t, :], x2[:, c % X_BUFS, t]).then_inc(stored, 16)
            sp.wait_ge(stored, NCH * 4 * 16)
        @block.gpsimd
        def _(pool):
            nc.gpsimd.memset(v_hi[:, :, :, P:2 * P], 1.0).then_inc(mask_made, 1)
            nc.gpsimd.memset(mask[:, :], 0.0).then_inc(mask_made, 1)
            pool.wait_ge(mask_made, 2)
            for rep in range(2):
                m = mask[:, rep * P:(rep + 1) * P].rearrange("p (j i) -> p j i", i=HD1)
                nc.gpsimd.affine_select(out=m, in_=m, compare_op=ALU.is_gt, fill=KV_SCALE, base=0,
                                        pattern=[[HD1, QUAD], [0, HD1]], channel_multiplier=-1).then_inc(mask_made, 1)
            pool.wait_ge(mask_made, 4)
            for rep in range(2):
                m = mask[:, rep * P:(rep + 1) * P].rearrange("p (j i) -> p j i", i=HD1)
                nc.gpsimd.affine_select(out=m, in_=m, compare_op=ALU.is_gt, fill=0.0, base=HD1,
                                        pattern=[[HD1, QUAD], [0, HD1]], channel_multiplier=-1).then_inc(mask_made, 1)

            def gather(c, t):
                n = c * 4 + t
                if c:
                    pool.wait_ge(combined, n - 3)
                for e in range(2):
                    nc.gpsimd.indirect_dma_start(y_in[:, t, e, :], None, y_rows,
                                                 bass.IndirectOffsetOnAxis(ap=k.slots[:, e, n:n + 1], axis=0)
                                                 ).then_inc(y_loaded[t], 16)

            for t in range(4):
                gather(0, t)

            def step(c, op, n, bank):
                if op == "KF":
                    pool.wait_ge(feat_hi, c * 8 + n + 1)
                    nc.gpsimd.tensor_tensor(k_lo[:, n, :], feat[:, n % 2, :], k_hi[:, n, :], ALU.subtract).then_inc(feat_lo, 1)
                    if c < NCH - 1:
                        gather(c + 1, n)
                if op == "QF":
                    pool.wait_ge(feat_hi, c * 8 + n + 5)
                    nc.gpsimd.tensor_tensor(q_lo[:, n, :], feat[:, n % 2, :], q_hi[:, n, :], ALU.subtract).then_inc(feat_lo, 1)
                if op == "AT":
                    b, m = divmod(n, KD)
                    pool.wait_ge(a_hi_done, c * 8 + n + 1)
                    nc.gpsimd.tensor_tensor(a_lo[:, m, b * N:(b + 1) * N], weighted[:, n % 2, :], a_hi[:, m, b * N:(b + 1) * N],
                                            ALU.subtract).then_inc(a_lo_done, 1)
            run(step)

        @block.scalar
        def _(act):
            A = nc.scalar.activation

            def step(c, op, n, bank):
                if op == "TC":
                    act.wait_ge(c_turned, c * 4 + n + 1)
                    if c:
                        act.wait_ge(v_done, c * 4)
                    A(ct[0][:, :, n * P:(n + 1) * P], ring[:, bank, :].rearrange("p (k i) -> p k i", i=P), ACT.Copy).then_inc(c_hi, 1)
                if op == "TX":
                    act.wait_ge(x_turned, c * 4 + n + 1)
                    if c:
                        act.wait_ge(g_done, c * 4)
                    A(xt[0][:, :, n * P:(n + 1) * P], ring[:, bank, :].rearrange("p (k i) -> p k i", i=P), ACT.Copy).then_inc(x_hi, 1)
                if op == "WS":
                    act.wait_ge(w_loaded[n % 2], (n // 2 + 1) * 16)
                    _, dst, b = pieces[n]
                    A(dst[0][:, b:b + 2, :], staged(n), ACT.Copy).then_inc(w_hi, 1)
                if op == "NA":
                    ln.root(nc, act, c)
                if op == "K":
                    act.wait_ge(low_done, c * 8 + n + 1)
                    A(low_exp[:, n % 2, :], low[:, n % 2, :], ACT.Exp).then_inc(low_exp_done, 1)
                if op == "V":
                    act.wait_ge(v_done, c * 4 + n + 1)
                    if c:
                        act.wait_ge(sum_done, c * 4)
                    A(v_hi[:, n, :, 0:P], ring[:, bank, :].rearrange("p (m i) -> p m i", i=P), ACT.Copy).then_inc(v_hi_done, 1)
                if op == "KF":
                    act.wait_ge(feat_done, c * 8 + n + 1)
                    A(k_hi[:, n, :], feat[:, n % 2, :], ACT.Copy).then_inc(feat_hi, 1)
                if op == "Q":
                    act.wait_ge(low_done, c * 8 + n + 5)
                    A(low_exp[:, n % 2, :], low[:, n % 2, :], ACT.Exp).then_inc(low_exp_done, 1)
                if op == "G":
                    act.wait_ge(g_done, c * 4 + n + 1)
                    if c:
                        act.wait_ge(denom_done, c * 8)
                    A(gate[:, n, :], ring[:, bank, :], ACT.Exp, bias=bg[:, n:n + 1], scale=-1.0).then_inc(gate_exp, 1)
                if op == "QF":
                    act.wait_ge(feat_done, c * 8 + n + 5)
                    if c:
                        act.wait_ge(mix_done, c * 8)
                    A(q_hi[:, n, :], feat[:, n % 2, :], ACT.Copy).then_inc(feat_hi, 1)
                if op == "SS":
                    act.wait_ge(kv_done, c * 4 + n * 2 + 2)
                    A(kv_hi[:, n], kv[:, n], ACT.Copy).then_inc(kv_hi_done, 1)
                if op == "AT":
                    b, m = divmod(n, KD)
                    act.wait_ge(weighted_done, c * 8 + n + 1)
                    if c:
                        act.wait_ge(out_done, c * 4)
                    A(a_hi[:, m, b * N:(b + 1) * N], weighted[:, n % 2, :], ACT.Copy).then_inc(a_hi_done, 1)
            act.wait_ge(small_loaded, 16)
            act.wait_ge(bg_negated, 1)
            run(step)

        @block.vector
        def _(dve):
            V = nc.vector

            def low_part(bank, f):
                if f >= 2:
                    dve.wait_ge(low_exp_done, f - 1)
                V.tensor_scalar(low[:, f % 2, :], ring[:, bank, :], 0.0, None, ALU.min).then_inc(low_done, 1)

            def feature(bank, f):
                dve.wait_ge(low_exp_done, f + 1)
                if f >= 2:
                    dve.wait_ge(feat_lo, f - 1)
                V.scalar_tensor_tensor(feat[:, f % 2, :], ring[:, bank, :], 0.0, low_exp[:, f % 2, :], ALU.max, ALU.add).then_inc(feat_done, 1)

            def step(c, op, n, bank):
                if op == "CB":
                    u, at = c % X_BUFS, c * 4 + n
                    if n == 0:
                        dve.wait_ge(x_loaded[u], (c // X_BUFS + 1) * 16)
                    dve.wait_ge(y_loaded[n], (c + 1) * 32)
                    V.scalar_tensor_tensor(x2[:, u, n, :], y_in[:, n, 0, :], k.mix[:, 0, at:at + 1], x2[:, u, n, :],
                                           ALU.mult, ALU.add).then_inc(first_added, 1)
                    dve.wait_ge(first_added, at + 1)
                    V.scalar_tensor_tensor(x2[:, u, n, :], y_in[:, n, 1, :], k.mix[:, 1, at:at + 1], x2[:, u, n, :],
                                           ALU.mult, ALU.add).then_inc(combined, 1)
                    dve.wait_ge(combined, at + 1)
                    ln.tile(nc, x2[:, u], n)
                if op == "NA":
                    if c:
                        dve.wait_ge(normed, c * 4)
                    ln.variance(nc, dve, c)
                if op == "NB":
                    ln.inverse(nc, dve, c)
                    if c:
                        dve.wait_ge(x_turned, c * 4)
                    for t in range(4):
                        V.tensor_scalar(xn[:, t, :], x2[:, c % X_BUFS, t, :], ln.mean[:, t:t + 1], ln.rstd[:, t:t + 1],
                                        ALU.subtract, ALU.mult).then_inc(normed, 1)
                if op in ("TC", "TX"):
                    hi_done, lo_done, dst = (c_hi, c_lo, ct) if op == "TC" else (x_hi, x_lo, xt)
                    tok = slice(n * P, (n + 1) * P)
                    dve.wait_ge(hi_done, c * 4 + n + 1)
                    V.tensor_tensor(dst[1][:, :, tok], ring[:, bank, :].rearrange("p (k i) -> p k i", i=P), dst[0][:, :, tok],
                                    ALU.subtract).then_inc(lo_done, 1)
                if op == "WS":
                    dve.wait_ge(w_hi, n + 1)
                    _, dst, b = pieces[n]
                    V.tensor_tensor(dst[1][:, b:b + 2, :], staged(n), dst[0][:, b:b + 2, :], ALU.subtract).then_inc(w_lo, 1)
                if op == "K":
                    dve.wait_ge(k_done, c * 4 + n + 1)
                    low_part(bank, c * 8 + n)
                if op == "V":
                    dve.wait_ge(v_hi_done, c * 4 + n + 1)
                    V.tensor_tensor(v_lo[:, n], ring[:, bank, :].rearrange("p (m i) -> p m i", i=P), v_hi[:, n, :, 0:P],
                                    ALU.subtract).then_inc(v_lo_done, 1)
                if op == "KF":
                    feature(bank, c * 8 + n)
                if op == "Q":
                    dve.wait_ge(q_done, c * 4 + n + 1)
                    low_part(bank, c * 8 + 4 + n)
                if op == "QF":
                    feature(bank, c * 8 + 4 + n)
                    dve.wait_ge(gate_exp, c * 4 + n + 1)
                    V.tensor_scalar(gate[:, n, :], gate[:, n, :], 1.0, None, ALU.add).then_inc(gate_done, 1)
                if op == "SM":
                    b, half = divmod(n, 2)
                    dve.wait_ge(sum_done, c * 4 + n + 1)
                    if c:
                        dve.wait_ge(kv_lo_done, c * 2)
                    V.tensor_tensor(kv[:, b, 2 * half:2 * half + 2].rearrange("p m s i -> p m (s i)"),
                                    ring[:, bank, :].rearrange("p (q i) -> p q i", q=2),
                                    mask[:, :].unsqueeze(1).to_broadcast([P, 2, 2 * P]), ALU.mult).then_inc(kv_done, 1)
                if op == "SS":
                    dve.wait_ge(kv_hi_done, c * 2 + n + 1)
                    V.tensor_tensor(kv_lo[:, n], kv[:, n], kv_hi[:, n], ALU.subtract).then_inc(kv_lo_done, 1)
                if op == "AT":
                    b, m = divmod(n, KD)
                    at = c * 8 + n
                    dve.wait_ge(mix_done, at + 1)
                    dve.wait_ge(gate_done, c * 4 + m + 1)
                    if at >= 2:
                        dve.wait_ge(weighted_done, at - 1)
                    V.scalar_tensor_tensor(denom[:, n % 2, :], ring[:, bank, N:2 * N], XATTN_EPS * KV_SCALE, gate[:, m, b * N:(b + 1) * N],
                                           ALU.add, ALU.mult).then_inc(denom_done, 1)
                    dve.wait_ge(denom_done, at + 1)
                    V.reciprocal(denom[:, n % 2, :], denom[:, n % 2, :]).then_inc(recip_done, 1)
                    dve.wait_ge(recip_done, at + 1)
                    if at >= 2:
                        dve.wait_ge(a_lo_done, at - 1)
                    V.tensor_tensor(weighted[:, n % 2, :], ring[:, bank, 0:N], denom[:, n % 2, :], ALU.mult).then_inc(weighted_done, 1)
                if op == "OUT":
                    dve.wait_ge(out_done, c * 4 + n + 1)
                    dve.wait_ge(normed, c * 4 + n + 1)
                    V.scalar_tensor_tensor(x2[:, c % X_BUFS, n, :], ring[:, bank, :], k.tanh_gates[:, 1:2], x2[:, c % X_BUFS, n, :],
                                           ALU.mult, ALU.add).then_inc(out_read, 1)
            dve.wait_ge(mask_made, 6)
            dve.wait_ge(small_loaded, 16)
            V.tensor_scalar(bg[:, :], bg[:, :], -1.0, None, ALU.mult).then_inc(bg_negated, 1)
            run(step)

        @block.tensor
        def _(pe):
            mm = nc.tensor.matmul

            def three(out, a, b, first, last):
                mm(out, a[0], b[0], start=first, stop=False)
                mm(out, a[0], b[1], start=False, stop=False)
                return mm(out, a[1], b[0], start=False, stop=last)

            def turn(bank, src, t):
                for b in range(KD):
                    last = nc.tensor.transpose(ring[:, bank, b * P:(b + 1) * P], src[:, t, b * P:(b + 1) * P], k.ident[:, :])
                return last

            def step(c, op, n, bank):
                if (c, op, n) in previous:
                    pc, pop, pn = previous[c, op, n]
                    read, per = READ[pop]
                    pe.wait_ge(read, pc * per + pn + (5 if pop == "Q" else 1))
                if op == "TC":
                    pe.wait_ge(ctx_loaded, (c + 1) * 16)
                    turn(bank, ctx_in, n).then_inc(c_turned, 1)
                if op == "TX":
                    pe.wait_ge(normed, c * 4 + n + 1)
                    turn(bank, xn, n).then_inc(x_turned, 1)
                if op in ("K", "V"):
                    o = op == "V"
                    pe.wait_ge(c_lo, c * 4 + n + 1)
                    pe.wait_ge(w_lo, 2)
                    for b in range(KD):
                        last = three(ring[:, bank, :], [a[:, b, n * P:(n + 1) * P] for a in ct],
                                     [a[:, b, o * D:(o + 1) * D] for a in wkv], b == 0, b == KD - 1)
                    last.then_inc(v_done if o else k_done, 1)
                if op in ("Q", "G"):
                    wt, made = (wq, q_done) if op == "Q" else (wg, g_done)
                    pe.wait_ge(x_lo, c * 4 + 4)
                    pe.wait_ge(w_lo, 4 if op == "Q" else 6)
                    for b in range(KD):
                        last = three(ring[:, bank, :], [a[:, b, n * P:(n + 1) * P] for a in wt], [a[:, b, :] for a in xt], b == 0, b == KD - 1)
                    last.then_inc(made, 1)
                if op == "SM":
                    b, half = divmod(n, 2)
                    pe.wait_ge(feat_lo, c * 8 + 4)
                    pe.wait_ge(v_lo_done, c * 4 + 4)
                    pe.wait_ge(mask_made, 1)
                    for q in range(2):
                        m = half * 2 + q
                        full, half_ = slice(q * N, (q + 1) * N), slice(q * N, q * N + P)
                        for t in (2 * b, 2 * b + 1):
                            kh, kl = (a[:, t, m * P:(m + 1) * P] for a in (k_hi, k_lo))
                            mm(ring[:, bank, full], kh, v_hi[:, t, m, :], start=(t == 2 * b), stop=False)
                            mm(ring[:, bank, half_], kh, v_lo[:, t, m, :], start=False, stop=False)
                            last = mm(ring[:, bank, full], kl, v_hi[:, t, m, :], start=False, stop=(t == 2 * b + 1))
                    last.then_inc(sum_done, 1)
                if op == "AT":
                    b, m = divmod(n, KD)
                    pe.wait_ge(feat_lo, c * 8 + 8)
                    pe.wait_ge(kv_lo_done, c * 2 + b + 1)
                    qs = [a[:, m, b * N:(b + 1) * N] for a in (q_hi, q_lo)]
                    for o in range(2):
                        last = three(ring[:, bank, o * N:(o + 1) * N], [a[:, b, m, o, :] for a in (kv_hi, kv_lo)], qs, True, True)
                    last.then_inc(mix_done, 1)
                if op == "OUT":
                    pe.wait_ge(a_lo_done, c * 8 + (n // 2 + 1) * 4)
                    pe.wait_ge(w_lo, NP)
                    for m in range(KD):
                        last = three(ring[:, bank, :], [a[:, m, n * P:(n + 1) * P] for a in (a_hi, a_lo)],
                                     [a[:, m, :] for a in wo], m == 0, m == KD - 1)
                    last.then_inc(out_done, 1)
            run(step)


EXPERTS2, SLOTS2, HID2 = 16, 128, 128
ES = EXPERTS2 * SLOTS2
NJ = ES // D
JE = D // SLOTS2
L2_EPS = 1e-12


def soft_moe_phase(nc, k, w, x3, gamma, beta, mu, scale, w1, b1_cols, w2, b2, out):
    with phase(nc) as st:
        sb, ps, sem = opener(nc, st)
        ln1, ln2 = LayerNorm(sb, sem, "s1", 2), LayerNorm(sb, sem, "s2", 2)
        gam, bet = sb("s_gamma", [P, D]), sb("s_beta", [P, D])
        scl, b1 = sb("s_scale", [P, 1]), sb("s_b1", [P, EXPERTS2])
        b2s = sb("s_b2", [EXPERTS2, D])
        x_in, x_ln, x_res = sb("s_x", [P, 2, D]), sb("s_xln", [P, 2, D]), sb("s_res", [P, 2, D])
        waste = sb("s_waste", [P, 2, D], F16)
        squares, l2, rs = sb("s_squares", [P, 2]), sb("s_l2", [P, 2]), sb("s_rs", [P, 2])
        xl = tuple(sb(f"s_xl_{q}", [P, 2, D], F16) for q in ("hi", "lo"))
        xt = tuple(sb(f"s_xt_{q}", [P, KD, N], F16) for q in ("hi", "lo"))
        lg = sb("s_lg", [P, 2, ES])
        top, low = sb("s_top", [P, 2, NJ]), sb("s_low", [P, 2])
        slot_top, slot_low = sb("s_slot_top", [P, 4, 2]), sb("s_slot_low", [P, 4, 2])
        slot_sum, slot_inv = sb("s_slot_sum", [P, 2, 2]), sb("s_slot_inv", [P, 2, 2])
        dt = sb("s_dt", [P, 2, 2, N])
        ed = tuple(sb(f"s_ed_{q}", [P, 2, ES], F16) for q in ("hi", "lo"))
        et = tuple(sb(f"s_et_{q}", [P, EXPERTS2, N], F16) for q in ("hi", "lo"))
        part = sb("s_part", [P, 2, EXPERTS2])
        part_t = sb("s_part_t", [EXPERTS2, 2, P])
        rn = sb("s_rn", [P, 2])
        si = tuple(sb(f"s_si_{q}", [P, 2, KD, D], F16) for q in ("hi", "lo"))
        h32 = sb("s_h32", [P, 2, D])
        hp = tuple(sb(f"s_h_{q}", [P, 2, D], F16) for q in ("hi", "lo"))
        so = tuple(sb(f"s_so_{q}", [P, 2, D], F16) for q in ("hi", "lo"))
        ones = sb("s_ones", [P, P])
        mu_in = [a.bitcast(F32).rearrange("p (k d) -> p k d", k=KD)
                 for a in (*(e[:, :, :].rearrange("p t s -> p (t s)") for e in ed), *(e[:, :, :].rearrange("p e i -> p (e i)") for e in et))]
        mu_square = [a[:, :, :].rearrange("p u d -> p (u d)").bitcast(F32) for a in (*hp, *so)]
        mu_norm = h32
        PIECES, BUFS = 2 * EXPERTS2, 8
        piece_in = [a[:, u, :, :].rearrange("p k d -> p (k d)").bitcast(F32)[:, i * D:(i + 1) * D]
                    for a in si for u in range(2) for i in range(2)]
        ring = ps("s_ring", [P, 6, D])
        acc = ps("s_acc", [P, 2, D])

        names = ("small", "ones_made", "mu_squared", "mu_summed", "mu_rooted", "mu_floored", "mu_inverted", "mu_scaled", "mu_hi", "mu_lo",
                 "piece_hi", "piece_lo", "x_loaded", "res_loaded", "x1_done", "x_affine", "x_gamma", "xln_done", "squared",
                 "l2_done", "l2_floored", "l2_inverted", "rs_done", "xn_done", "xl_hi", "xl_lo", "turned", "xt_hi", "xt_lo",
                 "logits", "lg_out", "top_done", "top_all", "low_done", "d_turned", "slot_top_done", "slot_low_done", "dt_exp",
                 "slot_mean", "slot_inverted", "dt_done", "u_turned", "ed_hi", "ed_lo", "e_done", "part_done",
                 "zn_done", "zn_inv", "rn_done", "part_turned", "part_out", "et_turned", "et_hi", "et_lo",
                 "s_done", "si_hi", "si_lo", "h_done", "h_act", "h_hi", "h_lo", "o_done", "o_hi", "o_lo",
                 "c_done", "out_done", "stored")
        S = {n: sem(f"s_{n}") for n in names}
        mu_loaded = [sem(f"s_mu_loaded{j}") for j in range(NJ)]
        piece_loaded = [sem(f"s_piece_loaded{u}") for u in range(BUFS)]
        block = st.enter_context(nc.Block())
        x_d, out_d = (a.rearrange("(c p) d -> p c d", p=P) for a in (x3, out))

        def ops(op, first, end, nxt=0):
            return [(nxt, op, n) for n in range(first, end)]

        def contract(j):
            return [o for e in range(JE * j, JE * j + JE) for o in [(0, "O", e), (0, "OL", e)] + ([(0, "C", e - 1)] if e else [])]

        TURNS = ES * 2 // (4 * P)
        weights = ops("L", 0, 2, 1)
        for n in range(TURNS + 3):
            if n >= 3:
                weights += [(1, "U", n - 3)]
            if 1 <= n <= TURNS:
                weights += [(1, "F", n - 1)]
            if 2 <= n <= TURNS + 1:
                weights += [(1, "W", n - 2)]
            if n < TURNS:
                weights += [(1, "D", n)]
            if n % 2 == 0 and n + 2 < 2 * NJ:
                weights += ops("L", n + 2, n + 4, 1)
            if n >= TURNS + 3 - NJ:
                weights += ops("E", 2 * (n - TURNS - 3 + NJ), 2 * (n - TURNS - 3 + NJ) + 2, 1)
        norms = [(1, op, 0) for op in ("N1a", "N1b", "N2a", "N2b", "N3a", "N3b")]
        rows = ops("X", 0, 2, 1) + ops("XL", 0, 1, 1)
        HALF = JE * 3 // 2
        experts = (contract(1)[:HALF] + ops("H", 2, 3) + contract(1)[HALF:] + contract(2)[:HALF] + ops("H", 3, 4)
                   + contract(2)[HALF:] + contract(3) + ops("C", EXPERTS2 - 1, EXPERTS2))
        body = (mixed(mixed(ops("S", 0, 2 * KD), ops("T", 0, TURNS)), norms[:4])
                + ops("H", 0, 1) + norms[4:5] + ops("S", 2 * KD, 3 * KD) + ops("B", 0, 1) + norms[5:] + ops("H", 1, 2)
                + mixed(contract(0), ops("S", 3 * KD, 4 * KD) + rows + weights[:2]) + mixed(experts, weights[2:]) + ops("OUT", 0, 1) + [(0, "skip", 0)])
        slots = ops("MA", 0, 1, 1)
        for j in range(NJ):
            slots += ops("MA", j + 1, min(j + 2, NJ), 1) + ops("MR", j, j + 1, 1) + ops("MB", j, j + 1, 1)
        before = mixed(slots, norms + rows) + mixed(weights, ops("P", 0, PIECES, 1))
        last = [op for op in body if not op[0]]

        READ = {"MA": ("mu_rooted", NJ), "X": ("xt_lo", 2), "L": ("lg_out", 2 * NJ), "D": ("dt_exp", TURNS), "U": ("ed_lo", TURNS), "T": ("et_lo", TURNS),
                "B": ("part_out", 1), "S": ("si_lo", NJ * KD), "H": ("h_act", NJ), "O": ("o_lo", EXPERTS2)}
        SECOND = {"F": "D", "OL": "O", "MR": "MA"}
        RING = 6

        def placed(ops_, uses):
            uses, result, home = list(uses), [], {}
            for nxt, op, n in ops_:
                bank = prev = None
                if op == "skip":
                    uses.append(uses[-RING])
                    continue
                if op in READ:
                    bank, prev = len(uses) % RING, uses[-RING]
                    uses.append((nxt, op, n))
                    home[nxt, op, n] = bank
                elif op in SECOND:
                    bank = home[nxt, SECOND[op], n]
                result.append((nxt, op, n, bank, prev))
            return result, [use and (use[0] - 1, *use[1:]) for use in uses[-RING:]]

        taken = sum(op in READ for _, op, _ in before)
        start, carry = placed(before, [None] * (2 * RING - taken % RING))
        first_ops, carry = placed(body, carry)
        loop_ops, loop_carry = placed(body, carry)
        last_ops, _ = placed(last, loop_carry)
        assert loop_carry == carry and sum(op in READ or op == "skip" for _, op, _ in body) % RING == 0

        def run(eng, step):
            def go(b, ops_):
                for nxt, op, n, bank, prev in ops_:
                    step(b + nxt, op, n, bank, prev and (b + prev[0], prev[1], prev[2]))
            go(-1, start)
            go(0, first_ops)
            with eng.Fori(1, B - 1) as b:
                go(b, loop_ops)
            go(B - 1, last_ops)

        def count(b, per_batch, n):
            return b * per_batch + (n + 1)

        def reusable(b, per_batch, n):
            return b * per_batch + max(n - 1, 0)

        def later(b):
            return not (isinstance(b, int) and b == 0)

        @block.sync
        def _(sp):
            sp.dma_start(x_in[:, :, :], x_d[:, 0:2, :]).then_inc(S["x_loaded"], 16)
            for dst, src in ((gam, gamma), (bet, beta), (scl, scale)):
                sp.dma_start(dst[:, :], src.partition_broadcast(P)).then_inc(S["small"], 16)
            sp.dma_start(b1[:, :], b1_cols).then_inc(S["small"], 16)
            sp.dma_start(b2s[:, :], b2).then_inc(S["small"], 16)
            mu_d, w1_d = mu.rearrange("(k p) s -> p k s", p=P), w1.rearrange("e (k p) h -> p e k h", p=P)

            def load_piece(n):
                if n >= BUFS:
                    sp.wait_ge(S["piece_lo"], n - BUFS + 1)
                dst, u = piece_in[n % BUFS], n % BUFS
                if n < EXPERTS2:
                    sp.dma_start(dst.rearrange("p (k h) -> p k h", k=KD), w1_d[:, n]).then_inc(piece_loaded[u], 16)
                else:
                    sp.dma_start(dst, w2[n - EXPERTS2]).then_inc(piece_loaded[u], 16)

            def load_rows(b):
                sp.wait_ge(S["turned"], b * 2)
                sp.dma_start(x_in[:, :, :], x_d[:, bass.ds(b * 2, 2), :]).then_inc(S["x_loaded"], 16)

            def batch(b, ahead=True):
                if later(b):
                    sp.wait_ge(S["stored"], b * 16)
                sp.dma_start(x_res[:, :, :], x_d[:, bass.ds(b * 2, 2), :]).then_inc(S["res_loaded"], 16)
                if ahead:
                    load_rows(b + 2)
                sp.wait_ge(S["out_done"], b * 2 + 2)
                sp.dma_start(out_d[:, bass.ds(b * 2, 2), :], x_res[:, :, :]).then_inc(S["stored"], 16)

            for j in range(NJ):
                sp.dma_start(mu_in[j], mu_d[:, :, j * D:(j + 1) * D]).then_inc(mu_loaded[j], 16)
            for n in range(PIECES):
                load_piece(n)
                if n == BUFS:
                    load_rows(1)
            batch(0)
            with sp.Fori(1, B - 2) as b:
                batch(b)
            batch(B - 2, ahead=False)
            batch(B - 1, ahead=False)
            sp.wait_ge(S["stored"], B * 16)

        def parts_of(n):
            return [a[:, :, n, :] for a in w.w1] if n < EXPERTS2 else [a[:, n - EXPERTS2, :] for a in w.w2]

        def as_part(piece, n):
            return piece.rearrange("p (k h) -> p k h", k=KD) if n < EXPERTS2 else piece

        @block.gpsimd
        def _(pool):
            def step(b, op, n, bank, prev):
                if op == "P":
                    pool.wait_ge(S["piece_hi"], n + 1)
                    hi, lo = parts_of(n)
                    nc.gpsimd.tensor_tensor(lo, as_part(piece_in[n % BUFS], n), hi, ALU.subtract).then_inc(S["piece_lo"], 1)
                if op == "N2b":
                    for t in range(2):
                        pool.wait_ge(S["x_affine"], count(b, 2, t))
                        nc.gpsimd.tensor_tensor(x_ln[:, t, :], x_ln[:, t, :], gam[:, :], ALU.mult).then_inc(S["x_gamma"], 1)
                    for t in range(2):
                        pool.wait_ge(S["x_gamma"], count(b, 2, t))
                        nc.gpsimd.tensor_tensor(x_ln[:, t, :], x_ln[:, t, :], bet[:, :], ALU.add).then_inc(S["xln_done"], 1)
                if op == "XL":
                    pool.wait_ge(S["xl_hi"], b + 1)
                    nc.gpsimd.tensor_tensor(xl[1][:, :, :], x_ln[:, :, :], xl[0][:, :, :], ALU.subtract).then_inc(S["xl_lo"], 1)
                if op == "H":
                    pool.wait_ge(S["h_hi"], count(b, NJ, n))
                    nc.gpsimd.tensor_tensor(hp[1][:, n % 2, :], h32[:, n % 2, :], hp[0][:, n % 2, :], ALU.subtract).then_inc(S["h_lo"], 1)
            nc.gpsimd.memset(ones[:, :], 1.0).then_inc(S["ones_made"], 1)
            pool.wait_ge(S["small"], 16 * 5)
            run(pool, step)

        @block.scalar
        def _(act):
            A = nc.scalar.activation

            def step(b, op, n, bank, prev):
                if op == "P":
                    act.wait_ge(piece_loaded[n % BUFS], (n // BUFS + 1) * 16)
                    A(parts_of(n)[0], as_part(piece_in[n % BUFS], n), ACT.Copy).then_inc(S["piece_hi"], 1)
                if op == "MA":
                    act.wait_ge(mu_loaded[n], 16)
                    if n:
                        act.wait_ge(S["mu_summed"], n)
                    for c in range(KD):
                        A(mu_square[c], mu_in[n][:, c, :], ACT.Square).then_inc(S["mu_squared"], 1)
                if op == "MR":
                    act.wait_ge(S["mu_summed"], n + 1)
                    if n >= 2:
                        act.wait_ge(S["mu_scaled"], n - 1)
                    A(mu_norm[:, n % 2, :], ring[:, bank, :], ACT.Sqrt).then_inc(S["mu_rooted"], 1)
                if op == "MB":
                    act.wait_ge(S["mu_scaled"], n + 1)
                    A(w.mu[0][:, :, n * D:(n + 1) * D], mu_in[n], ACT.Copy).then_inc(S["mu_hi"], 1)
                if op == "N1a":
                    ln1.root(nc, act, b)
                if op == "N2a":
                    ln2.root(nc, act, b)
                if op == "N3a":
                    if later(b):
                        act.wait_ge(S["l2_done"], b)
                    for t in range(2):
                        act.wait_ge(S["xln_done"], count(b, 2, t))
                        A(waste[:, t, :], x_ln[:, t, :], ACT.Square, accum_out=squares[:, t:t + 1]).then_inc(S["squared"], 1)
                    act.wait_ge(S["squared"], count(b, 2, 1))
                    if later(b):
                        act.wait_ge(S["l2_inverted"], b)
                    A(l2[:, :], squares[:, :], ACT.Sqrt).then_inc(S["l2_done"], 1)
                if op == "XL":
                    if later(b):
                        act.wait_ge(S["s_done"], b * (NJ * KD))
                    A(xl[0][:, :, :], x_ln[:, :, :], ACT.Copy).then_inc(S["xl_hi"], 1)
                if op == "X":
                    act.wait_ge(S["turned"], count(b, 2, n))
                    if later(b):
                        act.wait_ge(S["logits"], b * (2 * NJ))
                    A(xt[0][:, :, n * P:(n + 1) * P], ring[:, bank, :].rearrange("p (k i) -> p k i", i=P), ACT.Copy).then_inc(S["xt_hi"], 1)
                if op == "L":
                    j, t = divmod(n, 2)
                    act.wait_ge(S["logits"], count(b, 2 * NJ, n))
                    if later(b):
                        act.wait_ge(S["et_turned"], b * TURNS)
                        act.wait_ge(S["part_done"], b * (2 * NJ))
                    A(lg[:, t, j * D:(j + 1) * D], ring[:, bank, :], ACT.Copy).then_inc(S["lg_out"], 1)
                if op == "F":
                    act.wait_ge(S["slot_low_done"], count(b, TURNS, n))
                    if later(b) or n >= 2:
                        act.wait_ge(S["u_turned"], reusable(b, TURNS, n))
                    for e in range(2):
                        last_ = A(dt[:, n % 2, e, :], ring[:, bank, e * N:(e + 1) * N], ACT.Exp, bias=slot_low[:, n % 4, e:e + 1],
                                  accum_out=slot_sum[:, n % 2, e:e + 1])
                    last_.then_inc(S["dt_exp"], 1)
                if op == "U":
                    act.wait_ge(S["u_turned"], count(b, TURNS, n))
                    if later(b):
                        act.wait_ge(S["s_done"], b * (NJ * KD))
                    A(ed[0][:, :, 2 * n * P:(2 * n + 2) * P], ring[:, bank, :].rearrange("p (t s) -> p t s", t=2), ACT.Copy
                      ).then_inc(S["ed_hi"], 1)
                if op == "E":
                    j, t = divmod(n, 2)
                    act.wait_ge(S["low_done"], b * 2 + 2)
                    act.wait_ge(S["d_turned"], count(b, TURNS, 2 * j + 1))
                    A(lg[:, t, j * D:(j + 1) * D], lg[:, t, j * D:(j + 1) * D], ACT.Exp, bias=low[:, t:t + 1]).then_inc(S["e_done"], 1)
                if op == "T":
                    act.wait_ge(S["et_turned"], count(b, TURNS, n))
                    if later(b):
                        act.wait_ge(S["c_done"], b * EXPERTS2)
                    A(et[0][:, 2 * n:2 * n + 2, :], ring[:, bank, :].rearrange("p (e i) -> p e i", e=2), ACT.Copy).then_inc(S["et_hi"], 1)
                if op == "S":
                    j, m = divmod(n, KD)
                    act.wait_ge(S["s_done"], count(b, NJ * KD, n))
                    if isinstance(b, int) and b == 0 and n == 0:
                        act.wait_ge(S["piece_lo"], PIECES)
                    if later(b) or j >= 2:
                        act.wait_ge(S["h_done"], reusable(b, NJ, j))
                    A(si[0][:, j % 2, m, :], ring[:, bank, :], ACT.Copy, scale=1.0 / N).then_inc(S["si_hi"], 1)
                if op == "H":
                    act.wait_ge(S["h_done"], count(b, NJ, n))
                    if later(b) or n >= 2:
                        act.wait_ge(S["h_lo"], reusable(b, NJ, n))
                    for e in range(JE):
                        last_ = A(h32[:, n % 2, e * SLOTS2:(e + 1) * SLOTS2], ring[:, bank, e * SLOTS2:(e + 1) * SLOTS2], ACT.Gelu,
                                  bias=b1[:, n * JE + e:n * JE + e + 1])
                    last_.then_inc(S["h_act"], 1)
                if op == "O":
                    act.wait_ge(S["o_done"], count(b, EXPERTS2, n))
                    if later(b) or n >= 2:
                        act.wait_ge(S["c_done"], reusable(b, EXPERTS2, n))
                    A(so[0][:, n % 2, :], ring[:, bank, :], ACT.Copy).then_inc(S["o_hi"], 1)
            act.wait_ge(S["small"], 16 * 5)
            run(act, step)

        @block.vector
        def _(dve):
            V = nc.vector

            def step(b, op, n, bank, prev):
                if op == "MB":
                    slots, norm = slice(n * D, (n + 1) * D), mu_norm[:, n % 2, :]
                    dve.wait_ge(S["mu_rooted"], n + 1)
                    V.tensor_scalar(norm, norm, L2_EPS, None, ALU.max).then_inc(S["mu_floored"], 1)
                    dve.wait_ge(S["mu_floored"], n + 1)
                    V.reciprocal(norm, norm).then_inc(S["mu_inverted"], 1)
                    dve.wait_ge(S["mu_inverted"], n + 1)
                    V.tensor_tensor(mu_in[n], mu_in[n], norm.unsqueeze(1).to_broadcast([P, KD, D]), ALU.mult).then_inc(S["mu_scaled"], 1)
                    dve.wait_ge(S["mu_hi"], n + 1)
                    V.tensor_tensor(w.mu[1][:, :, slots], mu_in[n], w.mu[0][:, :, slots], ALU.subtract).then_inc(S["mu_lo"], 1)
                if op == "N1a":
                    dve.wait_ge(S["x_loaded"], b * 16 + 16)
                    for t in range(2):
                        ln1.tile(nc, x_in, t)
                    ln1.variance(nc, dve, b)
                if op == "N1b":
                    ln1.inverse(nc, dve, b)
                    if later(b):
                        dve.wait_ge(S["xl_lo"], b)
                        dve.wait_ge(S["xn_done"], b * 2)
                    for t in range(2):
                        V.tensor_scalar(x_ln[:, t, :], x_in[:, t, :], ln1.mean[:, t:t + 1], ln1.rstd[:, t:t + 1], ALU.subtract,
                                        ALU.mult).then_inc(S["x1_done"], 1)
                if op == "N2a":
                    dve.wait_ge(S["x1_done"], b * 2 + 2)
                    for t in range(2):
                        ln2.tile(nc, x_ln, t)
                    ln2.variance(nc, dve, b)
                if op == "N2b":
                    ln2.inverse(nc, dve, b)
                    for t in range(2):
                        V.tensor_scalar(x_ln[:, t, :], x_ln[:, t, :], ln2.mean[:, t:t + 1], ln2.rstd[:, t:t + 1], ALU.subtract,
                                        ALU.mult).then_inc(S["x_affine"], 1)
                if op == "N3b":
                    dve.wait_ge(S["l2_done"], b + 1)
                    V.tensor_scalar(l2[:, :], l2[:, :], L2_EPS, None, ALU.max).then_inc(S["l2_floored"], 1)
                    dve.wait_ge(S["l2_floored"], b + 1)
                    V.reciprocal(rs[:, :], l2[:, :]).then_inc(S["l2_inverted"], 1)
                    dve.wait_ge(S["l2_inverted"], b + 1)
                    V.tensor_scalar(rs[:, :], rs[:, :], scl[:, 0:1], None, ALU.mult).then_inc(S["rs_done"], 1)
                    dve.wait_ge(S["rs_done"], b + 1)
                    dve.wait_ge(S["xln_done"], b * 2 + 2)
                    for t in range(2):
                        V.tensor_scalar(x_in[:, t, :], x_ln[:, t, :], rs[:, t:t + 1], None, ALU.mult).then_inc(S["xn_done"], 1)
                if op == "X":
                    dve.wait_ge(S["xt_hi"], count(b, 2, n))
                    tok = slice(n * P, (n + 1) * P)
                    V.tensor_tensor(xt[1][:, :, tok], ring[:, bank, :].rearrange("p (k i) -> p k i", i=P), xt[0][:, :, tok], ALU.subtract
                                    ).then_inc(S["xt_lo"], 1)
                if op == "L":
                    j, t = divmod(n, 2)
                    dve.wait_ge(S["lg_out"], count(b, 2 * NJ, n))
                    V.tensor_reduce(top[:, t, j:j + 1], lg[:, t, j * D:(j + 1) * D], AX.X, ALU.max).then_inc(S["top_done"], 1)
                    if j == NJ - 1:
                        dve.wait_ge(S["top_done"], count(b, 2 * NJ, n))
                        V.tensor_reduce(low[:, t:t + 1], top[:, t, :], AX.X, ALU.max).then_inc(S["top_all"], 1)
                        dve.wait_ge(S["top_all"], count(b, 2, t))
                        V.tensor_scalar(low[:, t:t + 1], low[:, t:t + 1], -1.0, None, ALU.mult).then_inc(S["low_done"], 1)
                if op == "D":
                    dve.wait_ge(S["d_turned"], count(b, TURNS, n))
                    V.tensor_reduce(slot_top[:, n % 4, :], ring[:, bank, :].rearrange("p (e i) -> p e i", e=2), AX.X, ALU.max
                                    ).then_inc(S["slot_top_done"], 1)
                    dve.wait_ge(S["slot_top_done"], count(b, TURNS, n))
                    V.tensor_scalar(slot_low[:, n % 4, :], slot_top[:, n % 4, :], -1.0, None, ALU.mult).then_inc(S["slot_low_done"], 1)
                if op == "W":
                    dve.wait_ge(S["dt_exp"], count(b, TURNS, n))
                    V.tensor_scalar(slot_inv[:, n % 2, :], slot_sum[:, n % 2, :], 1.0 / N, None, ALU.mult).then_inc(S["slot_mean"], 1)
                    dve.wait_ge(S["slot_mean"], count(b, TURNS, n))
                    V.reciprocal(slot_inv[:, n % 2, :], slot_inv[:, n % 2, :]).then_inc(S["slot_inverted"], 1)
                    dve.wait_ge(S["slot_inverted"], count(b, TURNS, n))
                    for e in range(2):
                        last_ = V.tensor_scalar(dt[:, n % 2, e, :], dt[:, n % 2, e, :], slot_inv[:, n % 2, e:e + 1], None, ALU.mult)
                    last_.then_inc(S["dt_done"], 1)
                if op == "U":
                    dve.wait_ge(S["ed_hi"], count(b, TURNS, n))
                    s = slice(2 * n * P, (2 * n + 2) * P)
                    V.tensor_tensor(ed[1][:, :, s], ring[:, bank, :].rearrange("p (t s) -> p t s", t=2), ed[0][:, :, s], ALU.subtract
                                    ).then_inc(S["ed_lo"], 1)
                if op == "E":
                    j, t = divmod(n, 2)
                    dve.wait_ge(S["e_done"], count(b, 2 * NJ, n))
                    if later(b) and n == 0:
                        dve.wait_ge(S["part_turned"], b)
                    V.tensor_reduce(part[:, t, j * JE:(j + 1) * JE], lg[:, t, j * D:(j + 1) * D].rearrange("p (e i) -> p e i", i=SLOTS2),
                                    AX.X, ALU.add).then_inc(S["part_done"], 1)
                if op == "B":
                    dve.wait_ge(S["part_done"], (b + 1) * (2 * NJ))
                    if later(b):
                        dve.wait_ge(S["out_done"], b * 2)
                        dve.wait_ge(S["c_done"], b * EXPERTS2)
                    V.tensor_reduce(rn[:, :], part[:, :, :], AX.X, ALU.add).then_inc(S["zn_done"], 1)
                    dve.wait_ge(S["zn_done"], b + 1)
                    V.reciprocal(rn[:, :], rn[:, :]).then_inc(S["zn_inv"], 1)
                    dve.wait_ge(S["zn_inv"], b + 1)
                    V.tensor_scalar(rn[:, :], rn[:, :], k.tanh_gates[:, 3:4], None, ALU.mult).then_inc(S["rn_done"], 1)
                    dve.wait_ge(S["part_turned"], b + 1)
                    V.tensor_copy(part_t[:, :, :], ring[0:EXPERTS2, bank, 0:2 * P].rearrange("p (t i) -> p t i", i=P)).then_inc(S["part_out"], 1)
                if op == "T":
                    dve.wait_ge(S["et_hi"], count(b, TURNS, n))
                    V.tensor_tensor(et[1][:, 2 * n:2 * n + 2, :], ring[:, bank, :].rearrange("p (e i) -> p e i", e=2),
                                    et[0][:, 2 * n:2 * n + 2, :], ALU.subtract).then_inc(S["et_lo"], 1)
                if op == "S":
                    j, m = divmod(n, KD)
                    dve.wait_ge(S["si_hi"], count(b, NJ * KD, n))
                    V.scalar_tensor_tensor(si[1][:, j % 2, m, :], ring[:, bank, :], 1.0 / N, si[0][:, j % 2, m, :], ALU.mult, ALU.subtract
                                           ).then_inc(S["si_lo"], 1)
                if op == "H":
                    dve.wait_ge(S["h_act"], count(b, NJ, n))
                    if later(b) or n >= 2:
                        dve.wait_ge(S["o_done"], b * EXPERTS2 + max(n - 1, 0) * JE)
                    V.tensor_copy(hp[0][:, n % 2, :], h32[:, n % 2, :]).then_inc(S["h_hi"], 1)
                if op == "OL":
                    dve.wait_ge(S["o_hi"], count(b, EXPERTS2, n))
                    V.tensor_tensor(so[1][:, n % 2, :], ring[:, bank, :], so[0][:, n % 2, :], ALU.subtract).then_inc(S["o_lo"], 1)
                if op == "OUT":
                    dve.wait_ge(S["c_done"], (b + 1) * EXPERTS2)
                    dve.wait_ge(S["res_loaded"], b * 16 + 16)
                    dve.wait_ge(S["rn_done"], b + 1)
                    for t in range(2):
                        V.scalar_tensor_tensor(x_res[:, t, :], acc[:, t, :], rn[:, t:t + 1], x_res[:, t, :], ALU.mult, ALU.add
                                               ).then_inc(S["out_done"], 1)
            dve.wait_ge(S["small"], 16 * 5)
            run(dve, step)

        @block.tensor
        def _(pe):
            mm = nc.tensor.matmul

            def three(out_, a, b_, first, last_):
                mm(out_, a[0], b_[0], start=first, stop=False)
                mm(out_, a[0], b_[1], start=False, stop=False)
                return mm(out_, a[1], b_[0], start=False, stop=last_)

            def step(b, op, n, bank, prev):
                if prev:
                    name, per = READ[prev[1]]
                    pe.wait_ge(S[name], count(prev[0], per, prev[2]))
                if op == "X":
                    pe.wait_ge(S["xn_done"], count(b, 2, n))
                    for c in range(KD):
                        last_ = nc.tensor.transpose(ring[:, bank, c * P:(c + 1) * P], x_in[:, n, c * P:(c + 1) * P], k.ident[:, :])
                    last_.then_inc(S["turned"], 1)
                if op == "MA":
                    for c in range(KD):
                        pe.wait_ge(S["mu_squared"], n * KD + c + 1)
                        last_ = mm(ring[:, bank, :], ones[:, :], mu_square[c], start=(c == 0), stop=(c == KD - 1))
                    last_.then_inc(S["mu_summed"], 1)
                if op == "L":
                    j, t = divmod(n, 2)
                    if isinstance(b, int) and b == 0:
                        pe.wait_ge(S["mu_lo"], j + 1)
                    pe.wait_ge(S["xt_lo"], count(b, 2, t))
                    tok = slice(t * P, (t + 1) * P)
                    for c in range(KD):
                        last_ = three(ring[:, bank, :], [a[:, c, tok] for a in xt], [a[:, c, j * D:(j + 1) * D] for a in w.mu],
                                      c == 0, c == KD - 1)
                    last_.then_inc(S["logits"], 1)
                if op == "D":
                    pe.wait_ge(S["lg_out"], count(b, 2 * NJ, 2 * (n // 2) + 1))
                    for e in range(2):
                        for t in range(2):
                            at = (e * 2 + t) * P
                            last_ = nc.tensor.transpose(ring[:, bank, at:at + P], lg[:, t, (2 * n + e) * P:(2 * n + e + 1) * P], k.ident[:, :])
                    last_.then_inc(S["d_turned"], 1)
                if op == "U":
                    pe.wait_ge(S["dt_done"], count(b, TURNS, n))
                    for t in range(2):
                        for e in range(2):
                            at = (t * 2 + e) * P
                            last_ = nc.tensor.transpose(ring[:, bank, at:at + P], dt[:, n % 2, e, t * P:(t + 1) * P], k.ident[:, :])
                    last_.then_inc(S["u_turned"], 1)
                if op == "T":
                    pe.wait_ge(S["e_done"], count(b, 2 * NJ, 2 * (n // 2) + 1))
                    for e in range(2):
                        for t in range(2):
                            at = (e * 2 + t) * P
                            last_ = nc.tensor.transpose(ring[:, bank, at:at + P], lg[:, t, (2 * n + e) * P:(2 * n + e + 1) * P], k.ident[:, :])
                    last_.then_inc(S["et_turned"], 1)
                if op == "B":
                    pe.wait_ge(S["part_done"], (b + 1) * (2 * NJ))
                    for t in range(2):
                        last_ = nc.tensor.transpose(ring[0:EXPERTS2, bank, t * P:(t + 1) * P], part[:, t, :], k.ident[:, :])
                    last_.then_inc(S["part_turned"], 1)
                if op == "S":
                    j, m = divmod(n, KD)
                    pe.wait_ge(S["xl_lo"], b + 1)
                    pe.wait_ge(S["ed_lo"], count(b, TURNS, 2 * j + 1))
                    for t in range(2):
                        last_ = three(ring[:, bank, :], [a[:, t, m * P:(m + 1) * P] for a in xl],
                                      [a[:, t, j * D:(j + 1) * D] for a in ed], t == 0, t == 1)
                    last_.then_inc(S["s_done"], 1)
                if op == "H":
                    pe.wait_ge(S["si_lo"], b * (NJ * KD) + (n + 1) * KD)
                    if isinstance(b, int) and b == 0 and n == 0:
                        pe.wait_ge(S["piece_lo"], EXPERTS2)
                    for e in range(JE):
                        s = slice(e * SLOTS2, (e + 1) * SLOTS2)
                        for c in range(KD):
                            last_ = three(ring[:, bank, s], [a[:, c, n * JE + e, :] for a in w.w1], [a[:, n % 2, c, s] for a in si],
                                          c == 0, c == KD - 1)
                    last_.then_inc(S["h_done"], 1)
                if op == "O":
                    j, e = divmod(n, JE)
                    pe.wait_ge(S["h_lo"], count(b, NJ, j))
                    if isinstance(b, int) and b == 0 and n == 0:
                        pe.wait_ge(S["piece_lo"], PIECES)
                    s = slice(e * SLOTS2, (e + 1) * SLOTS2)
                    three(ring[:, bank, :], [a[:, j % 2, s] for a in hp], [a[:, n, :] for a in w.w2], True, True).then_inc(S["o_done"], 1)
                if op == "C":
                    if n == 0:
                        pe.wait_ge(S["part_out"], b + 1)
                        if later(b):
                            pe.wait_ge(S["out_done"], b * 2)
                        for t in range(2):
                            mm(acc[:, t, :], part_t[:, t, :], b2s[:, :], start=True, stop=False)
                        pe.wait_ge(S["et_lo"], (b + 1) * TURNS)
                    pe.wait_ge(S["o_lo"], count(b, EXPERTS2, n))
                    for t in range(2):
                        last_ = three(acc[:, t, :], [a[:, n, t * P:(t + 1) * P] for a in et], [a[:, n % 2, :] for a in so],
                                      False, n == EXPERTS2 - 1)
                    last_.then_inc(S["c_done"], 1)
            pe.wait_ge(S["ones_made"], 1)
            pe.wait_ge(S["small"], 16 * 5)
            run(pe, step)



class OnChip:
    pass


def transformer(nc, a, out):
    F, X = "L0_ffn_", "L1_xattn_"

    def scratch(name, shape, dt=F32):
        return nc.dram_tensor(name, shape, dt).ap()

    x1, xn, x1s, x3 = (scratch(name, (T, D)) for name in ("after_conv", "normed_rows", "after_shared", "after_xattn"))
    expert_rows = scratch("expert_rows", (SLOTS, D))
    flat = {name: a[name].rearrange("b n d -> (b n) d") for name in ("x", "ctx_2048")}
    with ExitStack() as whole:
        sb, _, _ = opener(nc, whole)
        k = OnChip()
        k.ident = sb("ident", [P, P])
        k.gates, k.tanh_gates = sb("gates", [P, 4]), sb("tanh_gates", [P, 4])
        constants(nc, k, a["g_xattn"], a["g_ffn"])

        with ExitStack() as st:
            sb, _, _ = opener(nc, st)
            q_t, c_t = (sb(name, [P, KD, SSM_H, B, SSM_I]) for name in ("q_t", "c_t"))
            conv_operands(nc, k, a["x"], a["ctx_2048"], q_t, c_t)
            conv_phase(nc, k, q_t, c_t, a["ssm_reversed"], a["L0_xattn_D"], a["x"], x1.rearrange("(b n) d -> b n d", n=N))

        with ExitStack() as routed:
            sb, _, _ = opener(nc, routed)
            k.slots, k.mix = sb("slots", [P, 2, TT], I32), sb("mix", [P, 2, TT])
            with ExitStack() as st:
                sb, _, _ = opener(nc, st)
                w = OnChip()
                k.logits = sb("router_logits", [P, TT, E])
                k.tile_expert, k.slot_token = sb("tile_expert", [P, TILES], I32), sb("slot_token", [P, TILES], I32)
                w.gate_hi, w.gate_lo, w.up_hi, w.up_lo = (sb(f"w_{n}", [P, E, KD, I_MOE], F16) for n in ("gate_hi", "gate_lo", "up_hi", "up_lo"))
                shared_phase(nc, k, w, x1, xn, x1s, a["router_t"], a[F + "gate_w"], a[F + "up_w"], a[F + "s_gate_w"],
                             a["s_gate_b_cols"], a[F + "s_up_w"], a["s_up_b_cols"], a[F + "s_down_w"], a[F + "s_down_b"])
                w.down_hi, w.down_lo = (sb(f"w_down_{q}", [P, E, MK, D], F16) for q in ("hi", "lo"))
                route_phase(nc, k, w, a[F + "down_w"])
                expert_phase(nc, k, w, xn, expert_rows)
            xattn_phase(nc, k, x1s, expert_rows, flat["ctx_2048"], a["wq_t"], a["wg_t"], a["bg_cols"], a["wkv_t"], a["wo_t"], x3)

        with ExitStack() as st:
            sb, _, _ = opener(nc, st)
            w = OnChip()
            w.mu = tuple(sb(f"w_mu_{q}", [P, KD, ES], F16) for q in ("hi", "lo"))
            w.w1 = tuple(sb(f"w_w1_{q}", [P, KD, EXPERTS2, HID2], F16) for q in ("hi", "lo"))
            w.w2 = tuple(sb(f"w_w2_{q}", [P, EXPERTS2, D], F16) for q in ("hi", "lo"))
            F = "L1_ffn_"
            soft_moe_phase(nc, k, w, x3, a[F + "gamma"], a[F + "beta"], a[F + "mu"], a[F + "scale"], a[F + "W1"],
                           a["b1_cols"], a[F + "W2"], a[F + "b2"], out)


def columns(bias):
    blocks = -(-bias.shape[0] // P)
    filled = np.zeros(blocks * P, bias.dtype)
    filled[:bias.shape[0]] = bias
    return np.ascontiguousarray(filled.reshape(blocks, P).T)


def kernel(**inputs):
    import concourse.bacc as bacc
    from concourse.bass_utils import run_bass_kernel_spmd

    a = dict(inputs)
    turned = lambda m: np.ascontiguousarray(m.T)
    ssm = a.pop("L0_xattn_ssm_kernel")
    a["ssm_reversed"] = np.zeros((ssm.shape[0], D + P), ssm.dtype)
    a["ssm_reversed"][:, :D] = ssm[:, ::-1]
    a["router_t"] = turned(a.pop("L0_ffn_router_w"))
    for new, old in (("wq_t", "Wq"), ("wg_t", "Wg"), ("wkv_t", "Wkv"), ("wo_t", "Wo")):
        a[new] = turned(a.pop("L1_xattn_" + old))
    for new, old in (("s_gate_b_cols", "L0_ffn_s_gate_b"), ("s_up_b_cols", "L0_ffn_s_up_b"), ("bg_cols", "L1_xattn_bg")):
        a[new] = columns(a.pop(old))
    a["b1_cols"] = turned(a.pop("L1_ffn_b1"))
    a["L1_ffn_mu"] = a["L1_ffn_mu"].reshape(D, ES)

    nc = bacc.Bacc("TRN2", target_bir_lowering=False, num_devices=1)
    arrays, args = {}, {}
    for name, value in a.items():
        value = np.ascontiguousarray(value)
        arrays[f"in_{name}"] = value
        args[name] = nc.dram_tensor(f"in_{name}", value.shape, mybir.dt.from_np(value.dtype), kind="ExternalInput").ap()
    out = nc.dram_tensor("out", (T, D), F32, kind="ExternalOutput").ap()
    transformer(nc, args, out)
    result = run_bass_kernel_spmd(nc, [arrays], core_ids=[0])
    return result.results[0]["out"].reshape(B, N, D)
```
